# Optimizing a Trainium2 kernel written in Bass

```python
import numpy as np
import jax
import jax.numpy as jnp

def _softmax(x, axis=-1):
    return jax.nn.softmax(x, axis=axis)

def _gelu(x):
    return jax.nn.gelu(x, approximate=True)

def _silu(x):
    return jax.nn.silu(x)

def _sigmoid(x):
    return jax.nn.sigmoid(x)

def _layernorm(x, axis=-1, eps=1e-05):
    m = jnp.mean(x, axis=axis, keepdims=True)
    v = jnp.var(x, axis=axis, keepdims=True)
    return (x - m) / jnp.sqrt(v + eps)

def _scatter_add(tgt, idx, src, axis=0):
    return tgt.at[idx].add(src)

def _segment_sum(src, seg, n):
    return jax.ops.segment_sum(src, seg, n)
kernel_name = 'mk_decoder_postln_d1_seqx_r4_c3453b'

def setup_inputs(seed: int=0):
    np.random.seed(seed)
    _w = jnp.asarray

    def _rec_inputs():
        import jax
        import jax.numpy as jnp
        _rk = jax.random.key(seed)
        x = -0.0002928 + 1 * jax.random.normal(jax.random.fold_in(_rk, 1), (4, 1024, 256), jnp.float32)
        _lenS = 1024 - jax.random.randint(jax.random.fold_in(_rk, 7), (4,), 0, max(1, 1024 // 4) + 1, jnp.int32)
        _lenS2 = 154 - jax.random.randint(jax.random.fold_in(_rk, 8), (4,), 0, max(1, 154 // 4) + 1, jnp.int32)
        _ctx_768P = jax.random.normal(jax.random.fold_in(_rk, 11), (4, 16, 192), jnp.float32)
        _ctx_768c = jax.random.dirichlet(jax.random.fold_in(_rk, 511), 0.3 * jnp.ones((16,), jnp.float32), (4, 154))
        _ctx_768t = jnp.einsum('bsk,bkd->bsd', _ctx_768c, _ctx_768P)
        _ctx_768t = _ctx_768t * jax.lax.rsqrt(jnp.mean(jnp.square(_ctx_768t)) + 1e-12) * 0.953939
        ctx_768 = 2.09791e-05 + 1.00001 * (_ctx_768t + 0.3 * jax.random.normal(jax.random.fold_in(_rk, 611), (4, 154, 192), jnp.float32))
        return (x, ctx_768)
    x, ctx_768 = _rec_inputs()

    def _L0_attn_setup():
        import jax, jax.numpy as jnp
        import numpy as np
        B, T, C, R = (8, 256, 256, 64)
        EPS = 1e-05
        key = jax.random.key(seed)
        ks = jax.random.split(key, 8)
        x = jax.random.normal(ks[0], (B, T, C), dtype=jnp.float32)
        W_attn = jax.random.normal(ks[1], (3 * C, C), dtype=jnp.float32) * 0.02
        W_proj = jax.random.normal(ks[2], (C, C), dtype=jnp.float32) * 0.02
        lora_attn_A = jax.random.normal(ks[3], (C, R), dtype=jnp.float32) * 0.02
        lora_attn_B = jax.random.normal(ks[4], (R, 3 * C), dtype=jnp.float32) * 0.02
        lora_proj_A = jax.random.normal(ks[5], (C, R), dtype=jnp.float32) * 0.02
        lora_proj_B = jax.random.normal(ks[6], (R, C), dtype=jnp.float32) * 0.02
        bn_gamma = jnp.ones((3 * C,), dtype=jnp.float32)
        bn_beta = jnp.zeros((3 * C,), dtype=jnp.float32)
        return {'x': x, 'W_attn': W_attn, 'W_proj': W_proj, 'lora_attn_A': lora_attn_A, 'lora_attn_B': lora_attn_B, 'lora_proj_A': lora_proj_A, 'lora_proj_B': lora_proj_B, 'bn_gamma': bn_gamma, 'bn_beta': bn_beta}
    _L0_attn_all = _L0_attn_setup()
    _L0_attn_in = {k: v for k, v in _L0_attn_all.items() if k in ('W_attn', 'W_proj', 'lora_attn_A', 'lora_attn_B', 'lora_proj_A', 'lora_proj_B', 'bn_gamma', 'bn_beta')}
    del _L0_attn_all

    def _L0_xattn_setup():
        import jax, jax.numpy as jnp
        import numpy as np
        HEADS = 8
        DIM_HEAD = 128
        ATTN_MATRIX_SCALE = 1.5
        SCALE = DIM_HEAD ** (-0.5)

        def _split_heads(t):
            b, n, _ = t.shape
            t = t.reshape(b, n, HEADS, DIM_HEAD)
            return t.transpose(2, 0, 1, 3).reshape(HEADS, b * n, DIM_HEAD)
        key = jax.random.key(seed)
        ks = jax.random.split(key, 7)
        b, n, m = (2, 512, 512)
        qd, cd, inner = (256, 192, HEADS * DIM_HEAD)
        x = jax.random.normal(ks[0], (b, n, qd), dtype=jnp.float32)
        context = jax.random.normal(ks[1], (b, m, cd), dtype=jnp.float32)
        Wq = jax.random.normal(ks[2], (qd, inner), dtype=jnp.float32) * qd ** (-0.5)
        Wk = jax.random.normal(ks[3], (cd, inner), dtype=jnp.float32) * cd ** (-0.5)
        Wv = jax.random.normal(ks[4], (cd, inner), dtype=jnp.float32) * cd ** (-0.5)
        Wout = jax.random.normal(ks[5], (inner, qd), dtype=jnp.float32) * inner ** (-0.5)
        bout = jnp.zeros((qd,), dtype=jnp.float32)
        return {'x': x, 'context': context, 'Wq': Wq, 'Wk': Wk, 'Wv': Wv, 'Wout': Wout, 'bout': bout}
    _L0_xattn_all = _L0_xattn_setup()
    _L0_xattn_in = {k: v for k, v in _L0_xattn_all.items() if k in ('Wq', 'Wk', 'Wv', 'Wout', 'bout')}
    del _L0_xattn_all

    def _L0_ffn_setup():
        import jax, jax.numpy as jnp
        import numpy as np
        NUM_HEADS = 16
        TOP_K = 2
        ROPE_BASE = 10000.0
        LN_EPS = 1e-05

        def _rope_sin_cos(S, D, dtype):
            inv_freq = 1.0 / ROPE_BASE ** (jnp.arange(0, D, 2, dtype=jnp.float32) / D)
            freqs = jnp.arange(S, dtype=jnp.float32)[:, None] * inv_freq[None, :]
            sin = jnp.sin(freqs).astype(dtype)[None, :, None, :]
            cos = jnp.cos(freqs).astype(dtype)[None, :, None, :]
            return (sin, cos)

        def _apply_rope(x, sin, cos):
            x1, x2 = (x[..., 0::2], x[..., 1::2])
            r1 = x1 * cos - x2 * sin
            r2 = x1 * sin + x2 * cos
            return jnp.stack([r1, r2], axis=-1).reshape(x.shape)

        def _layer_norm(x, w, b):
            mu = jnp.mean(x, axis=-1, keepdims=True)
            var = jnp.mean(jnp.square(x - mu), axis=-1, keepdims=True)
            return (x - mu) * jax.lax.rsqrt(var + LN_EPS) * w + b
        key = jax.random.key(seed)
        ks = jax.random.split(key, 8)
        B, S, E, NE = (2, 512, 256, 8)
        s = 0.02
        return {'x': jax.random.normal(ks[0], (B, S, E), dtype=jnp.float32), 'in_proj_w': jax.random.normal(ks[1], (3 * E, E), dtype=jnp.float32) * s, 'in_proj_b': jnp.zeros((3 * E,), dtype=jnp.float32), 'out_proj_w': jax.random.normal(ks[2], (E, E), dtype=jnp.float32) * s, 'out_proj_b': jnp.zeros((E,), dtype=jnp.float32), 'gate_w': jax.random.normal(ks[3], (NE, E), dtype=jnp.float32) * s, 'gate_b': jnp.zeros((NE,), dtype=jnp.float32), 'expert_w': jax.random.normal(ks[4], (NE, E, E), dtype=jnp.float32) * s, 'expert_b': jnp.zeros((NE, E), dtype=jnp.float32), 'ln1_w': jnp.ones((E,), dtype=jnp.float32), 'ln1_b': jnp.zeros((E,), dtype=jnp.float32), 'ln2_w': jnp.ones((E,), dtype=jnp.float32), 'ln2_b': jnp.zeros((E,), dtype=jnp.float32)}
    _L0_ffn_all = _L0_ffn_setup()
    _L0_ffn_in = {k: v for k, v in _L0_ffn_all.items() if k in ('in_proj_w', 'in_proj_b', 'out_proj_w', 'out_proj_b', 'gate_w', 'gate_b', 'expert_w', 'expert_b', 'ln1_w', 'ln1_b', 'ln2_w', 'ln2_b')}
    del _L0_ffn_all
    return {'x': x, 'ctx_768': ctx_768, 'L0_attn_W_attn': _L0_attn_in['W_attn'], 'L0_attn_W_proj': _L0_attn_in['W_proj'], 'L0_attn_lora_attn_A': _L0_attn_in['lora_attn_A'], 'L0_attn_lora_attn_B': _L0_attn_in['lora_attn_B'], 'L0_attn_lora_proj_A': _L0_attn_in['lora_proj_A'], 'L0_attn_lora_proj_B': _L0_attn_in['lora_proj_B'], 'L0_attn_bn_gamma': _L0_attn_in['bn_gamma'], 'L0_attn_bn_beta': _L0_attn_in['bn_beta'], 'L0_xattn_Wq': _L0_xattn_in['Wq'], 'L0_xattn_Wk': _L0_xattn_in['Wk'], 'L0_xattn_Wv': _L0_xattn_in['Wv'], 'L0_xattn_Wout': _L0_xattn_in['Wout'], 'L0_xattn_bout': _L0_xattn_in['bout'], 'L0_ffn_in_proj_w': _L0_ffn_in['in_proj_w'], 'L0_ffn_in_proj_b': _L0_ffn_in['in_proj_b'], 'L0_ffn_out_proj_w': _L0_ffn_in['out_proj_w'], 'L0_ffn_out_proj_b': _L0_ffn_in['out_proj_b'], 'L0_ffn_gate_w': _L0_ffn_in['gate_w'], 'L0_ffn_gate_b': _L0_ffn_in['gate_b'], 'L0_ffn_expert_w': _L0_ffn_in['expert_w'], 'L0_ffn_expert_b': _L0_ffn_in['expert_b'], 'L0_ffn_ln1_w': _L0_ffn_in['ln1_w'], 'L0_ffn_ln1_b': _L0_ffn_in['ln1_b'], 'L0_ffn_ln2_w': _L0_ffn_in['ln2_w'], 'L0_ffn_ln2_b': _L0_ffn_in['ln2_b']}

def reference(x, ctx_768, L0_attn_W_attn, L0_attn_W_proj, L0_attn_lora_attn_A, L0_attn_lora_attn_B, L0_attn_lora_proj_A, L0_attn_lora_proj_B, L0_attn_bn_gamma, L0_attn_bn_beta, L0_xattn_Wq, L0_xattn_Wk, L0_xattn_Wv, L0_xattn_Wout, L0_xattn_bout, L0_ffn_in_proj_w, L0_ffn_in_proj_b, L0_ffn_out_proj_w, L0_ffn_out_proj_b, L0_ffn_gate_w, L0_ffn_gate_b, L0_ffn_expert_w, L0_ffn_expert_b, L0_ffn_ln1_w, L0_ffn_ln1_b, L0_ffn_ln2_w, L0_ffn_ln2_b):
    import jax
    import jax.numpy as jnp

    def _L0_attn_ref(x, W_attn, W_proj, lora_attn_A, lora_attn_B, lora_proj_A, lora_proj_B, bn_gamma, bn_beta):
        import jax, jax.numpy as jnp
        import numpy as np
        B, T, C, R = (8, 256, 256, 64)
        EPS = 1e-05
        Bb, Tt, Cc = x.shape
        Wm_attn = W_attn + (lora_attn_A @ lora_attn_B).reshape(W_attn.shape)
        xa = jnp.einsum('btc,dc->btd', x, Wm_attn)
        mean = xa.mean(axis=(0, 1))
        var = xa.var(axis=(0, 1))
        xa = (xa - mean) * jax.lax.rsqrt(var + EPS) * bn_gamma + bn_beta
        q, k, v = jnp.split(xa, 3, axis=-1)
        scale = 1.0 / jnp.sqrt(jnp.asarray(Cc, dtype=x.dtype))
        att = jnp.einsum('btc,bsc->bts', q, k) * scale
        causal = jnp.tril(jnp.ones((Tt, Tt), dtype=bool))
        att = jnp.where(causal[None, :, :], att, -jnp.inf)
        att = jax.nn.softmax(att, axis=-1)
        y = jnp.einsum('bts,bsc->btc', att, v)
        y = jnp.einsum('btc,dc->btd', y, W_proj)
        Wm_proj = W_proj + (lora_proj_A @ lora_proj_B).reshape(W_proj.shape)
        y = jnp.einsum('btc,dc->btd', y, Wm_proj)
        return y

    def _L0_xattn_ref(x, context, Wq, Wk, Wv, Wout, bout):
        import jax, jax.numpy as jnp
        import numpy as np
        HEADS = 8
        DIM_HEAD = 128
        ATTN_MATRIX_SCALE = 1.5
        SCALE = DIM_HEAD ** (-0.5)

        def _split_heads(t):
            b, n, _ = t.shape
            t = t.reshape(b, n, HEADS, DIM_HEAD)
            return t.transpose(2, 0, 1, 3).reshape(HEADS, b * n, DIM_HEAD)
        b, n, _ = x.shape
        qh = _split_heads(jnp.einsum('bnq,qi->bni', x, Wq))
        kh = _split_heads(jnp.einsum('bmc,ci->bmi', context, Wk))
        vh = _split_heads(jnp.einsum('bmc,ci->bmi', context, Wv))
        sim = jnp.einsum('hid,hjd->hij', qh, kh) * SCALE
        mean = jnp.mean(sim, axis=-1, keepdims=True)
        sim = (sim - mean) * ATTN_MATRIX_SCALE + mean
        attn = jax.nn.softmax(sim, axis=-1)
        out = jnp.einsum('hij,hjd->hid', attn, vh)
        out = out.reshape(HEADS, b, n, DIM_HEAD).transpose(1, 2, 0, 3)
        out = out.reshape(b, n, HEADS * DIM_HEAD)
        return jnp.einsum('bni,iq->bnq', out, Wout) + bout

    def _L0_ffn_ref(x, in_proj_w, in_proj_b, out_proj_w, out_proj_b, gate_w, gate_b, expert_w, expert_b, ln1_w, ln1_b, ln2_w, ln2_b):
        import jax, jax.numpy as jnp
        import numpy as np
        NUM_HEADS = 16
        TOP_K = 2
        ROPE_BASE = 10000.0
        LN_EPS = 1e-05

        def _rope_sin_cos(S, D, dtype):
            inv_freq = 1.0 / ROPE_BASE ** (jnp.arange(0, D, 2, dtype=jnp.float32) / D)
            freqs = jnp.arange(S, dtype=jnp.float32)[:, None] * inv_freq[None, :]
            sin = jnp.sin(freqs).astype(dtype)[None, :, None, :]
            cos = jnp.cos(freqs).astype(dtype)[None, :, None, :]
            return (sin, cos)

        def _apply_rope(x, sin, cos):
            x1, x2 = (x[..., 0::2], x[..., 1::2])
            r1 = x1 * cos - x2 * sin
            r2 = x1 * sin + x2 * cos
            return jnp.stack([r1, r2], axis=-1).reshape(x.shape)

        def _layer_norm(x, w, b):
            mu = jnp.mean(x, axis=-1, keepdims=True)
            var = jnp.mean(jnp.square(x - mu), axis=-1, keepdims=True)
            return (x - mu) * jax.lax.rsqrt(var + LN_EPS) * w + b
        B, S, E = x.shape
        H = NUM_HEADS
        D = E // H
        xh = x.reshape(B, S, H, D)
        sin, cos = _rope_sin_cos(S, D, x.dtype)
        q_in = _apply_rope(xh, sin, cos).reshape(B, S, E)
        k_in = q_in
        v_in = x
        Wq, Wk, Wv = jnp.split(in_proj_w, 3, axis=0)
        bq, bk, bv = jnp.split(in_proj_b, 3, axis=0)
        q = (q_in @ Wq.T + bq).reshape(B, S, H, D)
        k = (k_in @ Wk.T + bk).reshape(B, S, H, D)
        v = (v_in @ Wv.T + bv).reshape(B, S, H, D)
        scale = 1.0 / jnp.sqrt(jnp.asarray(D, dtype=x.dtype))
        scores = jnp.einsum('bqhd,bkhd->bhqk', q, k) * scale
        causal = jnp.tril(jnp.ones((S, S), dtype=bool))
        scores = jnp.where(causal[None, None], scores, jnp.asarray(-jnp.inf, dtype=scores.dtype))
        attn = jax.nn.softmax(scores, axis=-1)
        ctx = jnp.einsum('bhqk,bkhd->bqhd', attn, v).reshape(B, S, E)
        attn_out = ctx @ out_proj_w.T + out_proj_b
        x1 = _layer_norm(x + attn_out, ln1_w, ln1_b)
        gates = jax.nn.softmax(x1 @ gate_w.T + gate_b, axis=-1)
        _, top_idx = jax.lax.top_k(gates, TOP_K)
        top_gates = jnp.take_along_axis(gates, top_idx, axis=-1)
        expert_outputs = jnp.einsum('bsd,efd->bsef', x1, expert_w) + expert_b[None, None]
        sel = jnp.take_along_axis(expert_outputs, top_idx[..., None], axis=2)
        moe_out = jnp.sum(sel * top_gates[..., None], axis=2)
        return _layer_norm(x1 + moe_out, ln2_w, ln2_b)
    x = _layernorm(x + _L0_attn_ref(x, L0_attn_W_attn, L0_attn_W_proj, L0_attn_lora_attn_A, L0_attn_lora_attn_B, L0_attn_lora_proj_A, L0_attn_lora_proj_B, L0_attn_bn_gamma, L0_attn_bn_beta), axis=-1)
    x = _layernorm(x + _L0_xattn_ref(x, ctx_768, L0_xattn_Wq, L0_xattn_Wk, L0_xattn_Wv, L0_xattn_Wout, L0_xattn_bout), axis=-1)
    x = _layernorm(x + _L0_ffn_ref(x, L0_ffn_in_proj_w, L0_ffn_in_proj_b, L0_ffn_out_proj_w, L0_ffn_out_proj_b, L0_ffn_gate_w, L0_ffn_gate_b, L0_ffn_expert_w, L0_ffn_expert_b, L0_ffn_ln1_w, L0_ffn_ln1_b, L0_ffn_ln2_w, L0_ffn_ln2_b), axis=-1)
    return x

_drawn_inputs = setup_inputs


def setup_inputs(seed=0):
    import zlib

    import numpy as np

    out = dict(_drawn_inputs(seed))
    spreads = {'L0_attn_bn_gamma': (1.0, 0.6),
     'L0_attn_bn_beta': (0.0, 0.738),
     'L0_xattn_bout': (0.0, 0.1),
     'L0_ffn_in_proj_b': (0.0, 0.442),
     'L0_ffn_out_proj_b': (0.0, 0.1),
     'L0_ffn_gate_b': (0.0, 0.328),
     'L0_ffn_expert_b': (0.0, 0.646),
     'L0_ffn_ln1_w': (1.0, 0.2),
     'L0_ffn_ln1_b': (0.0, 0.1),
     'L0_ffn_ln2_w': (1.0, 0.2),
     'L0_ffn_ln2_b': (0.0, 0.1)}
    factors = {'L0_attn_W_attn': 3.482,
     'L0_attn_W_proj': 2.95,
     'L0_attn_lora_attn_A': 8.0,
     'L0_attn_lora_attn_B': 8.0,
     'L0_attn_lora_proj_A': 8.0,
     'L0_attn_lora_proj_B': 8.0,
     'L0_ffn_in_proj_w': 3.577}
    for name, (base, spread) in spreads.items():
        noise = np.random.default_rng([zlib.crc32(name.encode()), seed]).standard_normal(out[name].shape)
        drawn = base * np.exp(spread * noise) if base else spread * noise
        out[name] = jnp.asarray(drawn.astype(out[name].dtype))
    for name, factor in factors.items():
        out[name] = (out[name] * factor).astype(out[name].dtype)
    return out
```

```python
import numpy as np
import concourse.bass as bass
from concourse import mybir
from contextlib import ExitStack

F32 = mybir.dt.float32
F32R = mybir.dt.float32r
BF16 = mybir.dt.bfloat16
U32 = mybir.dt.uint32
ALU = mybir.AluOpType
ACT = mybir.ActivationFunctionType
X = mybir.AxisListType.X
XY = mybir.AxisListType.XY

P = 128
B, T, C = 4, 1024, 256
CT = C // P
NT = T // P
TOKENS = B * T
EPS = 1e-5
SCALE1 = C ** -0.5
QKV = 3 * C
DT = QKV // P
LORA = 64

M, J, CD = 154, B * 154, 192
H2, D2 = 8, 128
KT2, KP2 = 2, CD // 2
JT = (J + P - 1) // P
JH = J // 2
INNER = H2 * D2
SCALE2 = D2 ** -0.5
SHARPEN = 1.5
CHUNK = 512
CHUNKS = T // CHUNK
TPC = CHUNK // P

H3, D3 = 16, 16
SCALE3 = D3 ** -0.5
PAIRS = H3 // 2
NE = 8


class Scope:

    def __init__(self, nc, name):
        self.nc, self.name, self.stack, self.sems = nc, name, ExitStack(), []

    def __enter__(self):
        self.stack.__enter__()
        return self

    def __exit__(self, *e):
        return self.stack.__exit__(*e)

    def sb(self, name, shape, dt=F32):
        return self.stack.enter_context(self.nc.sbuf_tensor(f"{self.name}_{name}", shape, dt))

    def ps(self, name, shape, dt=F32):
        return self.stack.enter_context(self.nc.psum_tensor(f"{self.name}_{name}", shape, dt))

    def sem(self, name):
        s = self.stack.enter_context(self.nc.semaphore(f"{self.name}_{name}"))
        self.sems.append(s)
        return s

    def clear(self):
        with self.nc.Block(no_gpsimd_drain=True) as block:
            @block.sync
            def _(sp):
                for s in self.sems:
                    sp.sem_clear(s)


def mm3(nc, out, lhs, rhs, start, stop):
    (ah, al), (bh, bl) = lhs, rhs
    nc.tensor.matmul(out, al, bh, start=start, stop=False)
    nc.tensor.matmul(out, ah, bl, start=False, stop=False)
    return nc.tensor.matmul(out, ah, bh, start=False, stop=stop)


def fold_layer1(nc, io, keep):
    WmT, Mv, cb, bn_scale, bn_shift = (keep[k] for k in ("WmT", "Mv", "cb", "bn_scale", "bn_shift"))
    ident = keep["ident"]
    with Scope(nc, "fold") as s:
        x_all = s.sb("x_all", [P, B * NT, C + 1])
        WaT = s.sb("WaT", [P, CT, QKV])
        AaT = s.sb("AaT", [LORA, C])
        Ba = s.sb("Ba", [LORA, QKV])
        ApT = s.sb("ApT", [LORA, C])
        Bp = s.sb("Bp", [LORA, C])
        Wp = s.sb("Wp", [P, CT, C])
        WpT = s.sb("WpT", [P, CT, C])
        WmpT = s.sb("WmpT", [P, CT, C])
        Wcomb = s.sb("Wcomb", [P, CT, C])
        WcombS = s.sb("WcombS", [P, CT, C])
        Wv = s.sb("Wv", [P, CT, C])
        G = s.sb("G", [P, CT, C + 1])
        prod = s.sb("prod", [P, CT, QKV])
        ones = s.sb("ones", [P, P])
        gamma = s.sb("gamma", [P, DT])
        beta = s.sb("beta", [P, DT])
        mean = s.sb("mean", [P, DT])
        ex2 = s.sb("ex2", [P, DT])
        msq = s.sb("msq", [P, DT])
        var = s.sb("var", [P, DT])
        nhalf = s.sb("nhalf", [P, DT])
        rstd = s.sb("rstd", [P, DT])
        shiftB = s.sb("shiftB", [P, CT, P])
        psL = [s.ps(f"psL{i}", [P, 1024]) for i in range(CT)]
        psM = s.ps("psM", [P, 512])
        psG = [s.ps(f"psG{i}", [P, 512]) for i in range(CT)]
        psX = s.ps("psX", [P, 512])

        x_in = [s.sem(f"x_in{n}") for n in range(B)]
        w_in, c_in = s.sem("w_in"), s.sem("c_in")
        consts = s.sem("consts")
        lora_a, lora_p, wm_done, wmp_done = (s.sem(n) for n in ("lora_a", "lora_p", "wm_done", "wmp_done"))
        comb_ps, comb_done, wvt_ps, wv_done = (s.sem(n) for n in ("comb_ps", "comb_done", "wvt_ps", "wv_done"))
        gram_ps, gram_done, h_ps, prod_done = (s.sem(n) for n in ("gram_ps", "gram_done", "h_ps", "prod_done"))
        stat_ps, stat, pow_done, fold_ps = (s.sem(n) for n in ("stat_ps", "stat", "pow_done", "fold_ps"))

        with nc.Block(no_gpsimd_drain=True) as block:
            @block.sync
            def _(sp):
                sp.dma_start(AaT[:, :], io["AaT"]).then_inc(w_in, 16)
                sp.dma_start(Ba[:, :], io["Ba"]).then_inc(w_in, 16)
                sp.dma_start(WaT[:, :, :], io["WaT"].rearrange("(k p) d -> p k d", p=P)).then_inc(w_in, 16)
                for b in range(B):
                    sp.dma_start(x_all[:, b * NT:(b + 1) * NT, 0:C],
                                 io["x"][b * T:(b + 1) * T, :].rearrange("(n p) c -> p n c", p=P)).then_inc(x_in[b], 16)

            @block.scalar
            def _(act):
                act.dma_start(ApT[:, :], io["ApT"]).then_inc(c_in, 16)
                act.dma_start(Bp[:, :], io["Bp"]).then_inc(c_in, 16)
                act.dma_start(Wp[:, :, :], io["Wp"].rearrange("(k p) d -> p k d", p=P)).then_inc(c_in, 16)
                act.dma_start(WpT[:, :, :], io["WpT"].rearrange("(k p) d -> p k d", p=P)).then_inc(c_in, 16)
                act.dma_start(gamma[:, :], io["gamma"]).then_inc(c_in, 16)
                act.dma_start(beta[:, :], io["beta"]).then_inc(c_in, 16)
                act.dma_start(ident[:, :], io["ident"]).then_inc(c_in, 16)

            @block.gpsimd
            def _(pool):
                nc.gpsimd.memset(x_all[:, :, C:C + 1], 1.0).then_inc(consts, 1)
                nc.gpsimd.memset(ones[:, :], 1.0).then_inc(consts, 1)
                nc.gpsimd.memset(nhalf[:, :], -0.5).then_inc(consts, 1)
                pool.wait_ge(consts, 3)
                pool.wait_ge(stat, 4)
                nc.gpsimd.tensor_tensor(rstd[:, :], var[:, :], nhalf[:, :], ALU.pow).then_inc(pow_done, 1)

            @block.tensor
            def _(pe):
                pe.wait_ge(w_in, 48)
                for k in range(CT):
                    for r in range(3):
                        last = nc.tensor.matmul(psL[k][:, r * C:(r + 1) * C],
                                                Ba[:, r * C + k * P:r * C + (k + 1) * P], AaT[:, :],
                                                start=True, stop=True)
                    last.then_inc(lora_a, 1)
                pe.wait_ge(c_in, 112)
                for k in range(CT):
                    last = nc.tensor.matmul(psM[:, k * C:(k + 1) * C], Bp[:, k * P:(k + 1) * P], ApT[:, :],
                                            start=True, stop=True)
                last.then_inc(lora_p, 1)
                pe.wait_ge(consts, 1)
                for n in range(B * NT):
                    if n % NT == 0:
                        pe.wait_ge(x_in[n // NT], 16)
                    for k in range(CT):
                        last = nc.tensor.matmul(psG[k][:, 0:C + 1], x_all[:, n, k * P:(k + 1) * P],
                                                x_all[:, n, :], start=(n == 0), stop=(n == B * NT - 1))
                last.then_inc(gram_ps, 1)
                pe.wait_ge(wmp_done, 1)
                for d in range(CT):
                    for k in range(CT):
                        last = nc.tensor.matmul(psM[:, d * C:(d + 1) * C], Wp[:, k, d * P:(d + 1) * P],
                                                WmpT[:, k, :], start=(k == 0), stop=(k == CT - 1))
                last.then_inc(comb_ps, 1)
                pe.wait_ge(wm_done, 2)
                for d in range(CT):
                    for k in range(CT):
                        last = nc.tensor.transpose(psX[:, d * C + k * P:d * C + (k + 1) * P],
                                                   WmT[:, k, 2 * C + d * P:2 * C + (d + 1) * P], ident[:, :])
                last.then_inc(wvt_ps, 1)
                pe.wait_ge(gram_done, 1)
                for c in range(CT):
                    for lo, hi in ((0, 512), (512, QKV)):
                        for k in range(CT):
                            last = nc.tensor.matmul(psL[c][:, lo:hi], G[:, k, c * P:(c + 1) * P],
                                                    WmT[:, k, lo:hi], start=(k == 0), stop=(k == CT - 1))
                    last.then_inc(h_ps, 1)
                pe.wait_ge(prod_done, 2)
                pe.wait_ge(consts, 2)
                for d in range(DT):
                    for k in range(CT):
                        nc.tensor.matmul(psG[0][:, d:d + 1], prod[:, k, d * P:(d + 1) * P], ones[:, 0:1],
                                         start=(k == 0), stop=(k == CT - 1))
                for d in range(DT):
                    for k in range(CT):
                        last = nc.tensor.matmul(psG[0][:, DT + d:DT + d + 1], WmT[:, k, d * P:(d + 1) * P],
                                                G[:, k, C:C + 1], start=(k == 0), stop=(k == CT - 1))
                last.then_inc(stat_ps, 1)
                pe.wait_ge(stat, 8)
                for c in range(CT):
                    for k in range(CT):
                        last = nc.tensor.matmul(psM[:, c * C:(c + 1) * C], Wv[:, k, c * P:(c + 1) * P],
                                                WcombS[:, k, :], start=(k == 0), stop=(k == CT - 1))
                for k in range(CT):
                    last = nc.tensor.matmul(psX[:, 0:C], shiftB[:, k, :], Wcomb[:, k, :],
                                            start=(k == 0), stop=(k == CT - 1))
                last.then_inc(fold_ps, 1)

            @block.vector
            def _(dve):
                dve.wait_ge(w_in, 48)
                for k in range(CT):
                    dve.wait_ge(lora_a, k + 1)
                    nc.vector.tensor_tensor(
                        WmT[:, k, :].rearrange("p (i r) -> p i r", r=3),
                        WaT[:, k, :].rearrange("p (i r) -> p i r", r=3),
                        psL[k][:, 0:QKV].rearrange("p (r i) -> p i r", r=3), ALU.add).then_inc(wm_done, 1)
                dve.wait_ge(c_in, 112)
                dve.wait_ge(lora_p, 1)
                nc.vector.tensor_tensor(WmpT[:, :, :], WpT[:, :, :],
                                        psM[:, :].rearrange("p (k e) -> p k e", k=CT), ALU.add).then_inc(wmp_done, 1)
                dve.wait_ge(comb_ps, 1)
                nc.vector.tensor_copy(Wcomb[:, :, :], psM[:, :].rearrange("p (k e) -> p k e", k=CT)).then_inc(comb_done, 1)
                dve.wait_ge(wvt_ps, 1)
                nc.vector.tensor_copy(Wv[:, :, :], psX[:, :].rearrange("p (k e) -> p k e", k=CT)).then_inc(wv_done, 1)
                dve.wait_ge(gram_ps, 1)
                nc.vector.tensor_copy(G[:, 0, :], psG[0][:, 0:C + 1])
                nc.vector.tensor_copy(G[:, 1, :], psG[1][:, 0:C + 1]).then_inc(gram_done, 1)
                for c in range(CT):
                    dve.wait_ge(h_ps, c + 1)
                    nc.vector.tensor_tensor(prod[:, c, :], WmT[:, c, :], psL[c][:, 0:QKV], ALU.mult).then_inc(prod_done, 1)
                dve.wait_ge(stat_ps, 1)
                nc.vector.tensor_scalar(ex2[:, :], psG[0][:, 0:DT], 1.0 / TOKENS, EPS, ALU.mult, ALU.add).then_inc(stat, 1)
                nc.vector.tensor_scalar(mean[:, :], psG[0][:, DT:2 * DT], 1.0 / TOKENS, None, ALU.mult).then_inc(stat, 1)
                dve.wait_ge(stat, 2)
                nc.vector.tensor_tensor(msq[:, :], mean[:, :], mean[:, :], ALU.mult).then_inc(stat, 1)
                dve.wait_ge(stat, 3)
                nc.vector.tensor_tensor(var[:, :], ex2[:, :], msq[:, :], ALU.subtract).then_inc(stat, 1)
                dve.wait_ge(pow_done, 1)
                nc.vector.tensor_tensor(bn_scale[:, :], gamma[:, :], rstd[:, :], ALU.mult).then_inc(stat, 1)
                dve.wait_ge(stat, 5)
                nc.vector.tensor_tensor(msq[:, :], mean[:, :], bn_scale[:, :], ALU.mult).then_inc(stat, 1)
                dve.wait_ge(stat, 6)
                nc.vector.tensor_tensor(bn_shift[:, :], beta[:, :], msq[:, :], ALU.subtract).then_inc(stat, 1)
                dve.wait_ge(stat, 7)
                dve.wait_ge(comb_done, 1)
                for k in range(CT):
                    nc.vector.tensor_scalar(WcombS[:, k, :], Wcomb[:, k, :], bn_scale[:, 4 + k:5 + k], None, ALU.mult)
                    last = nc.vector.tensor_scalar(shiftB[:, k, :], ones[:, :], bn_shift[:, 4 + k:5 + k], None, ALU.mult)
                last.then_inc(stat, 1)
                dve.wait_ge(stat, 8)
                nc.vector.tensor_scalar(bn_scale[:, 0:CT], bn_scale[:, 0:CT], SCALE1, None, ALU.mult)
                nc.vector.tensor_scalar(bn_shift[:, 0:CT], bn_shift[:, 0:CT], SCALE1, None, ALU.mult)
                dve.wait_ge(fold_ps, 1)
                nc.vector.tensor_copy(Mv[:, :, :], psM[:, :].rearrange("p (k e) -> p k e", k=CT))
                nc.vector.tensor_copy(cb[:, :], psX[:, 0:C])
        s.clear()


def layer1(nc, io, x_next):
    with Scope(nc, "keep1") as keep:
        k = dict(WmT=keep.sb("WmT", [P, CT, QKV]), Mv=keep.sb("Mv", [P, CT, C]), cb=keep.sb("cb", [P, C]),
                 bn_scale=keep.sb("bn_scale", [P, DT]), bn_shift=keep.sb("bn_shift", [P, DT]),
                 ident=keep.sb("ident", [P, P]))
        fold_layer1(nc, io, k)
        WmT, Mv, cb, bn_scale, bn_shift, ident = (k[n] for n in ("WmT", "Mv", "cb", "bn_scale", "bn_shift", "ident"))
        with Scope(nc, "attn1") as s:
            xn = s.sb("xn", [P, NT, C])
            xT = s.sb("xT", [P, CT, T])
            qT = s.sb("qT", [P, CT, T])
            kT = s.sb("kT", [P, CT, T])
            V = s.sb("V", [P, NT, C])
            prob = s.sb("prob", [P, 2, T])
            probT = s.sb("probT", [P, 2, T])
            y = s.sb("y", [P, NT, C])
            stats = s.sb("stats", [P, NT, 6])
            mv = s.sb("mv", [P, NT, 2])
            veps = s.sb("veps", [P, NT])
            rstd = s.sb("rstd", [P, NT])
            nmax = s.sb("nmax", [P, NT])
            rsum = s.sb("rsum", [P, NT])
            rinv = s.sb("rinv", [P, NT])
            nhalf = s.sb("nhalf", [P, 1])
            identb = s.sb("identb", [P, P], BF16)
            maskf = s.sb("maskf", [P, P])
            maskb = s.sb("maskb", [P, P], BF16)
            psS = [s.ps(f"psS{i}", [P, 1024]) for i in range(2)]
            psT = [s.ps(f"psT{i}", [P, 512]) for i in range(2)]
            psO = [s.ps(f"psO{i}", [P, 512]) for i in range(2)]

            x_in, consts, const_in = s.sem("x_in"), s.sem("consts"), s.sem("const_in")
            qk_ps, qk_done, v_ps, v_done = s.sem("qk_ps"), s.sem("qk_done"), s.sem("v_ps"), s.sem("v_done")
            s_ps, max_done, exp_done = s.sem("s_ps"), s.sem("max_done"), s.sem("exp_done")
            t_ps, t_done, o_ps, y_done = s.sem("t_ps"), s.sem("t_done"), s.sem("o_ps"), s.sem("y_done")
            rinv_done, st_done, veps_done, rstd_done, ln_done, out_st = (
                s.sem(n) for n in ("rinv_done", "st_done", "veps_done", "rstd_done", "ln_done", "out_st"))

            groups = []
            for t in range(NT):
                for g in range(0, t + 1, 4):
                    groups.append((t, g, min(4, t + 1 - g)))
            first_group = {t: min(i for i, g in enumerate(groups) if g[0] == t) for t in range(NT)}
            last_group = {t: max(i for i, g in enumerate(groups) if g[0] == t) for t in range(NT)}

            with nc.Block(no_gpsimd_drain=True) as block:
                @block.sync
                def _(sp):
                    sp.dma_start(maskf[:, :], io["mask"]).then_inc(const_in, 16)

                @block.scalar
                def _(act):
                    nc.scalar.activation(identb[:, :], ident[:, :], ACT.Copy)
                    act.wait_ge(const_in, 16)
                    nc.scalar.activation(maskb[:, :], maskf[:, :], ACT.Copy)

                @block.gpsimd
                def _(pool):
                    nc.gpsimd.memset(nhalf[:, :], -0.5).then_inc(consts, 1)
                    pool.wait_ge(consts, 1)
            s.clear()

            with nc.Fori(0, B) as b:
                with nc.Block(no_gpsimd_drain=True) as block:
                    @block.sync
                    def _(sp):
                        sp.dma_start(xT[:, :, :], io["xT"][:, bass.ts(b, T)].rearrange("(k p) t -> p k t", p=P)).then_inc(x_in, 16)
                        sp.dma_start(xn[:, :, :], io["x"][bass.ts(b, T), :].rearrange("(n p) c -> p n c", p=P)).then_inc(x_in, 16)
                        sp.wait_ge(ln_done, NT)
                        sp.dma_start(x_next[bass.ts(b, T), :].rearrange("(n p) c -> p n c", p=P), y[:, :, :]).then_inc(out_st, 16)
                        sp.wait_ge(out_st, 16)

                    @block.tensor
                    def _(pe):
                        pe.wait_ge(x_in, 32)
                        n = 0
                        for d in range(2 * CT):
                            for c in range(CHUNKS):
                                bank = psS[n // 2 % 2][:, (n % 2) * 512:(n % 2) * 512 + 512]
                                if n >= 4:
                                    pe.wait_ge(qk_done, n - 3)
                                for k in range(CT):
                                    last = nc.tensor.matmul(bank, WmT[:, k, d * P:(d + 1) * P],
                                                            xT[:, k, c * CHUNK:(c + 1) * CHUNK],
                                                            start=(k == 0), stop=(k == CT - 1))
                                last.then_inc(qk_ps, 1)
                                n += 1
                        for t in range(NT):
                            if t >= 2:
                                pe.wait_ge(v_done, t - 1)
                            for k in range(CT):
                                last = nc.tensor.matmul(psO[t % 2][:, 0:C], xT[:, k, t * P:(t + 1) * P], Mv[:, k, :],
                                                        start=(k == 0), stop=(k == CT - 1))
                            last.then_inc(v_ps, 1)
                        pe.wait_ge(qk_done, 8)

                        def scores(t):
                            if t >= 2:
                                pe.wait_ge(exp_done, t - 1)
                            for c in range(0, (t + 1) * P, 512):
                                w = min(512, (t + 1) * P - c)
                                diag = c + w == (t + 1) * P
                                for k in range(CT):
                                    last = nc.tensor.matmul(psS[t % 2][:, c:c + w], qT[:, k, t * P:(t + 1) * P],
                                                            kT[:, k, c:c + w], start=(k == 0),
                                                            stop=(k == CT - 1 and not diag))
                                if diag:
                                    last = nc.tensor.matmul(psS[t % 2][:, t * P:(t + 1) * P], identb[:, :], maskb[:, :],
                                                            start=False, stop=True)
                            last.then_inc(s_ps, 1)

                        def transposed(t):
                            pe.wait_ge(exp_done, t + 1)
                            for i in range(first_group[t], last_group[t] + 1):
                                _, g, n = groups[i]
                                if i >= 2:
                                    pe.wait_ge(t_done, i - 1)
                                for j in range(n):
                                    last = nc.tensor.transpose(psT[i % 2][:, j * P:(j + 1) * P],
                                                               prob[:, t % 2, (g + j) * P:(g + j + 1) * P], ident[:, :])
                                last.then_inc(t_ps, 1)

                        def weighted(t):
                            pe.wait_ge(t_done, last_group[t] + 1)
                            if t == 0:
                                pe.wait_ge(v_done, NT)
                            if t >= 2:
                                pe.wait_ge(y_done, t - 1)
                            for j in range(t + 1):
                                last = nc.tensor.matmul(psO[t % 2][:, 0:C], probT[:, t % 2, j * P:(j + 1) * P], V[:, j, :],
                                                        start=(j == 0), stop=(j == t))
                            last.then_inc(o_ps, 1)

                        scores(0)
                        for t in range(NT):
                            if t + 1 < NT:
                                scores(t + 1)
                            transposed(t)
                            weighted(t)

                    @block.scalar
                    def _(act):
                        n = 0
                        for d in range(2 * CT):
                            dst = qT if d < CT else kT
                            for c in range(CHUNKS):
                                act.wait_ge(qk_ps, n + 1)
                                bank = psS[n // 2 % 2][:, (n % 2) * 512:(n % 2) * 512 + 512]
                                nc.scalar.activation(dst[:, d % CT, c * CHUNK:(c + 1) * CHUNK], bank, ACT.Identity,
                                                     bias=bn_shift[:, d:d + 1], scale=bn_scale[:, d:d + 1]).then_inc(qk_done, 1)
                                n += 1
                        for t in range(NT):
                            act.wait_ge(max_done, t + 1)
                            if t >= 2:
                                act.wait_ge(t_ps, last_group[t - 2] + 1)
                            nc.scalar.activation(prob[:, t % 2, 0:(t + 1) * P], psS[t % 2][:, 0:(t + 1) * P], ACT.Exp,
                                                 bias=nmax[:, t:t + 1], accum_out=rsum[:, t:t + 1]).then_inc(exp_done, 1)

                    @block.gpsimd
                    def _(pool):
                        for t in range(NT):
                            pool.wait_ge(veps_done, t + 1)
                            nc.gpsimd.tensor_tensor(rstd[:, t:t + 1], veps[:, t:t + 1], nhalf[:, :], ALU.pow).then_inc(rstd_done, 1)

                    @block.vector
                    def _(dve):
                        for t in range(NT):
                            dve.wait_ge(v_ps, t + 1)
                            nc.vector.tensor_tensor(V[:, t, :], psO[t % 2][:, 0:C], cb[:, :], ALU.add).then_inc(v_done, 1)
                        dve.wait_ge(x_in, 32)

                        def row_max(t):
                            dve.wait_ge(s_ps, t + 1)
                            nc.vector.tensor_reduce(nmax[:, t:t + 1], psS[t % 2][:, 0:(t + 1) * P], X, ALU.max,
                                                    negate=True).then_inc(max_done, 1)

                        def normalise(t):
                            dve.wait_ge(rstd_done, t + 1)
                            nc.vector.tensor_scalar(y[:, t, :], y[:, t, :], mv[:, t, 0:1], rstd[:, t:t + 1],
                                                    ALU.subtract, ALU.mult).then_inc(ln_done, 1)

                        row_max(0)
                        for t in range(NT):
                            if t + 1 < NT:
                                row_max(t + 1)
                            for i in range(first_group[t], last_group[t] + 1):
                                _, g, n = groups[i]
                                dve.wait_ge(t_ps, i + 1)
                                if t >= 2:
                                    dve.wait_ge(o_ps, t - 1)
                                nc.vector.tensor_copy(probT[:, t % 2, g * P:(g + n) * P], psT[i % 2][:, 0:n * P]).then_inc(t_done, 1)
                            if t >= 1:
                                normalise(t - 1)
                            dve.wait_ge(exp_done, t + 1)
                            nc.vector.reciprocal(rinv[:, t:t + 1], rsum[:, t:t + 1]).then_inc(rinv_done, 1)
                            dve.wait_ge(rinv_done, t + 1)
                            dve.wait_ge(o_ps, t + 1)
                            nc.vector.scalar_tensor_tensor(out=y[:, t, :], in0=psO[t % 2][:, 0:C], scalar=rinv[:, t:t + 1],
                                                           in1=xn[:, t, :], op0=ALU.mult, op1=ALU.add).then_inc(y_done, 1)
                            dve.wait_ge(y_done, t + 1)
                            nc.vector.bn_stats(stats[:, t, :], y[:, t, :]).then_inc(st_done, 1)
                            dve.wait_ge(st_done, 2 * t + 1)
                            nc.vector.bn_aggr(mv[:, t, :], stats[:, t, :]).then_inc(st_done, 1)
                            dve.wait_ge(st_done, 2 * t + 2)
                            nc.vector.tensor_scalar(veps[:, t:t + 1], mv[:, t, 1:2], EPS, None, ALU.add).then_inc(veps_done, 1)
                        normalise(NT - 1)
                s.clear()


def keys_and_values2(nc, io, w):
    Wq, K, V, Wout = w["Wq"], w["K"], w["V"], w["Wout"]
    with Scope(nc, "keys2") as s:
        ctxT = s.sb("ctxT", [KP2, KT2, J])
        Wk = s.sb("Wk", [KP2, KT2, INNER])
        Wv = s.sb("Wv", [KP2, KT2, INNER])
        Wqf = s.sb("Wqf", [P, CT, INNER])
        kf = s.sb("kf", [P, 2, J])
        ksum = s.sb("ksum", [P, H2])
        kb = s.sb("kb", [P, H2])
        psK = [s.ps(f"psK{i}", [P, 2, 512]) for i in range(2)]
        psV = [s.ps(f"psV{i}", [P, 512]) for i in range(2)]
        c_in, q_in, w_in, consts = s.sem("c_in"), s.sem("q_in"), s.sem("w_in"), s.sem("consts")
        k_ps, k_sum, kb_done, k_done = s.sem("k_ps"), s.sem("k_sum"), s.sem("kb_done"), s.sem("k_done")
        q_hi, v_ps, v_hi, v_lo = s.sem("q_hi"), s.sem("v_ps"), s.sem("v_hi"), s.sem("v_lo")
        pieces = [(j, min(P, J - j * P), n) for j in range(JT) for n in range(INNER // 512)]

        with nc.Block(no_gpsimd_drain=True) as block:
            @block.sync
            def _(sp):
                sp.dma_start(ctxT[:, :, :], io["ctxT"].rearrange("(k p) j -> p k j", p=KP2)).then_inc(c_in, 16)
                sp.dma_start(Wk[:, :, :], io["Wk2"].rearrange("(k p) d -> p k d", p=KP2)).then_inc(c_in, 16)
                sp.dma_start(Wqf[:, :, :], io["Wq2"].rearrange("(k p) d -> p k d", p=P)).then_inc(q_in, 16)
                sp.dma_start(Wv[:, :, :], io["Wv2"].rearrange("(k p) d -> p k d", p=KP2)).then_inc(c_in, 16)
                sp.dma_start(Wout[:, :, :], io["Wout"].rearrange("(h p) e -> p h e", p=P)).then_inc(w_in, 16)
                sp.dma_start(w["bout"][:, :], io["bout"].partition_broadcast(P)).then_inc(w_in, 16)
                sp.dma_start(w["ident"][:, :], io["ident"]).then_inc(w_in, 16)
                sp.wait_ge(w_in, 48)

            @block.gpsimd
            def _(pool):
                nc.gpsimd.memset(w["nhalf"][:, :], -0.5).then_inc(consts, 1)
                pool.wait_ge(consts, 1)

            @block.tensor
            def _(pe):
                pe.wait_ge(c_in, 48)
                for h in range(H2):
                    if h >= 2:
                        pe.wait_ge(k_sum, h - 1)
                    for a in range(2):
                        for k in range(KT2):
                            last = nc.tensor.matmul(psK[h % 2][:, a, 0:JH], Wk[:, k, h * D2:(h + 1) * D2],
                                                    ctxT[:, k, a * JH:(a + 1) * JH], start=(k == 0), stop=(k == KT2 - 1))
                    last.then_inc(k_ps, 1)
                for i, (j, rows, n) in enumerate(pieces):
                    if i >= 2:
                        pe.wait_ge(v_lo, i - 1)
                    for k in range(KT2):
                        last = nc.tensor.matmul(psV[i % 2][0:rows, :], ctxT[:, k, j * P:j * P + rows],
                                                Wv[:, k, n * 512:(n + 1) * 512], start=(k == 0), stop=(k == KT2 - 1))
                    last.then_inc(v_ps, 1)

            @block.scalar
            def _(act):
                for h in range(H2):
                    act.wait_ge(k_ps, h + 1)
                    if h >= 2:
                        act.wait_ge(k_done, 3 * (h - 1))
                    nc.scalar.activation(kf[:, h % 2, :].rearrange("p (a w) -> p a w", a=2), psK[h % 2][:, :, 0:JH],
                                         ACT.Copy, accum_out=ksum[:, h:h + 1]).then_inc(k_sum, 1)
                act.wait_ge(q_in, 16)
                nc.scalar.activation(Wq[0][:, :, :], Wqf[:, :, :], ACT.Copy).then_inc(q_hi, 1)
                for i, (j, rows, n) in enumerate(pieces):
                    act.wait_ge(v_ps, i + 1)
                    nc.scalar.activation(V[0][0:rows, j, n * 512:(n + 1) * 512], psV[i % 2][0:rows, :], ACT.Copy).then_inc(v_hi, 1)

            @block.vector
            def _(dve):
                for h in range(H2):
                    dve.wait_ge(k_sum, h + 1)
                    nc.vector.tensor_scalar(kb[:, h:h + 1], ksum[:, h:h + 1], (1.0 - SHARPEN) * SCALE2 / J, None,
                                            ALU.mult).then_inc(kb_done, 1)
                    dve.wait_ge(kb_done, h + 1)
                    nc.vector.tensor_scalar(kf[:, h % 2, :], kf[:, h % 2, :], SHARPEN * SCALE2, kb[:, h:h + 1],
                                            ALU.mult, ALU.add).then_inc(k_done, 1)
                    dve.wait_ge(k_done, 3 * h + 1)
                    nc.vector.tensor_copy(K[0][:, h, :], kf[:, h % 2, :]).then_inc(k_done, 1)
                    dve.wait_ge(k_done, 3 * h + 2)
                    nc.vector.tensor_tensor(K[1][:, h, :], kf[:, h % 2, :], K[0][:, h, :].bitcast(F32),
                                            ALU.subtract).then_inc(k_done, 1)
                dve.wait_ge(q_hi, 1)
                nc.vector.tensor_tensor(Wq[1][:, :, :], Wqf[:, :, :], Wq[0][:, :, :].bitcast(F32), ALU.subtract)
                for i, (j, rows, n) in enumerate(pieces):
                    dve.wait_ge(v_hi, i + 1)
                    nc.vector.tensor_tensor(V[1][0:rows, j, n * 512:(n + 1) * 512], psV[i % 2][0:rows, :],
                                            V[0][0:rows, j, n * 512:(n + 1) * 512].bitcast(F32), ALU.subtract).then_inc(v_lo, 1)
        s.clear()


def layer2(nc, io, x_prev, x_next):
    with Scope(nc, "keep2") as keep:
        w = dict(Wq=[keep.sb(f"Wq{i}", [P, CT, INNER], F32R) for i in range(2)],
                 K=[keep.sb(f"K{i}", [P, H2, J], F32R) for i in range(2)],
                 V=[keep.sb(f"V{i}", [P, JT, INNER], F32R) for i in range(2)],
                 Wout=keep.sb("Wout", [P, H2, C]), bout=keep.sb("bout", [P, C]), ident=keep.sb("ident", [P, P]),
                 nhalf=keep.sb("nhalf", [P, 1]))
        keys_and_values2(nc, io, w)
        Wq, K, V, Wout, ident = w["Wq"], w["K"], w["V"], w["Wout"], w["ident"]
        with Scope(nc, "attn2") as s:
            xn = s.sb("xn", [P, NT, C])
            xb = s.sb("xb", [P, NT, C])
            xT = [s.sb(f"xT{i}", [P, CT, T], F32R) for i in range(2)]
            q = [s.sb(f"q{i}", [P, 2, CHUNK], F32R) for i in range(2)]
            prob = s.sb("prob", [P, 2 * TPC, J])
            pT = [s.sb(f"pT{i}", [P, 3, CHUNK], F32R) for i in range(2)]
            outT = s.sb("outT", [P, H2, CHUNK])
            y = s.sb("y", [P, NT, C])
            NS = CHUNKS * H2 * TPC
            nmax = s.sb("nmax", [P, NS])
            rsum = s.sb("rsum", [P, NS])
            rinv = s.sb("rinv", [P, NS])
            stats = s.sb("stats", [P, NT, 6])
            mv = s.sb("mv", [P, NT, 2])
            veps = s.sb("veps", [P, NT])
            rstd = s.sb("rstd", [P, NT])
            psS = [s.ps(f"psS{i}", [P, 2, 512]) for i in range(2)]
            psT = [s.ps(f"psT{i}", [P, 512]) for i in range(2)]
            psQ = s.ps("psQ", [P, 512])
            psO = s.ps("psO", [P, 512])

            x_in, xb_done = s.sem("x_in"), s.sem("xb_done")
            q_ps, q_hi, q_lo = s.sem("q_ps"), s.sem("q_hi"), s.sem("q_lo")
            s_ps, max_done, exp_done, rinv_done, norm_done = (
                s.sem(n) for n in ("s_ps", "max_done", "exp_done", "rinv_done", "norm_done"))
            slot_ps, slot_hi, slot_free = s.sem("slot_ps"), s.sem("slot_hi"), s.sem("slot_free")
            pv_ps, o_done = s.sem("pv_ps"), s.sem("o_done")
            y_done, st_done, veps_done, rstd_done, ln_done, out_st = (
                s.sem(n) for n in ("y_done", "st_done", "veps_done", "rstd_done", "ln_done", "out_st"))

            UNITS = CHUNKS * H2
            slots = [("x", c, k) for c in range(CHUNKS) for k in range(CT)]
            for u in range(UNITS):
                slots += [("p", u, j) for j in range(JT)]
                if u % H2 == H2 - 1:
                    slots += [("y", u // H2, t) for t in range(TPC)]
            at = {name: i for i, name in enumerate(slots)}
            his = {name: sum(n[0] != "y" for n in slots[:i + 1]) for name, i in at.items()}

            with nc.Fori(0, B) as b:
                with nc.Block(no_gpsimd_drain=True) as block:
                    @block.sync
                    def _(sp):
                        sp.dma_start(xn[:, :, :], x_prev[bass.ts(b, T), :].rearrange("(n p) c -> p n c", p=P)).then_inc(x_in, 16)
                        sp.wait_ge(ln_done, NT)
                        sp.dma_start(x_next[bass.ts(b, T), :].rearrange("(n p) c -> p n c", p=P), y[:, :, :]).then_inc(out_st, 16)
                        sp.wait_ge(out_st, 16)

                    @block.gpsimd
                    def _(pool):
                        pool.wait_ge(x_in, 16)
                        for t in range(NT):
                            nc.gpsimd.tensor_tensor(xb[:, t, :], xn[:, t, :], w["bout"][:, :], ALU.add).then_inc(xb_done, 1)
                        for t in range(NT):
                            pool.wait_ge(veps_done, t + 1)
                            nc.gpsimd.tensor_tensor(rstd[:, t:t + 1], veps[:, t:t + 1], w["nhalf"][:, :], ALU.pow).then_inc(rstd_done, 1)

                    @block.tensor
                    def _(pe):
                        def take(name):
                            if at[name] >= 2:
                                pe.wait_ge(slot_free, at[name] - 1)
                            return psT[at[name] % 2]

                        def project_q(u):
                            c, h = divmod(u, H2)
                            if u >= 1:
                                pe.wait_ge(q_lo, u)
                            for k in range(CT):
                                last = mm3(nc, psQ[:, :], [a[:, k, h * D2:(h + 1) * D2] for a in Wq],
                                           [a[:, k, c * CHUNK:(c + 1) * CHUNK] for a in xT], k == 0, k == CT - 1)
                            last.then_inc(q_ps, 1)

                        def scores(u, t):
                            n = TPC * u + t
                            if t == 0:
                                pe.wait_ge(q_lo, u + 1)
                            if n >= 2:
                                pe.wait_ge(exp_done, n - 1)
                            for a in range(2):
                                last = mm3(nc, psS[n % 2][:, a, 0:JH], [z[:, u % 2, t * P:(t + 1) * P] for z in q],
                                           [z[:, u % H2, a * JH:(a + 1) * JH] for z in K], True, True)
                            last.then_inc(s_ps, 1)

                        def transpose_block(u, j):
                            rows = min(P, J - j * P)
                            bank = take(("p", u, j))
                            if j == 0:
                                pe.wait_ge(norm_done, TPC * (u + 1))
                            for t in range(TPC):
                                last = nc.tensor.transpose(bank[0:rows, t * P:(t + 1) * P],
                                                           prob[:, u % 2 * TPC + t, j * P:j * P + rows], ident[:, :])
                            last.then_inc(slot_ps, 1)

                        def weighted(u, j):
                            rows = min(P, J - j * P)
                            h = u % H2
                            pe.wait_ge(slot_free, at["p", u, j] + 1)
                            if j == 0 and u >= 1:
                                pe.wait_ge(o_done, u)
                            mm3(nc, psO[:, :], [z[0:rows, j, h * D2:(h + 1) * D2] for z in V],
                                [z[0:rows, (JT * u + j) % 3, :] for z in pT], j == 0, j == JT - 1).then_inc(pv_ps, 1)

                        def project_out(c, t):
                            bank = take(("y", c, t))
                            pe.wait_ge(o_done, (c + 1) * H2)
                            for h in range(H2):
                                last = nc.tensor.matmul(bank[:, 0:C], outT[:, h, t * P:(t + 1) * P], Wout[:, h, :],
                                                        start=(h == 0), stop=(h == H2 - 1))
                            last.then_inc(slot_ps, 1)

                        pe.wait_ge(x_in, 16)
                        for c in range(CHUNKS):
                            for k in range(CT):
                                bank = take(("x", c, k))
                                for t in range(TPC):
                                    last = nc.tensor.transpose(bank[:, t * P:(t + 1) * P],
                                                               xn[:, c * TPC + t, k * P:(k + 1) * P], ident[:, :])
                                last.then_inc(slot_ps, 1)
                        pe.wait_ge(slot_free, CHUNKS * CT)
                        project_q(0)
                        for u in range(UNITS + 1):
                            now, past = u < UNITS, u >= 1
                            if now:
                                scores(u, 0)
                            if past:
                                transpose_block(u - 1, 0)
                                transpose_block(u - 1, 1)
                            if now:
                                scores(u, 1)
                            if past:
                                weighted(u - 1, 0)
                                transpose_block(u - 1, 2)
                            if now:
                                scores(u, 2)
                            if past:
                                weighted(u - 1, 1)
                                transpose_block(u - 1, 3)
                            if now:
                                scores(u, 3)
                            if past:
                                weighted(u - 1, 2)
                                transpose_block(u - 1, 4)
                                weighted(u - 1, 3)
                                weighted(u - 1, 4)
                            if u + 1 < UNITS:
                                project_q(u + 1)
                            if past and u % H2 == 0:
                                for t in range(TPC):
                                    project_out((u - 1) // H2, t)

                    @block.scalar
                    def _(act):
                        def x_high(c, k):
                            act.wait_ge(slot_ps, at["x", c, k] + 1)
                            nc.scalar.activation(xT[0][:, k, c * CHUNK:(c + 1) * CHUNK], psT[at["x", c, k] % 2][:, :],
                                                 ACT.Copy).then_inc(slot_hi, 1)

                        def exps(u, t):
                            n = TPC * u + t
                            act.wait_ge(max_done, n + 1)
                            if u >= 2 and t == 0:
                                act.wait_ge(slot_ps, at["p", u - 2, JT - 1] + 1)
                            nc.scalar.activation(prob[:, u % 2 * TPC + t, :].rearrange("p (a w) -> p a w", a=2),
                                                 psS[n % 2][:, :, 0:JH], ACT.Exp, bias=nmax[:, n:n + 1],
                                                 accum_out=rsum[:, n:n + 1]).then_inc(exp_done, 1)

                        def p_high(u, j):
                            rows, g = min(P, J - j * P), JT * u + j
                            act.wait_ge(slot_ps, at["p", u, j] + 1)
                            if g >= 3:
                                act.wait_ge(pv_ps, g - 2)
                            nc.scalar.activation(pT[0][0:rows, g % 3, :], psT[at["p", u, j] % 2][0:rows, :],
                                                 ACT.Copy).then_inc(slot_hi, 1)

                        def q_high(u):
                            act.wait_ge(q_ps, u + 1)
                            if u >= 2:
                                act.wait_ge(s_ps, TPC * (u - 1))
                            nc.scalar.activation(q[0][:, u % 2, :], psQ[:, :], ACT.Copy).then_inc(q_hi, 1)

                        for c in range(CHUNKS):
                            for k in range(CT):
                                x_high(c, k)
                        q_high(0)
                        for u in range(UNITS + 1):
                            now, past = u < UNITS, u >= 1
                            if now:
                                exps(u, 0)
                            if past:
                                p_high(u - 1, 0)
                                p_high(u - 1, 1)
                            if now:
                                exps(u, 1)
                            if past:
                                p_high(u - 1, 2)
                            if now:
                                exps(u, 2)
                            if past:
                                p_high(u - 1, 3)
                            if now:
                                exps(u, 3)
                            if past:
                                p_high(u - 1, 4)
                            if u + 1 < UNITS:
                                q_high(u + 1)

                    @block.vector
                    def _(dve):
                        def x_low(c, k):
                            dve.wait_ge(slot_hi, his["x", c, k])
                            nc.vector.tensor_tensor(xT[1][:, k, c * CHUNK:(c + 1) * CHUNK], psT[at["x", c, k] % 2][:, :],
                                                    xT[0][:, k, c * CHUNK:(c + 1) * CHUNK].bitcast(F32),
                                                    ALU.subtract).then_inc(slot_free, 1)

                        def row_max(u, t):
                            n = TPC * u + t
                            dve.wait_ge(s_ps, n + 1)
                            nc.vector.tensor_reduce(nmax[:, n:n + 1], psS[n % 2][:, :, 0:JH], XY, ALU.max,
                                                    negate=True).then_inc(max_done, 1)

                        def normalise_p(u, t):
                            n = TPC * u + t
                            dve.wait_ge(exp_done, n + 1)
                            nc.vector.reciprocal(rinv[:, n:n + 1], rsum[:, n:n + 1]).then_inc(rinv_done, 1)
                            dve.wait_ge(rinv_done, n + 1)
                            nc.vector.tensor_scalar(prob[:, u % 2 * TPC + t, :], prob[:, u % 2 * TPC + t, :],
                                                    rinv[:, n:n + 1], None, ALU.mult).then_inc(norm_done, 1)

                        def p_low(u, j):
                            rows, g = min(P, J - j * P), JT * u + j
                            dve.wait_ge(slot_hi, his["p", u, j])
                            nc.vector.tensor_tensor(pT[1][0:rows, g % 3, :], psT[at["p", u, j] % 2][0:rows, :],
                                                    pT[0][0:rows, g % 3, :].bitcast(F32), ALU.subtract).then_inc(slot_free, 1)

                        def q_low(u):
                            dve.wait_ge(q_hi, u + 1)
                            nc.vector.tensor_tensor(q[1][:, u % 2, :], psQ[:, :], q[0][:, u % 2, :].bitcast(F32),
                                                    ALU.subtract).then_inc(q_lo, 1)

                        def head_out(u):
                            dve.wait_ge(pv_ps, JT * (u + 1))
                            nc.vector.tensor_copy(outT[:, u % H2, :], psO[:, :]).then_inc(o_done, 1)

                        def residual(c, t):
                            n = c * TPC + t
                            dve.wait_ge(slot_ps, at["y", c, t] + 1)
                            dve.wait_ge(xb_done, NT)
                            nc.vector.tensor_tensor(y[:, n, :], psT[at["y", c, t] % 2][:, 0:C], xb[:, n, :],
                                                    ALU.add).then_inc(slot_free, 1)
                            dve.wait_ge(slot_free, at["y", c, t] + 1)
                            nc.vector.bn_stats(stats[:, n, :], y[:, n, :]).then_inc(st_done, 1)
                            dve.wait_ge(st_done, 2 * n + 1)
                            nc.vector.bn_aggr(mv[:, n, :], stats[:, n, :]).then_inc(st_done, 1)
                            dve.wait_ge(st_done, 2 * n + 2)
                            nc.vector.tensor_scalar(veps[:, n:n + 1], mv[:, n, 1:2], EPS, None, ALU.add).then_inc(veps_done, 1)

                        for c in range(CHUNKS):
                            for k in range(CT):
                                x_low(c, k)
                        q_low(0)
                        for u in range(UNITS + 1):
                            now, past = u < UNITS, u >= 1
                            if now:
                                row_max(u, 0)
                            if past:
                                p_low(u - 1, 0)
                                p_low(u - 1, 1)
                            if now:
                                row_max(u, 1)
                                normalise_p(u, 0)
                            if past:
                                p_low(u - 1, 2)
                            if now:
                                row_max(u, 2)
                                normalise_p(u, 1)
                            if past:
                                p_low(u - 1, 3)
                            if now:
                                row_max(u, 3)
                                normalise_p(u, 2)
                            if past:
                                p_low(u - 1, 4)
                            if now:
                                normalise_p(u, 3)
                            if past:
                                head_out(u - 1)
                            if u + 1 < UNITS:
                                q_low(u + 1)
                            if past and u % H2 == 0:
                                c = (u - 1) // H2
                                for t in range(TPC):
                                    residual(c, t)
                                for n in range(c * TPC, (c + 1) * TPC):
                                    dve.wait_ge(rstd_done, n + 1)
                                    nc.vector.tensor_scalar(y[:, n, :], y[:, n, :], mv[:, n, 0:1], rstd[:, n:n + 1],
                                                            ALU.subtract, ALU.mult).then_inc(ln_done, 1)
                s.clear()


def split(nc, block, name, s, pairs, ready, ready_at):
    hi_done, lo_done = s.sem(f"{name}_hi"), s.sem(f"{name}_lo")

    @block.scalar
    def _(act):
        act.wait_ge(ready, ready_at)
        for full, (hi, lo) in pairs:
            nc.scalar.activation(hi, full, ACT.Copy).then_inc(hi_done, 1)

    @block.vector
    def _(dve):
        for n, (full, (hi, lo)) in enumerate(pairs):
            dve.wait_ge(hi_done, n + 1)
            nc.vector.tensor_tensor(lo, full, hi.bitcast(F32), ALU.subtract).then_inc(lo_done, 1)


def load_layer3(nc, io, w):
    with Scope(nc, "load3") as s:
        Wf = s.sb("Wf", [P, CT, 4 * C])
        selF = s.sb("selF", [P, 16, P])
        maskf = s.sb("maskf", [P, 2, P])
        w_in, consts = s.sem("w_in"), s.sem("consts")
        with nc.Block(no_gpsimd_drain=True) as block:
            @block.sync
            def _(sp):
                loads = [(Wf[:, :, 0:3 * C], io["Win"].rearrange("(k p) d -> p k d", p=P)),
                         (Wf[:, :, 3 * C:4 * C], io["Wo3"].rearrange("(k p) d -> p k d", p=P)),
                         (selF[:, :, :], io["sel"].rearrange("n p m -> p n m")),
                         (w["bqk"][:, :], io["bqk"]), (w["ones_row"][:, :], io["ones_row"]),
                         (w["cos"][:, :, :], io["cos"].rearrange("(n p) d -> p n d", p=P)),
                         (w["sin"][:, :, :], io["sin"].rearrange("(n p) d -> p n d", p=P)),
                         (w["ident"][:, :], io["ident"]),
                         (maskf[:, 0, :], io["mask"]), (maskf[:, 1, :], io["maskT"])]
                loads += [(w[n][:, :], io[n].partition_broadcast(P)) for n in ("bv", "bo", "ln1w", "ln1b")]
                for dst, src in loads:
                    sp.dma_start(dst, src).then_inc(w_in, 16)
                sp.wait_ge(w_in, 16 * len(loads))

            @block.gpsimd
            def _(pool):
                nc.gpsimd.memset(w["nhalf"][:, :], -0.5).then_inc(consts, 1)
                nc.gpsimd.memset(w["V"][:, :, :, :], 1.0).then_inc(consts, 1)
                pool.wait_ge(consts, 2)
            split(nc, block, "w", s, [(Wf[:, :, :], [w[f"W{i}"][:, :, :] for i in range(2)])], w_in, 224)

            @block.scalar
            def _(act):
                nc.scalar.activation(w["sel"][:, :, :], selF[:, :, :], ACT.Copy)
                nc.scalar.activation(w["identb"][:, :], w["ident"][:, :], ACT.Copy)
                for i, name in enumerate(("maskb", "maskTb")):
                    nc.scalar.activation(w[name][:, :], maskf[:, i, :], ACT.Copy)
        s.clear()


def layer3_attention(nc, io, x_prev, x_next):
    with Scope(nc, "keep3") as keep:
        sb = keep.sb
        w = dict(W0=sb("W0", [P, CT, 4 * C], F32R), W1=sb("W1", [P, CT, 4 * C], F32R), sel=sb("sel", [P, 16, P], F32R),
                 bqk=sb("bqk", [P, 4]), ones_row=sb("ones_row", [P, 1]), cos=sb("cos", [P, NT, D3]),
                 sin=sb("sin", [P, NT, D3]), ident=sb("ident", [P, P]), identb=sb("identb", [P, P], BF16),
                 maskb=sb("maskb", [P, P], BF16), maskTb=sb("maskTb", [P, P], BF16), bv=sb("bv", [P, C]),
                 bo=sb("bo", [P, C]), ln1w=sb("ln1w", [P, C]), ln1b=sb("ln1b", [P, C]), nhalf=sb("nhalf", [P, 1]),
                 V=sb("V", [P, NT, H3, D3 + 1]))
        load_layer3(nc, io, w)
        W = [w["W0"], w["W1"]]
        sel, V, ident, identb = w["sel"], w["V"], w["ident"], w["identb"]
        xn = sb("xn", [P, NT, C])
        qs = sb("qs", [P, PAIRS, T], F32R)
        ks = sb("ks", [P, PAIRS, T], F32R)
        ctx = sb("ctx", [P, NT, C])

        with nc.Fori(0, B) as b:
            with Scope(nc, "proj3") as s:
                rope = s.sb("rope", [P, NT, C])
                rope2 = s.sb("rope2", [P, NT, C])
                xT = [s.sb(f"xT{i}", [P, CT, T], F32R) for i in range(2)]
                rT = [s.sb(f"rT{i}", [P, CT, T], F32R) for i in range(2)]
                qk = [s.sb(f"qk{i}", [P, 2 * CT, T], F32R) for i in range(2)]
                NB = 8
                bank = [s.ps(f"bank{i}", [P, 512]) for i in range(NB)]
                x_in, rope_done, slot_ps, act_read, dve_read = (
                    s.sem(n) for n in ("x_in", "rope_done", "slot_ps", "act_read", "dve_read"))
                slots = [("x", c, k) for c in range(CHUNKS) for k in range(CT)]
                slots += [("v", t, 0) for t in range(NT)]
                slots += [("r", c, k) for c in range(CHUNKS) for k in range(CT)]
                slots += [("qk", m, c) for m in range(2 * CT) for c in range(CHUNKS)]
                slots += [(z, g, c) for g in range(PAIRS) for c in range(CHUNKS) for z in ("sq", "sk")]
                at = {n: i for i, n in enumerate(slots)}
                by_act = {n: sum(m[0] in ("x", "r", "qk", "sk") for m in slots[:i + 1]) for n, i in at.items()}
                by_dve = {n: sum(m[0] != "sk" for m in slots[:i + 1]) for n, i in at.items()}

                with nc.Block(no_gpsimd_drain=True) as block:
                    @block.sync
                    def _(sp):
                        sp.dma_start(xn[:, :, :], x_prev[bass.ts(b, T), :].rearrange("(n p) c -> p n c", p=P)).then_inc(x_in, 16)

                    @block.tensor
                    def _(pe):
                        def take(name):
                            i = at[name]
                            if i >= NB:
                                before = slots[i - NB]
                                if before[0] == "sk":
                                    pe.wait_ge(act_read, by_act[before])
                                else:
                                    pe.wait_ge(dve_read, by_dve[before])
                            return bank[i % NB]

                        pe.wait_ge(x_in, 16)
                        for name in slots:
                            kind, a, c = name
                            if kind == "r" and a == 0 and c == 0:
                                pe.wait_ge(rope_done, 4)
                            if kind == "v" and a == 0:
                                pe.wait_ge(dve_read, by_dve["x", CHUNKS - 1, CT - 1])
                            if kind == "qk" and a == 0 and c == 0:
                                pe.wait_ge(dve_read, by_dve["r", CHUNKS - 1, CT - 1])
                            if kind == "sq" and a % 4 == 0 and c == 0:
                                pe.wait_ge(dve_read, by_dve["qk", 2 * CT - 1, CHUNKS - 1])
                            ps = take(name)
                            if kind in "xr":
                                src = xn if kind == "x" else rope
                                for t in range(TPC):
                                    last = nc.tensor.transpose(ps[:, t * P:(t + 1) * P],
                                                               src[:, a * TPC + t, c * P:(c + 1) * P], ident[:, :])
                            elif kind == "v":
                                for k in range(CT):
                                    last = mm3(nc, ps[:, 0:C], [z[:, k, a * P:(a + 1) * P] for z in xT],
                                               [z[:, k, 2 * C:3 * C] for z in W], k == 0, k == CT - 1)
                            elif kind == "qk":
                                for k in range(CT):
                                    last = mm3(nc, ps[:, :], [z[:, k, a * P:(a + 1) * P] for z in W],
                                               [z[:, k, c * CHUNK:(c + 1) * CHUNK] for z in rT], k == 0, k == CT - 1)
                            else:
                                n, m = (0, 0) if kind == "sq" else (8, CT)
                                for i in range(2):
                                    last = nc.tensor.matmul(ps[:, :], sel[:, n + 2 * (a % 4) + i, :],
                                                            qk[i][:, m + a // 4, c * CHUNK:(c + 1) * CHUNK],
                                                            start=(i == 0), stop=(i == 1))
                            last.then_inc(slot_ps, 1)

                    @block.scalar
                    def _(act):
                        for name in slots:
                            kind, a, c = name
                            ps, cols = bank[at[name] % NB], slice(c * CHUNK, (c + 1) * CHUNK)
                            if kind in ("v", "sq"):
                                continue
                            act.wait_ge(slot_ps, at[name] + 1)
                            if kind in "xr":
                                dst = (xT if kind == "x" else rT)[0][:, c, a * CHUNK:(a + 1) * CHUNK]
                                i = nc.scalar.activation(dst, ps[:, :], ACT.Copy)
                            elif kind == "qk":
                                i = nc.scalar.activation(qk[0][:, a, cols], ps[:, :], ACT.Identity, bias=w["bqk"][:, a:a + 1])
                            else:
                                i = nc.scalar.activation(ks[:, a, cols], ps[:, :], ACT.Identity, bias=w["ones_row"][:, 0:1])
                            i.then_inc(act_read, 1)

                    @block.vector
                    def _(dve):
                        dve.wait_ge(x_in, 16)
                        x4 = xn[:, :, :].rearrange("p n (h i two) -> p n h i two", h=H3, two=2)
                        r4 = rope2[:, :, :].rearrange("p n (h i two) -> p n h i two", h=H3, two=2)
                        cosb = w["cos"][:, :, :].unsqueeze(2).to_broadcast([P, NT, H3, D3])
                        sin4 = w["sin"][:, :, :].rearrange("p n (i two) -> p n i two", two=2)
                        nc.vector.tensor_tensor(rope[:, :, :].rearrange("p n (h d) -> p n h d", h=H3),
                                                xn[:, :, :].rearrange("p n (h d) -> p n h d", h=H3), cosb, ALU.mult).then_inc(rope_done, 1)
                        for z in range(2):
                            nc.vector.tensor_tensor(r4[:, :, :, :, z], x4[:, :, :, :, 1 - z],
                                                    sin4[:, :, :, z].unsqueeze(2).to_broadcast([P, NT, H3, D3 // 2]),
                                                    ALU.mult).then_inc(rope_done, 1)
                        dve.wait_ge(rope_done, 3)
                        nc.vector.tensor_tensor(rope[:, :, :], rope[:, :, :], rope2[:, :, :], ALU.add).then_inc(rope_done, 1)
                        for name in slots:
                            kind, a, c = name
                            ps, cols = bank[at[name] % NB], slice(c * CHUNK, (c + 1) * CHUNK)
                            if kind == "sk":
                                continue
                            if kind in ("x", "r", "qk"):
                                dve.wait_ge(act_read, by_act[name])
                            else:
                                dve.wait_ge(slot_ps, at[name] + 1)
                            if kind in "xr":
                                hi, lo = [z[:, c, a * CHUNK:(a + 1) * CHUNK] for z in (xT if kind == "x" else rT)]
                                i = nc.vector.tensor_tensor(lo, ps[:, :], hi.bitcast(F32), ALU.subtract)
                            elif kind == "v":
                                i = nc.vector.tensor_tensor(V[:, a, :, 0:D3], ps[:, 0:C].rearrange("p (h d) -> p h d", h=H3),
                                                            w["bv"][:, :].rearrange("p (h d) -> p h d", h=H3), ALU.add)
                            elif kind == "qk":
                                i = nc.vector.scalar_tensor_tensor(out=qk[1][:, a, cols], in0=ps[:, :], scalar=w["bqk"][:, a:a + 1],
                                                                   in1=qk[0][:, a, cols].bitcast(F32), op0=ALU.add, op1=ALU.subtract)
                            else:
                                i = nc.vector.tensor_copy(qs[:, a, cols], ps[:, :])
                            i.then_inc(dve_read, 1)
                s.clear()

            with Scope(nc, "max3") as s:
                mx = s.sb("mx", [P, NT, 2, H3])
                mf = s.sb("mf", [P, NT, H3])
                mT = s.sb("mT", [H3, T], F32R)
                psS = [s.ps(f"psS{i}", [P, 4, 512]) for i in range(2)]
                s_ps, max_done, mf_done, t_ps, mT_done, rows_in = (
                    s.sem(n) for n in ("s_ps", "max_done", "mf_done", "t_ps", "mT_done", "rows_in"))
                units = [(t, c, gg) for t in range(NT) for c in range(t // TPC + 1) for gg in range(PAIRS // 2)]

                def width(t, c):
                    return min(CHUNK, (t + 1) * P - c * CHUNK)

                with nc.Block(no_gpsimd_drain=True) as block:
                    @block.tensor
                    def _(pe):
                        for n, (t, c, gg) in enumerate(units):
                            if n >= 2:
                                pe.wait_ge(max_done, n - 1)
                            ps, wd, diag = psS[n % 2], width(t, c), c == t // TPC
                            for i in range(4):
                                g, rows = 2 * gg + i // 2, slice(64 * (i % 2), 64 * (i % 2) + 64)
                                last = nc.tensor.matmul(ps[:, i, 0:wd], qs[rows, g, t * P:(t + 1) * P],
                                                        ks[rows, g, c * CHUNK:c * CHUNK + wd], start=True, stop=not diag)
                            if diag:
                                for i in range(4):
                                    last = nc.tensor.matmul(ps[:, i, wd - P:wd], identb[:, :], w["maskb"][:, :],
                                                            start=False, stop=True)
                            last.then_inc(s_ps, 1)
                        pe.wait_ge(mf_done, 2)
                        for t in range(NT):
                            last = nc.tensor.transpose(psS[0][0:H3, t // TPC, t % TPC * P:(t % TPC + 1) * P], mf[:, t, :], ident[:, :])
                        last.then_inc(t_ps, 1)

                    @block.vector
                    def _(dve):
                        for n, (t, c, gg) in enumerate(units):
                            dve.wait_ge(s_ps, n + 1)
                            out = mx[:, t, c, :].rearrange("p (two g) -> p g two", two=2)[:, 2 * gg:2 * gg + 2, :]
                            nc.vector.tensor_reduce(out, psS[n % 2][:, :, 0:width(t, c)].rearrange("p (g two) w -> p g two w", two=2),
                                                    X, ALU.max).then_inc(max_done, 1)
                        dve.wait_ge(max_done, len(units))
                        nc.vector.tensor_copy(mf[:, 0:TPC, :], mx[:, 0:TPC, 0, :]).then_inc(mf_done, 1)
                        nc.vector.tensor_tensor(mf[:, TPC:NT, :], mx[:, TPC:NT, 0, :], mx[:, TPC:NT, 1, :], ALU.max).then_inc(mf_done, 1)

                    @block.scalar
                    def _(act):
                        act.wait_ge(t_ps, 1)
                        nc.scalar.activation(mT[:, :].rearrange("h (c t) -> h c t", c=CHUNKS), psS[0][0:H3, 0:CHUNKS, :],
                                             ACT.Copy, scale=-1.0).then_inc(mT_done, 1)

                    @block.sync
                    def _(sp):
                        sp.wait_ge(mT_done, 1)
                        for p in range(2):
                            for g in range(PAIRS):
                                sp.dma_start(qs[64 * p + 32:64 * p + 33, g, :].bitcast(F32), mT[8 * p + g:8 * p + g + 1, :].bitcast(F32)).then_inc(rows_in, 16)
                        sp.wait_ge(rows_in, 16 * H3)
                s.clear()

            with Scope(nc, "attn3") as s:
                pT = s.sb("pT", [P, 3, 2, CHUNK])
                rinv = s.sb("rinv", [P, 2, TPC, 2, 1])
                psS = [s.ps(f"psS{i}", [P, 2, 512]) for i in range(3)]
                psC = [s.ps(f"psC{i}", [P, TPC, 2, D3 + 1]) for i in range(2)]
                s_ps, exp_done, c_ps, r_done, c_done = (s.sem(n) for n in ("s_ps", "exp_done", "c_ps", "r_done", "c_done"))
                rounds = [(c, g) for c in range(CHUNKS) for g in range(PAIRS)]
                units = [(r, c, g, j) for r, (c, g) in enumerate(rounds) for j in range((c + 1) * TPC)]

                def span(c, j):
                    lo = max(j * P, c * CHUNK)
                    return lo, (c + 1) * CHUNK - lo, j * P >= c * CHUNK

                with nc.Block(no_gpsimd_drain=True) as block:
                    @block.tensor
                    def _(pe):
                        def scores(n):
                            r, c, g, j = units[n]
                            lo, wd, diag = span(c, j)
                            if n >= 3:
                                pe.wait_ge(exp_done, n - 2)
                            for p in range(2):
                                last = nc.tensor.matmul(psS[n % 3][:, p, 0:wd], ks[64 * p:64 * p + 64, g, j * P:(j + 1) * P],
                                                        qs[64 * p:64 * p + 64, g, lo:lo + wd], start=True, stop=not diag)
                            if diag:
                                for p in range(2):
                                    last = nc.tensor.matmul(psS[n % 3][:, p, 0:P], identb[:, :], w["maskTb"][:, :],
                                                            start=False, stop=True)
                            last.then_inc(s_ps, 1)

                        def weighted(n):
                            r, c, g, j = units[n]
                            lo, wd, diag = span(c, j)
                            pe.wait_ge(exp_done, n + 1)
                            if j == 0 and r >= 2:
                                pe.wait_ge(c_done, r - 1)
                            for p in range(2):
                                for i in range(wd // P):
                                    t = lo // P + i - c * TPC
                                    last = nc.tensor.matmul(psC[r % 2][:, t, p, :], pT[:, n % 3, p, i * P:(i + 1) * P],
                                                            V[:, j, 2 * g + p, :], start=(j == 0 and p == 0 and i == 0),
                                                            stop=(j == c * TPC + t), skip_group_check=True)
                            last.then_inc(c_ps, 1)

                        scores(0)
                        scores(1)
                        for n in range(len(units)):
                            if n + 2 < len(units):
                                scores(n + 2)
                            weighted(n)

                    @block.scalar
                    def _(act):
                        for n, (r, c, g, j) in enumerate(units):
                            act.wait_ge(s_ps, n + 1)
                            if n >= 3:
                                act.wait_ge(c_ps, n - 2)
                            wd = span(c, j)[1]
                            nc.scalar.activation(pT[:, n % 3, :, 0:wd], psS[n % 3][:, :, 0:wd], ACT.Exp, scale=SCALE3).then_inc(exp_done, 1)

                    @block.vector
                    def _(dve):
                        done = 0
                        for r, (c, g) in enumerate(rounds):
                            done += (c + 1) * TPC
                            dve.wait_ge(c_ps, done)
                            nc.vector.reciprocal(rinv[:, r % 2, :, :, :], psC[r % 2][:, :, :, D3:D3 + 1]).then_inc(r_done, 1)
                            dve.wait_ge(r_done, r + 1)
                            nc.vector.tensor_tensor(
                                ctx[:, c * TPC:(c + 1) * TPC, 2 * g * D3:(2 * g + 2) * D3].rearrange("p t (h d) -> p t h d", h=2),
                                psC[r % 2][:, :, :, 0:D3], rinv[:, r % 2, :, :, :].to_broadcast([P, TPC, 2, D3]),
                                ALU.mult).then_inc(c_done, 1)
                s.clear()

            with Scope(nc, "out3") as s:
                cT = [s.sb(f"cT{i}", [P, CT, T], F32R) for i in range(2)]
                y = s.sb("y", [P, NT, C])
                stats = s.sb("stats", [P, NT, 6])
                mv = s.sb("mv", [P, NT, 2])
                veps = s.sb("veps", [P, NT])
                rstd = s.sb("rstd", [P, NT])
                psT = [s.ps(f"psT{i}", [P, 512]) for i in range(4)]
                psY = [s.ps(f"psY{i}", [P, 512]) for i in range(4)]
                xb_done, t_ps, hi_done, lo_done, y_ps, y_done = (
                    s.sem(n) for n in ("xb_done", "t_ps", "hi_done", "lo_done", "y_ps", "y_done"))
                st_done, veps_done, rstd_done, ln_done, aff_done, out_st = (
                    s.sem(n) for n in ("st_done", "veps_done", "rstd_done", "ln_done", "aff_done", "out_st"))
                groups = [(c, k) for c in range(CHUNKS) for k in range(CT)]
                with nc.Block(no_gpsimd_drain=True) as block:
                    @block.sync
                    def _(sp):
                        sp.wait_ge(aff_done, 2 * NT)
                        sp.dma_start(x_next[bass.ts(b, T), :].rearrange("(n p) c -> p n c", p=P), y[:, :, :]).then_inc(out_st, 16)
                        sp.wait_ge(out_st, 16)

                    @block.tensor
                    def _(pe):
                        for n, (c, k) in enumerate(groups):
                            for t in range(TPC):
                                last = nc.tensor.transpose(psT[n][:, t * P:(t + 1) * P], ctx[:, c * TPC + t, k * P:(k + 1) * P], ident[:, :])
                            last.then_inc(t_ps, 1)
                        for t in range(NT):
                            pe.wait_ge(lo_done, CT * (t // TPC + 1))
                            if t >= 4:
                                pe.wait_ge(y_done, t - 3)
                            for k in range(CT):
                                last = mm3(nc, psY[t % 4][:, 0:C], [z[:, k, t * P:(t + 1) * P] for z in cT],
                                           [z[:, k, 3 * C:4 * C] for z in W], k == 0, k == CT - 1)
                            last.then_inc(y_ps, 1)

                    @block.scalar
                    def _(act):
                        for n, (c, k) in enumerate(groups):
                            act.wait_ge(t_ps, n + 1)
                            nc.scalar.activation(cT[0][:, k, c * CHUNK:(c + 1) * CHUNK], psT[n][:, :], ACT.Copy).then_inc(hi_done, 1)

                    @block.gpsimd
                    def _(pool):
                        for t in range(NT):
                            nc.gpsimd.tensor_tensor(xn[:, t, :], xn[:, t, :], w["bo"][:, :], ALU.add).then_inc(xb_done, 1)
                        for t in range(NT):
                            pool.wait_ge(veps_done, t + 1)
                            nc.gpsimd.tensor_tensor(rstd[:, t:t + 1], veps[:, t:t + 1], w["nhalf"][:, :], ALU.pow).then_inc(rstd_done, 1)

                    @block.vector
                    def _(dve):
                        for n, (c, k) in enumerate(groups):
                            dve.wait_ge(hi_done, n + 1)
                            cols = slice(c * CHUNK, (c + 1) * CHUNK)
                            nc.vector.tensor_tensor(cT[1][:, k, cols], psT[n][:, :], cT[0][:, k, cols].bitcast(F32), ALU.subtract).then_inc(lo_done, 1)

                        def affine(t):
                            dve.wait_ge(rstd_done, t + 1)
                            nc.vector.tensor_scalar(y[:, t, :], y[:, t, :], mv[:, t, 0:1], rstd[:, t:t + 1],
                                                    ALU.subtract, ALU.mult).then_inc(ln_done, 1)
                            dve.wait_ge(ln_done, t + 1)
                            nc.vector.tensor_tensor(y[:, t, :], y[:, t, :], w["ln1w"][:, :], ALU.mult).then_inc(aff_done, 1)
                            dve.wait_ge(aff_done, 2 * t + 1)
                            nc.vector.tensor_tensor(y[:, t, :], y[:, t, :], w["ln1b"][:, :], ALU.add).then_inc(aff_done, 1)

                        for t in range(NT):
                            dve.wait_ge(y_ps, t + 1)
                            dve.wait_ge(xb_done, t + 1)
                            nc.vector.tensor_tensor(y[:, t, :], psY[t % 4][:, 0:C], xn[:, t, :], ALU.add).then_inc(y_done, 1)
                            dve.wait_ge(y_done, t + 1)
                            nc.vector.bn_stats(stats[:, t, :], y[:, t, :]).then_inc(st_done, 1)
                            dve.wait_ge(st_done, 2 * t + 1)
                            nc.vector.bn_aggr(mv[:, t, :], stats[:, t, :]).then_inc(st_done, 1)
                            dve.wait_ge(st_done, 2 * t + 2)
                            nc.vector.tensor_scalar(veps[:, t:t + 1], mv[:, t, 1:2], EPS, None, ALU.add).then_inc(veps_done, 1)
                            if t >= 1:
                                affine(t - 1)
                        affine(NT - 1)
                s.clear()


def experts(nc, io, x_prev, x1_in, out):
    with Scope(nc, "keep4") as keep:
        sb = keep.sb
        We = [sb(f"We{i}", [P, CT, NE * C], F32R) for i in range(2)]
        Wg = [sb(f"Wg{i}", [P, CT, NE], F32R) for i in range(2)]
        eb = sb("eb", [NE, C])
        gb, ln2w, ln2b = sb("gb", [P, NE]), sb("ln2w", [P, C]), sb("ln2b", [P, C])
        ident, nhalf, number = sb("ident", [P, P]), sb("nhalf", [P, 1]), sb("number", [P, NE])
        with Scope(nc, "load4") as s:
            Wf = s.sb("Wf", [P, CT, NE * C])
            Wgf = s.sb("Wgf", [P, CT, NE])
            w_in, consts = s.sem("w_in"), s.sem("consts")
            with nc.Block(no_gpsimd_drain=True) as block:
                @block.sync
                def _(sp):
                    for dst, src in ((Wf[:, :, :], io["We"].rearrange("(k p) f -> p k f", p=P)),
                                     (Wgf[:, :, :], io["Wg"].rearrange("(k p) e -> p k e", p=P)), (eb[:, :], io["eb"]),
                                     (gb[:, :], io["gb"].partition_broadcast(P)), (ln2w[:, :], io["ln2w"].partition_broadcast(P)),
                                     (ln2b[:, :], io["ln2b"].partition_broadcast(P)), (ident[:, :], io["ident"]),
                                     (number[:, :], io["number"].partition_broadcast(P))):
                        sp.dma_start(dst, src).then_inc(w_in, 16)
                    sp.wait_ge(w_in, 128)

                @block.gpsimd
                def _(pool):
                    nc.gpsimd.memset(nhalf[:, :], -0.5).then_inc(consts, 1)
                    pool.wait_ge(consts, 1)
                split(nc, block, "w", s, [(Wf[:, k, :], [z[:, k, :] for z in We]) for k in range(CT)]
                      + [(Wgf[:, :, :], [z[:, :, :] for z in Wg])], w_in, 128)
            s.clear()

        with Scope(nc, "moe") as s:
            xn = s.sb("xn", [P, NT, C])
            x1 = s.sb("x1", [P, NT, C])
            xT = [s.sb(f"xT{i}", [P, CT, T], F32R) for i in range(2)]
            lg = s.sb("lg", [P, NT, NE])
            ex = s.sb("ex", [P, NT, NE])
            gate = s.sb("gate", [P, NT, NE])
            is1, is2 = s.sb("is1", [P, NT, NE]), s.sb("is2", [P, NT, NE])
            top = s.sb("top", [P, NT, 8])
            idx = s.sb("idx", [P, NT, 8], U32)
            idxf = s.sb("idxf", [P, NT, 8])
            gsum, ginv = s.sb("gsum", [P, NT]), s.sb("ginv", [P, NT])
            gT = s.sb("gT", [NE, T])
            acc = s.sb("acc", [P, NT, C])
            stats = s.sb("stats", [P, 2 * NT, 6])
            mv = s.sb("mv", [P, 2 * NT, 2])
            veps = s.sb("veps", [P, 2 * NT])
            rstd = s.sb("rstd", [P, 2 * NT])
            psE = [s.ps(f"psE{i}", [P, 2, C]) for i in range(6)]
            psB = [s.ps(f"psB{i}", [P, 512]) for i in range(2)]
            x_in, t_ps, hi_done, lo_done = s.sem("x_in"), s.sem("t_ps"), s.sem("hi_done"), s.sem("lo_done")
            g_ps, lg_done, top_done, ex_done, gate_step, gate_done, gT_ps, gT_done = (
                s.sem(n) for n in ("g_ps", "lg_done", "top_done", "ex_done", "gate_step", "gate_done", "gT_ps", "gT_done"))
            e_ps, e_done, b_ps, b_done = s.sem("e_ps"), s.sem("e_done"), s.sem("b_ps"), s.sem("b_done")
            st_done, veps_done, rstd_done, ln2_done, aff_w, aff_b, res_done, fin_done, out_st = (
                s.sem(n) for n in ("st_done", "veps_done", "rstd_done", "ln2_done", "aff_w", "aff_b", "res_done", "fin_done", "out_st"))
            groups = [(c, k) for c in range(CHUNKS) for k in range(CT)]
            EP = NE // 2
            norms = [("moe", 0)]
            for t in range(1, NT):
                norms += [("moe", t), ("out", t - 1)]
            norms.append(("out", NT - 1))
            nth = {name: n for n, name in enumerate(norms)}

            with nc.Fori(0, B) as b:
                with nc.Block(no_gpsimd_drain=True) as block:
                    @block.sync
                    def _(sp):
                        sp.dma_start(x1[:, :, :], x1_in[bass.ts(b, T), :].rearrange("(n p) c -> p n c", p=P)).then_inc(x_in, 16)
                        sp.dma_start(xn[:, :, :], x_prev[bass.ts(b, T), :].rearrange("(n p) c -> p n c", p=P)).then_inc(x_in, 16)
                        sp.wait_ge(fin_done, NT)
                        sp.dma_start(out[bass.ts(b, T), :].rearrange("(n p) c -> p n c", p=P), acc[:, :, :]).then_inc(out_st, 16)
                        sp.wait_ge(out_st, 16)

                    @block.tensor
                    def _(pe):
                        pe.wait_ge(x_in, 32)
                        for n, (c, k) in enumerate(groups):
                            for t in range(TPC):
                                last = nc.tensor.transpose(psE[n][:, t // 2, t % 2 * P:(t % 2 + 1) * P],
                                                           x1[:, c * TPC + t, k * P:(k + 1) * P], ident[:, :])
                            last.then_inc(t_ps, 1)
                        pe.wait_ge(lo_done, len(groups))
                        for t in range(NT):
                            for k in range(CT):
                                last = mm3(nc, psB[0][:, t * NE:(t + 1) * NE], [z[:, k, t * P:(t + 1) * P] for z in xT],
                                           [z[:, k, :] for z in Wg], k == 0, k == CT - 1)
                        last.then_inc(g_ps, 1)

                        def expert_pair(n):
                            t, e = divmod(n, EP)
                            if n >= 6:
                                pe.wait_ge(e_done, 2 * (n - 5))
                            for k in range(CT):
                                last = mm3(nc, psE[n % 6][:, :, :], [z[:, k, t * P:(t + 1) * P] for z in xT],
                                           [z[:, k, 2 * e * C:(2 * e + 2) * C] for z in We], k == 0, k == CT - 1)
                            last.then_inc(e_ps, 1)

                        for n in range(NT * EP):
                            expert_pair(n)
                            if n == 5:
                                pe.wait_ge(gate_done, 1)
                                for t in range(NT):
                                    last = nc.tensor.transpose(psB[t // TPC][0:NE, t % TPC * P:(t % TPC + 1) * P], gate[:, t, :], ident[:, :])
                                last.then_inc(gT_ps, 1)
                                pe.wait_ge(gT_done, 2)
                                for t in range(2):
                                    nc.tensor.matmul(psB[t][:, 0:C], gT[:, t * P:(t + 1) * P], eb[:, :], start=True, stop=True).then_inc(b_ps, 1)
                            if n % EP == EP - 1 and 2 <= n // EP + 1 < NT and n > 5:
                                t = n // EP + 1
                                pe.wait_ge(b_done, t - 1)
                                nc.tensor.matmul(psB[t % 2][:, 0:C], gT[:, t * P:(t + 1) * P], eb[:, :], start=True, stop=True).then_inc(b_ps, 1)

                    @block.scalar
                    def _(act):
                        for n, (c, k) in enumerate(groups):
                            act.wait_ge(t_ps, n + 1)
                            nc.scalar.activation(xT[0][:, k, c * CHUNK:(c + 1) * CHUNK], psE[n][:, :, :].rearrange("p a w -> p (a w)"),
                                                 ACT.Copy).then_inc(hi_done, 1)
                        act.wait_ge(gate_step, 1)
                        nc.scalar.activation(ex[:, :, :], ex[:, :, :], ACT.Exp).then_inc(ex_done, 1)
                        act.wait_ge(gT_ps, 1)
                        for c in range(CHUNKS):
                            nc.scalar.activation(gT[:, c * CHUNK:(c + 1) * CHUNK], psB[c][0:NE, :], ACT.Copy).then_inc(gT_done, 1)

                    @block.gpsimd
                    def _(pool):
                        for n in range(2 * NT):
                            pool.wait_ge(veps_done, n + 1)
                            i = nc.gpsimd.tensor_tensor(rstd[:, n:n + 1], veps[:, n:n + 1], nhalf[:, :], ALU.pow)
                            i.then_inc(rstd_done, 1)

                    @block.vector
                    def _(dve):
                        for n, (c, k) in enumerate(groups):
                            dve.wait_ge(hi_done, n + 1)
                            cols = slice(c * CHUNK, (c + 1) * CHUNK)
                            nc.vector.tensor_tensor(xT[1][:, k, cols], psE[n][:, :, :].rearrange("p a w -> p (a w)"),
                                                    xT[0][:, k, cols].bitcast(F32), ALU.subtract).then_inc(lo_done, 1)
                        dve.wait_ge(g_ps, 1)
                        nc.vector.tensor_tensor(lg[:, :, :], psB[0][:, 0:NT * NE].rearrange("p (t e) -> p t e", e=NE),
                                                gb[:, :].unsqueeze(1).to_broadcast([P, NT, NE]), ALU.add).then_inc(lg_done, 1)
                        dve.wait_ge(lg_done, 1)
                        for t in range(NT):
                            last = nc.vector.max(top[:, t, :], lg[:, t, :])
                        last.then_inc(top_done, 1)
                        dve.wait_ge(top_done, 1)
                        nc.vector.tensor_tensor(ex[:, :, :], lg[:, :, :], top[:, :, 0:1].to_broadcast([P, NT, NE]),
                                                ALU.subtract).then_inc(gate_step, 1)
                        for t in range(NT):
                            last = nc.vector.max_index(idx[:, t, :], top[:, t, :], lg[:, t, :])
                        last.then_inc(top_done, 1)
                        dve.wait_ge(top_done, 2)
                        nc.vector.tensor_copy(idxf[:, :, :], idx[:, :, :]).then_inc(gate_step, 1)
                        dve.wait_ge(gate_step, 2)
                        numbers = number[:, :].unsqueeze(1).to_broadcast([P, NT, NE])
                        nc.vector.tensor_tensor(is1[:, :, :], numbers, idxf[:, :, 0:1].to_broadcast([P, NT, NE]), ALU.is_equal).then_inc(gate_step, 1)
                        nc.vector.tensor_tensor(is2[:, :, :], numbers, idxf[:, :, 1:2].to_broadcast([P, NT, NE]), ALU.is_equal).then_inc(gate_step, 1)
                        dve.wait_ge(gate_step, 4)
                        nc.vector.tensor_tensor(is1[:, :, :], is1[:, :, :], is2[:, :, :], ALU.add).then_inc(gate_step, 1)
                        dve.wait_ge(ex_done, 1)
                        nc.vector.tensor_reduce(gsum[:, :], ex[:, :, :], X, ALU.add).then_inc(gate_step, 1)
                        dve.wait_ge(gate_step, 6)
                        nc.vector.reciprocal(ginv[:, :], gsum[:, :]).then_inc(gate_step, 1)
                        nc.vector.tensor_tensor(gate[:, :, :], ex[:, :, :], is1[:, :, :], ALU.mult).then_inc(gate_step, 1)
                        dve.wait_ge(gate_step, 8)
                        nc.vector.tensor_tensor(gate[:, :, :], gate[:, :, :], ginv[:, :].unsqueeze(2).to_broadcast([P, NT, NE]),
                                                ALU.mult).then_inc(gate_done, 1)

                        def statistics(n, src):
                            nc.vector.bn_stats(stats[:, n, :], src).then_inc(st_done, 1)
                            dve.wait_ge(st_done, 2 * n + 1)
                            nc.vector.bn_aggr(mv[:, n, :], stats[:, n, :]).then_inc(st_done, 1)
                            dve.wait_ge(st_done, 2 * n + 2)
                            nc.vector.tensor_scalar(veps[:, n:n + 1], mv[:, n, 1:2], EPS, None, ALU.add).then_inc(veps_done, 1)

                        def scaled(n, t, done):
                            dve.wait_ge(rstd_done, n + 1)
                            nc.vector.tensor_scalar(acc[:, t, :], acc[:, t, :], mv[:, n, 0:1], rstd[:, n:n + 1],
                                                    ALU.subtract, ALU.mult).then_inc(done, 1)

                        def ending(t):
                            scaled(nth["moe", t], t, ln2_done)
                            dve.wait_ge(ln2_done, t + 1)
                            nc.vector.tensor_tensor(acc[:, t, :], acc[:, t, :], ln2w[:, :], ALU.mult).then_inc(aff_w, 1)
                            dve.wait_ge(aff_w, t + 1)
                            nc.vector.tensor_tensor(acc[:, t, :], acc[:, t, :], ln2b[:, :], ALU.add).then_inc(aff_b, 1)
                            dve.wait_ge(aff_b, t + 1)
                            nc.vector.tensor_tensor(acc[:, t, :], acc[:, t, :], xn[:, t, :], ALU.add).then_inc(res_done, 1)
                            dve.wait_ge(res_done, t + 1)
                            statistics(nth["out", t], acc[:, t, :])

                        for t in range(NT):
                            dve.wait_ge(b_ps, t + 1)
                            if t == 0:
                                dve.wait_ge(gate_done, 1)
                            nc.vector.tensor_tensor(acc[:, t, :], psB[t % 2][:, 0:C], x1[:, t, :], ALU.add).then_inc(b_done, 1)
                            dve.wait_ge(b_done, t + 1)
                            for e in range(NE):
                                n = t * EP + e // 2
                                if e % 2 == 0:
                                    dve.wait_ge(e_ps, n + 1)
                                if t * NE + e > 0 and e > 0:
                                    dve.wait_ge(e_done, t * NE + e)
                                nc.vector.scalar_tensor_tensor(out=acc[:, t, :], in0=psE[n % 6][:, e % 2, :], scalar=gate[:, t, e:e + 1],
                                                               in1=acc[:, t, :], op0=ALU.mult, op1=ALU.add).then_inc(e_done, 1)
                            dve.wait_ge(e_done, (t + 1) * NE)
                            statistics(nth["moe", t], acc[:, t, :])
                            if t >= 2:
                                scaled(nth["out", t - 2], t - 2, fin_done)
                            if t >= 1:
                                ending(t - 1)
                        scaled(nth["out", NT - 2], NT - 2, fin_done)
                        ending(NT - 1)
                        scaled(nth["out", NT - 1], NT - 1, fin_done)
                s.clear()


def build(nc, io, out):
    x1, x2, x3 = (nc.dram_tensor(n, (TOKENS, C), F32).ap() for n in ("x_layer1", "x_layer2", "x_attended"))
    layer1(nc, io, x1)
    layer2(nc, io, x1, x2)
    layer3_attention(nc, io, x2, x3)
    experts(nc, io, x2, x3, out)


def lay_out(inputs):
    v = {k: np.asarray(a) for k, a in inputs.items()}
    c = np.ascontiguousarray
    x = v["x"].reshape(TOKENS, C)
    eye = np.eye(P, dtype=np.float32)
    later = np.triu(np.full((P, P), -1e30, np.float32), 1)
    a = dict(
        x=x, xT=c(x.T), WaT=c(v["L0_attn_W_attn"].T), AaT=c(v["L0_attn_lora_attn_A"].T), Ba=v["L0_attn_lora_attn_B"],
        ApT=c(v["L0_attn_lora_proj_A"].T), Bp=v["L0_attn_lora_proj_B"], Wp=v["L0_attn_W_proj"],
        WpT=c(v["L0_attn_W_proj"].T), gamma=c(v["L0_attn_bn_gamma"].reshape(DT, P).T),
        beta=c(v["L0_attn_bn_beta"].reshape(DT, P).T), ident=eye, mask=later)
    a.update(
        ctxT=c(v["ctx_768"].reshape(J, CD).T), Wq2=v["L0_xattn_Wq"], Wk2=v["L0_xattn_Wk"], Wv2=v["L0_xattn_Wv"],
        Wout=v["L0_xattn_Wout"], bout=v["L0_xattn_bout"])
    inverse = (1.0 / 10000.0 ** (np.arange(0, D3, 2, dtype=np.float32) / D3)).astype(np.float32)
    angle = np.arange(T, dtype=np.float32)[:, None] * inverse[None, :]
    cos, sin = np.cos(angle), np.sin(angle)
    sel = np.zeros((2, 4, 2, P, P), np.float32)
    d = np.arange(D3)
    for pair in range(4):
        for p in range(2):
            rows, base = (2 * pair + p) * D3 + d, 64 * p
            sel[0, pair, 0, rows, base + d] = 1
            sel[0, pair, 0, rows, base + D3 + d] = 1
            sel[0, pair, 1, rows, base + 3 * D3 + d] = 1
            sel[1, pair, 0, rows, base + d] = 1
            sel[1, pair, 0, rows, base + 3 * D3 + d] = 1
            sel[1, pair, 1, rows, base + D3 + d] = 1
    ones_row = np.zeros((P, 1), np.float32)
    ones_row[[32, 96]] = 1
    a.update(
        Win=c(v["L0_ffn_in_proj_w"].T), Wo3=c(v["L0_ffn_out_proj_w"].T),
        bqk=c(v["L0_ffn_in_proj_b"][:2 * C].reshape(2 * CT, P).T), bv=v["L0_ffn_in_proj_b"][2 * C:],
        bo=v["L0_ffn_out_proj_b"], ln1w=v["L0_ffn_ln1_w"], ln1b=v["L0_ffn_ln1_b"], ln2w=v["L0_ffn_ln2_w"], ln2b=v["L0_ffn_ln2_b"],
        Wg=c(v["L0_ffn_gate_w"].T), gb=v["L0_ffn_gate_b"], eb=v["L0_ffn_expert_b"],
        We=c(v["L0_ffn_expert_w"].transpose(2, 0, 1).reshape(C, NE * C)),
        cos=c(np.repeat(cos, 2, 1)), sin=c(np.stack([-sin, sin], -1).reshape(T, D3)), sel=sel.reshape(16, P, P),
        ones_row=ones_row, maskT=c(later.T), number=np.arange(NE, dtype=np.float32))
    return a


def kernel(**inputs):
    import numpy as _np
    import concourse.bacc as _bacc
    from concourse import mybir as _mybir
    from concourse.bass_utils import run_bass_kernel_spmd as _run

    nc = _bacc.Bacc("TRN2", target_bir_lowering=False, num_devices=1)
    arrays = lay_out(inputs)
    io = {}
    for name, a in arrays.items():
        io[name] = nc.dram_tensor(f"in_{name}", a.shape, _mybir.dt.from_np(a.dtype), kind="ExternalInput").ap()
    out = nc.dram_tensor("out", (TOKENS, C), _mybir.dt.float32, kind="ExternalOutput").ap()
    build(nc, io, out)
    r = _run(nc, [{f"in_{name}": a for name, a in arrays.items()}], core_ids=[0])
    return r.results[0]["out"].reshape(B, T, C)
```

```python
import numpy as np
import concourse.bass as bass
from concourse import mybir
from contextlib import ExitStack

F32 = mybir.dt.float32
F32R = mybir.dt.float32r
BF16 = mybir.dt.bfloat16
U32 = mybir.dt.uint32
ALU = mybir.AluOpType
ACT = mybir.ActivationFunctionType
X = mybir.AxisListType.X
XY = mybir.AxisListType.XY

P = 128
B, T, C = 4, 1024, 256
CT = C // P
NT = T // P
TOKENS = B * T
EPS = 1e-5
SCALE1 = C ** -0.5
QKV = 3 * C
DT = QKV // P
LORA = 64

M, J, CD = 154, B * 154, 192
H2, D2 = 8, 128
KT2, KP2 = 2, CD // 2
JT = (J + P - 1) // P
JH = J // 2
INNER = H2 * D2
SCALE2 = D2 ** -0.5
SHARPEN = 1.5
CHUNK = 512
CHUNKS = T // CHUNK
TPC = CHUNK // P

H3, D3 = 16, 16
SCALE3 = D3 ** -0.5
PAIRS = H3 // 2
ROWS3 = 32
NE = 8


class Scope:

    def __init__(self, nc, name):
        self.nc, self.name, self.stack, self.sems = nc, name, ExitStack(), []

    def __enter__(self):
        self.stack.__enter__()
        return self

    def __exit__(self, *e):
        return self.stack.__exit__(*e)

    def sb(self, name, shape, dt=F32):
        return self.stack.enter_context(self.nc.sbuf_tensor(f"{self.name}_{name}", shape, dt))

    def ps(self, name, shape, dt=F32):
        return self.stack.enter_context(self.nc.psum_tensor(f"{self.name}_{name}", shape, dt))

    def sem(self, name):
        s = self.stack.enter_context(self.nc.semaphore(f"{self.name}_{name}"))
        self.sems.append(s)
        return s

    def clear(self):
        with self.nc.Block(no_gpsimd_drain=True) as block:
            @block.sync
            def _(sp):
                for s in self.sems:
                    sp.sem_clear(s)


def mm3(nc, out, lhs, rhs, start, stop):
    (ah, al), (bh, bl) = lhs, rhs
    nc.tensor.matmul(out, al, bh, start=start, stop=False)
    nc.tensor.matmul(out, ah, bl, start=False, stop=False)
    return nc.tensor.matmul(out, ah, bh, start=False, stop=stop)


def fold_layer1(nc, io, keep):
    WmT, Mv, cb, bn_scale, bn_shift = (keep[k] for k in ("WmT", "Mv", "cb", "bn_scale", "bn_shift"))
    ident = keep["ident"]
    with Scope(nc, "fold") as s:
        x_all = s.sb("x_all", [P, B * NT, C + 1])
        WaT = s.sb("WaT", [P, CT, QKV])
        AaT = s.sb("AaT", [LORA, C])
        Ba = s.sb("Ba", [LORA, QKV])
        ApT = s.sb("ApT", [LORA, C])
        Bp = s.sb("Bp", [LORA, C])
        Wp = s.sb("Wp", [P, CT, C])
        WpT = s.sb("WpT", [P, CT, C])
        WmpT = s.sb("WmpT", [P, CT, C])
        Wcomb = s.sb("Wcomb", [P, CT, C])
        WcombS = s.sb("WcombS", [P, CT, C])
        Wv = s.sb("Wv", [P, CT, C])
        G = s.sb("G", [P, CT, C + 1])
        prod = s.sb("prod", [P, CT, QKV])
        ones = s.sb("ones", [P, P])
        gamma = s.sb("gamma", [P, DT])
        beta = s.sb("beta", [P, DT])
        mean = s.sb("mean", [P, DT])
        ex2 = s.sb("ex2", [P, DT])
        msq = s.sb("msq", [P, DT])
        var = s.sb("var", [P, DT])
        nhalf = s.sb("nhalf", [P, DT])
        rstd = s.sb("rstd", [P, DT])
        shiftB = s.sb("shiftB", [P, CT, P])
        psL = [s.ps(f"psL{i}", [P, 1024]) for i in range(CT)]
        psM = s.ps("psM", [P, 512])
        psG = [s.ps(f"psG{i}", [P, 512]) for i in range(CT)]
        psX = s.ps("psX", [P, 512])

        x_in = [s.sem(f"x_in{n}") for n in range(B)]
        w_in, c_in = s.sem("w_in"), s.sem("c_in")
        consts = s.sem("consts")
        lora_a, lora_p, wm_done, wmp_done = (s.sem(n) for n in ("lora_a", "lora_p", "wm_done", "wmp_done"))
        comb_ps, comb_done, wvt_ps, wv_done = (s.sem(n) for n in ("comb_ps", "comb_done", "wvt_ps", "wv_done"))
        gram_ps, gram_done, h_ps, prod_done = (s.sem(n) for n in ("gram_ps", "gram_done", "h_ps", "prod_done"))
        stat_ps, stat, pow_done, fold_ps = (s.sem(n) for n in ("stat_ps", "stat", "pow_done", "fold_ps"))

        with nc.Block(no_gpsimd_drain=True) as block:
            @block.sync
            def _(sp):
                sp.dma_start(AaT[:, :], io["AaT"]).then_inc(w_in, 16)
                sp.dma_start(Ba[:, :], io["Ba"]).then_inc(w_in, 16)
                sp.dma_start(WaT[:, :, :], io["WaT"].rearrange("(k p) d -> p k d", p=P)).then_inc(w_in, 16)
                for b in range(B):
                    sp.dma_start(x_all[:, b * NT:(b + 1) * NT, 0:C],
                                 io["x"][b * T:(b + 1) * T, :].rearrange("(n p) c -> p n c", p=P)).then_inc(x_in[b], 16)

            @block.scalar
            def _(act):
                act.dma_start(ApT[:, :], io["ApT"]).then_inc(c_in, 16)
                act.dma_start(Bp[:, :], io["Bp"]).then_inc(c_in, 16)
                act.dma_start(Wp[:, :, :], io["Wp"].rearrange("(k p) d -> p k d", p=P)).then_inc(c_in, 16)
                act.dma_start(WpT[:, :, :], io["WpT"].rearrange("(k p) d -> p k d", p=P)).then_inc(c_in, 16)
                act.dma_start(gamma[:, :], io["gamma"]).then_inc(c_in, 16)
                act.dma_start(beta[:, :], io["beta"]).then_inc(c_in, 16)
                act.dma_start(ident[:, :], io["ident"]).then_inc(c_in, 16)

            @block.gpsimd
            def _(pool):
                nc.gpsimd.memset(x_all[:, :, C:C + 1], 1.0).then_inc(consts, 1)
                nc.gpsimd.memset(ones[:, :], 1.0).then_inc(consts, 1)
                nc.gpsimd.memset(nhalf[:, :], -0.5).then_inc(consts, 1)
                pool.wait_ge(consts, 3)
                pool.wait_ge(stat, 4)
                nc.gpsimd.tensor_tensor(rstd[:, :], var[:, :], nhalf[:, :], ALU.pow).then_inc(pow_done, 1)

            @block.tensor
            def _(pe):
                pe.wait_ge(w_in, 48)
                for k in range(CT):
                    for r in range(3):
                        last = nc.tensor.matmul(psL[k][:, r * C:(r + 1) * C],
                                                Ba[:, r * C + k * P:r * C + (k + 1) * P], AaT[:, :],
                                                start=True, stop=True)
                    last.then_inc(lora_a, 1)
                pe.wait_ge(c_in, 112)
                for k in range(CT):
                    last = nc.tensor.matmul(psM[:, k * C:(k + 1) * C], Bp[:, k * P:(k + 1) * P], ApT[:, :],
                                            start=True, stop=True)
                last.then_inc(lora_p, 1)
                pe.wait_ge(consts, 1)
                for n in range(B * NT):
                    if n % NT == 0:
                        pe.wait_ge(x_in[n // NT], 16)
                    for k in range(CT):
                        last = nc.tensor.matmul(psG[k][:, 0:C + 1], x_all[:, n, k * P:(k + 1) * P],
                                                x_all[:, n, :], start=(n == 0), stop=(n == B * NT - 1))
                last.then_inc(gram_ps, 1)
                pe.wait_ge(wmp_done, 1)
                for d in range(CT):
                    for k in range(CT):
                        last = nc.tensor.matmul(psM[:, d * C:(d + 1) * C], Wp[:, k, d * P:(d + 1) * P],
                                                WmpT[:, k, :], start=(k == 0), stop=(k == CT - 1))
                last.then_inc(comb_ps, 1)
                pe.wait_ge(wm_done, 2)
                for d in range(CT):
                    for k in range(CT):
                        last = nc.tensor.transpose(psX[:, d * C + k * P:d * C + (k + 1) * P],
                                                   WmT[:, k, 2 * C + d * P:2 * C + (d + 1) * P], ident[:, :])
                last.then_inc(wvt_ps, 1)
                pe.wait_ge(gram_done, 1)
                for c in range(CT):
                    for lo, hi in ((0, 512), (512, QKV)):
                        for k in range(CT):
                            last = nc.tensor.matmul(psL[c][:, lo:hi], G[:, k, c * P:(c + 1) * P],
                                                    WmT[:, k, lo:hi], start=(k == 0), stop=(k == CT - 1))
                    last.then_inc(h_ps, 1)
                pe.wait_ge(prod_done, 2)
                pe.wait_ge(consts, 2)
                for d in range(DT):
                    for k in range(CT):
                        nc.tensor.matmul(psG[0][:, d:d + 1], prod[:, k, d * P:(d + 1) * P], ones[:, 0:1],
                                         start=(k == 0), stop=(k == CT - 1))
                for d in range(DT):
                    for k in range(CT):
                        last = nc.tensor.matmul(psG[0][:, DT + d:DT + d + 1], WmT[:, k, d * P:(d + 1) * P],
                                                G[:, k, C:C + 1], start=(k == 0), stop=(k == CT - 1))
                last.then_inc(stat_ps, 1)
                pe.wait_ge(stat, 8)
                for c in range(CT):
                    for k in range(CT):
                        last = nc.tensor.matmul(psM[:, c * C:(c + 1) * C], Wv[:, k, c * P:(c + 1) * P],
                                                WcombS[:, k, :], start=(k == 0), stop=(k == CT - 1))
                for k in range(CT):
                    last = nc.tensor.matmul(psX[:, 0:C], shiftB[:, k, :], Wcomb[:, k, :],
                                            start=(k == 0), stop=(k == CT - 1))
                last.then_inc(fold_ps, 1)

            @block.vector
            def _(dve):
                dve.wait_ge(w_in, 48)
                for k in range(CT):
                    dve.wait_ge(lora_a, k + 1)
                    nc.vector.tensor_tensor(
                        WmT[:, k, :].rearrange("p (i r) -> p i r", r=3),
                        WaT[:, k, :].rearrange("p (i r) -> p i r", r=3),
                        psL[k][:, 0:QKV].rearrange("p (r i) -> p i r", r=3), ALU.add).then_inc(wm_done, 1)
                dve.wait_ge(c_in, 112)
                dve.wait_ge(lora_p, 1)
                nc.vector.tensor_tensor(WmpT[:, :, :], WpT[:, :, :],
                                        psM[:, :].rearrange("p (k e) -> p k e", k=CT), ALU.add).then_inc(wmp_done, 1)
                dve.wait_ge(comb_ps, 1)
                nc.vector.tensor_copy(Wcomb[:, :, :], psM[:, :].rearrange("p (k e) -> p k e", k=CT)).then_inc(comb_done, 1)
                dve.wait_ge(wvt_ps, 1)
                nc.vector.tensor_copy(Wv[:, :, :], psX[:, :].rearrange("p (k e) -> p k e", k=CT)).then_inc(wv_done, 1)
                dve.wait_ge(gram_ps, 1)
                nc.vector.tensor_copy(G[:, 0, :], psG[0][:, 0:C + 1])
                nc.vector.tensor_copy(G[:, 1, :], psG[1][:, 0:C + 1]).then_inc(gram_done, 1)
                for c in range(CT):
                    dve.wait_ge(h_ps, c + 1)
                    nc.vector.tensor_tensor(prod[:, c, :], WmT[:, c, :], psL[c][:, 0:QKV], ALU.mult).then_inc(prod_done, 1)
                dve.wait_ge(stat_ps, 1)
                nc.vector.tensor_scalar(ex2[:, :], psG[0][:, 0:DT], 1.0 / TOKENS, EPS, ALU.mult, ALU.add).then_inc(stat, 1)
                nc.vector.tensor_scalar(mean[:, :], psG[0][:, DT:2 * DT], 1.0 / TOKENS, None, ALU.mult).then_inc(stat, 1)
                dve.wait_ge(stat, 2)
                nc.vector.tensor_tensor(msq[:, :], mean[:, :], mean[:, :], ALU.mult).then_inc(stat, 1)
                dve.wait_ge(stat, 3)
                nc.vector.tensor_tensor(var[:, :], ex2[:, :], msq[:, :], ALU.subtract).then_inc(stat, 1)
                dve.wait_ge(pow_done, 1)
                nc.vector.tensor_tensor(bn_scale[:, :], gamma[:, :], rstd[:, :], ALU.mult).then_inc(stat, 1)
                dve.wait_ge(stat, 5)
                nc.vector.tensor_tensor(msq[:, :], mean[:, :], bn_scale[:, :], ALU.mult).then_inc(stat, 1)
                dve.wait_ge(stat, 6)
                nc.vector.tensor_tensor(bn_shift[:, :], beta[:, :], msq[:, :], ALU.subtract).then_inc(stat, 1)
                dve.wait_ge(stat, 7)
                dve.wait_ge(comb_done, 1)
                for k in range(CT):
                    nc.vector.tensor_scalar(WcombS[:, k, :], Wcomb[:, k, :], bn_scale[:, 4 + k:5 + k], None, ALU.mult)
                    last = nc.vector.tensor_scalar(shiftB[:, k, :], ones[:, :], bn_shift[:, 4 + k:5 + k], None, ALU.mult)
                last.then_inc(stat, 1)
                dve.wait_ge(stat, 8)
                nc.vector.tensor_scalar(bn_scale[:, 0:CT], bn_scale[:, 0:CT], SCALE1, None, ALU.mult)
                nc.vector.tensor_scalar(bn_shift[:, 0:CT], bn_shift[:, 0:CT], SCALE1, None, ALU.mult)
                dve.wait_ge(fold_ps, 1)
                nc.vector.tensor_copy(Mv[:, :, :], psM[:, :].rearrange("p (k e) -> p k e", k=CT))
                nc.vector.tensor_copy(cb[:, :], psX[:, 0:C])
        s.clear()


def layer1(nc, io, x_next):
    with Scope(nc, "keep1") as keep:
        k = dict(WmT=keep.sb("WmT", [P, CT, QKV]), Mv=keep.sb("Mv", [P, CT, C]), cb=keep.sb("cb", [P, C]),
                 bn_scale=keep.sb("bn_scale", [P, DT]), bn_shift=keep.sb("bn_shift", [P, DT]),
                 ident=keep.sb("ident", [P, P]))
        fold_layer1(nc, io, k)
        WmT, Mv, cb, bn_scale, bn_shift, ident = (k[n] for n in ("WmT", "Mv", "cb", "bn_scale", "bn_shift", "ident"))
        with Scope(nc, "attn1") as s:
            xn = s.sb("xn", [P, NT, C])
            xT = s.sb("xT", [P, CT, T])
            qT = s.sb("qT", [P, CT, T])
            kT = s.sb("kT", [P, CT, T])
            V = s.sb("V", [P, NT, C])
            prob = s.sb("prob", [P, 2, T])
            probT = s.sb("probT", [P, 2, T])
            y = s.sb("y", [P, NT, C])
            stats = s.sb("stats", [P, NT, 6])
            mv = s.sb("mv", [P, NT, 2])
            veps = s.sb("veps", [P, NT])
            rstd = s.sb("rstd", [P, NT])
            nmax = s.sb("nmax", [P, NT])
            rsum = s.sb("rsum", [P, NT])
            rinv = s.sb("rinv", [P, NT])
            nhalf = s.sb("nhalf", [P, 1])
            identb = s.sb("identb", [P, P], BF16)
            maskf = s.sb("maskf", [P, P])
            maskb = s.sb("maskb", [P, P], BF16)
            psS = [s.ps(f"psS{i}", [P, 1024]) for i in range(2)]
            psT = [s.ps(f"psT{i}", [P, 512]) for i in range(2)]
            psO = [s.ps(f"psO{i}", [P, 512]) for i in range(2)]

            x_in, consts, const_in = s.sem("x_in"), s.sem("consts"), s.sem("const_in")
            qk_ps, qk_done, v_ps, v_done = s.sem("qk_ps"), s.sem("qk_done"), s.sem("v_ps"), s.sem("v_done")
            s_ps, max_done, exp_done = s.sem("s_ps"), s.sem("max_done"), s.sem("exp_done")
            t_ps, t_done, o_ps, y_done = s.sem("t_ps"), s.sem("t_done"), s.sem("o_ps"), s.sem("y_done")
            rinv_done, st_done, veps_done, rstd_done, ln_done, out_st = (
                s.sem(n) for n in ("rinv_done", "st_done", "veps_done", "rstd_done", "ln_done", "out_st"))

            groups = []
            for t in range(NT):
                for g in range(0, t + 1, 4):
                    groups.append((t, g, min(4, t + 1 - g)))
            first_group = {t: min(i for i, g in enumerate(groups) if g[0] == t) for t in range(NT)}
            last_group = {t: max(i for i, g in enumerate(groups) if g[0] == t) for t in range(NT)}

            with nc.Block(no_gpsimd_drain=True) as block:
                @block.sync
                def _(sp):
                    sp.dma_start(maskf[:, :], io["mask"]).then_inc(const_in, 16)

                @block.scalar
                def _(act):
                    nc.scalar.activation(identb[:, :], ident[:, :], ACT.Copy)
                    act.wait_ge(const_in, 16)
                    nc.scalar.activation(maskb[:, :], maskf[:, :], ACT.Copy)

                @block.gpsimd
                def _(pool):
                    nc.gpsimd.memset(nhalf[:, :], -0.5).then_inc(consts, 1)
                    pool.wait_ge(consts, 1)
            s.clear()

            with nc.Fori(0, B) as b:
                with nc.Block(no_gpsimd_drain=True) as block:
                    @block.sync
                    def _(sp):
                        sp.dma_start(xT[:, :, :], io["xT"][:, bass.ts(b, T)].rearrange("(k p) t -> p k t", p=P)).then_inc(x_in, 16)
                        sp.dma_start(xn[:, :, :], io["x"][bass.ts(b, T), :].rearrange("(n p) c -> p n c", p=P)).then_inc(x_in, 16)
                        sp.wait_ge(ln_done, NT)
                        sp.dma_start(x_next[bass.ts(b, T), :].rearrange("(n p) c -> p n c", p=P), y[:, :, :]).then_inc(out_st, 16)
                        sp.wait_ge(out_st, 16)

                    @block.tensor
                    def _(pe):
                        pe.wait_ge(x_in, 32)
                        n = 0
                        for d in range(2 * CT):
                            for c in range(CHUNKS):
                                bank = psS[n // 2 % 2][:, (n % 2) * 512:(n % 2) * 512 + 512]
                                if n >= 4:
                                    pe.wait_ge(qk_done, n - 3)
                                for k in range(CT):
                                    last = nc.tensor.matmul(bank, WmT[:, k, d * P:(d + 1) * P],
                                                            xT[:, k, c * CHUNK:(c + 1) * CHUNK],
                                                            start=(k == 0), stop=(k == CT - 1))
                                last.then_inc(qk_ps, 1)
                                n += 1
                        for t in range(NT):
                            if t >= 2:
                                pe.wait_ge(v_done, t - 1)
                            for k in range(CT):
                                last = nc.tensor.matmul(psO[t % 2][:, 0:C], xT[:, k, t * P:(t + 1) * P], Mv[:, k, :],
                                                        start=(k == 0), stop=(k == CT - 1))
                            last.then_inc(v_ps, 1)
                        pe.wait_ge(qk_done, 8)

                        def scores(t):
                            if t >= 2:
                                pe.wait_ge(exp_done, t - 1)
                            for c in range(0, (t + 1) * P, 512):
                                w = min(512, (t + 1) * P - c)
                                diag = c + w == (t + 1) * P
                                for k in range(CT):
                                    last = nc.tensor.matmul(psS[t % 2][:, c:c + w], qT[:, k, t * P:(t + 1) * P],
                                                            kT[:, k, c:c + w], start=(k == 0),
                                                            stop=(k == CT - 1 and not diag))
                                if diag:
                                    last = nc.tensor.matmul(psS[t % 2][:, t * P:(t + 1) * P], identb[:, :], maskb[:, :],
                                                            start=False, stop=True)
                            last.then_inc(s_ps, 1)

                        def transposed(t):
                            pe.wait_ge(exp_done, t + 1)
                            for i in range(first_group[t], last_group[t] + 1):
                                _, g, n = groups[i]
                                if i >= 2:
                                    pe.wait_ge(t_done, i - 1)
                                for j in range(n):
                                    last = nc.tensor.transpose(psT[i % 2][:, j * P:(j + 1) * P],
                                                               prob[:, t % 2, (g + j) * P:(g + j + 1) * P], ident[:, :])
                                last.then_inc(t_ps, 1)

                        def weighted(t):
                            pe.wait_ge(t_done, last_group[t] + 1)
                            if t == 0:
                                pe.wait_ge(v_done, NT)
                            if t >= 2:
                                pe.wait_ge(y_done, t - 1)
                            for j in range(t + 1):
                                last = nc.tensor.matmul(psO[t % 2][:, 0:C], probT[:, t % 2, j * P:(j + 1) * P], V[:, j, :],
                                                        start=(j == 0), stop=(j == t))
                            last.then_inc(o_ps, 1)

                        scores(0)
                        for t in range(NT):
                            if t + 1 < NT:
                                scores(t + 1)
                            transposed(t)
                            weighted(t)

                    @block.scalar
                    def _(act):
                        n = 0
                        for d in range(2 * CT):
                            dst = qT if d < CT else kT
                            for c in range(CHUNKS):
                                act.wait_ge(qk_ps, n + 1)
                                bank = psS[n // 2 % 2][:, (n % 2) * 512:(n % 2) * 512 + 512]
                                nc.scalar.activation(dst[:, d % CT, c * CHUNK:(c + 1) * CHUNK], bank, ACT.Identity,
                                                     bias=bn_shift[:, d:d + 1], scale=bn_scale[:, d:d + 1]).then_inc(qk_done, 1)
                                n += 1
                        for t in range(NT):
                            act.wait_ge(max_done, t + 1)
                            if t >= 2:
                                act.wait_ge(t_ps, last_group[t - 2] + 1)
                            nc.scalar.activation(prob[:, t % 2, 0:(t + 1) * P], psS[t % 2][:, 0:(t + 1) * P], ACT.Exp,
                                                 bias=nmax[:, t:t + 1], accum_out=rsum[:, t:t + 1]).then_inc(exp_done, 1)

                    @block.gpsimd
                    def _(pool):
                        for t in range(NT):
                            pool.wait_ge(veps_done, t + 1)
                            nc.gpsimd.tensor_tensor(rstd[:, t:t + 1], veps[:, t:t + 1], nhalf[:, :], ALU.pow).then_inc(rstd_done, 1)

                    @block.vector
                    def _(dve):
                        for t in range(NT):
                            dve.wait_ge(v_ps, t + 1)
                            nc.vector.tensor_tensor(V[:, t, :], psO[t % 2][:, 0:C], cb[:, :], ALU.add).then_inc(v_done, 1)
                        dve.wait_ge(x_in, 32)

                        def row_max(t):
                            dve.wait_ge(s_ps, t + 1)
                            nc.vector.tensor_reduce(nmax[:, t:t + 1], psS[t % 2][:, 0:(t + 1) * P], X, ALU.max,
                                                    negate=True).then_inc(max_done, 1)

                        def normalise(t):
                            dve.wait_ge(rstd_done, t + 1)
                            nc.vector.tensor_scalar(y[:, t, :], y[:, t, :], mv[:, t, 0:1], rstd[:, t:t + 1],
                                                    ALU.subtract, ALU.mult).then_inc(ln_done, 1)

                        row_max(0)
                        for t in range(NT):
                            if t + 1 < NT:
                                row_max(t + 1)
                            for i in range(first_group[t], last_group[t] + 1):
                                _, g, n = groups[i]
                                dve.wait_ge(t_ps, i + 1)
                                if t >= 2:
                                    dve.wait_ge(o_ps, t - 1)
                                nc.vector.tensor_copy(probT[:, t % 2, g * P:(g + n) * P], psT[i % 2][:, 0:n * P]).then_inc(t_done, 1)
                            if t >= 1:
                                normalise(t - 1)
                            dve.wait_ge(exp_done, t + 1)
                            nc.vector.reciprocal(rinv[:, t:t + 1], rsum[:, t:t + 1]).then_inc(rinv_done, 1)
                            dve.wait_ge(rinv_done, t + 1)
                            dve.wait_ge(o_ps, t + 1)
                            nc.vector.scalar_tensor_tensor(out=y[:, t, :], in0=psO[t % 2][:, 0:C], scalar=rinv[:, t:t + 1],
                                                           in1=xn[:, t, :], op0=ALU.mult, op1=ALU.add).then_inc(y_done, 1)
                            dve.wait_ge(y_done, t + 1)
                            nc.vector.bn_stats(stats[:, t, :], y[:, t, :]).then_inc(st_done, 1)
                            dve.wait_ge(st_done, 2 * t + 1)
                            nc.vector.bn_aggr(mv[:, t, :], stats[:, t, :]).then_inc(st_done, 1)
                            dve.wait_ge(st_done, 2 * t + 2)
                            nc.vector.tensor_scalar(veps[:, t:t + 1], mv[:, t, 1:2], EPS, None, ALU.add).then_inc(veps_done, 1)
                        normalise(NT - 1)
                s.clear()


def keys_and_values2(nc, io, w):
    Wq, K, V, Wout = w["Wq"], w["K"], w["V"], w["Wout"]
    with Scope(nc, "keys2") as s:
        ctxT = s.sb("ctxT", [KP2, KT2, J])
        Wk = s.sb("Wk", [KP2, KT2, INNER])
        Wv = s.sb("Wv", [KP2, KT2, INNER])
        Wqf = s.sb("Wqf", [P, CT, INNER])
        kf = s.sb("kf", [P, 2, J])
        ksum = s.sb("ksum", [P, H2])
        kb = s.sb("kb", [P, H2])
        psK = [s.ps(f"psK{i}", [P, 2, 512]) for i in range(2)]
        psV = [s.ps(f"psV{i}", [P, 512]) for i in range(2)]
        c_in, q_in, w_in, consts = s.sem("c_in"), s.sem("q_in"), s.sem("w_in"), s.sem("consts")
        k_ps, k_sum, kb_done, k_done = s.sem("k_ps"), s.sem("k_sum"), s.sem("kb_done"), s.sem("k_done")
        q_hi, v_ps, v_hi, v_lo = s.sem("q_hi"), s.sem("v_ps"), s.sem("v_hi"), s.sem("v_lo")
        pieces = [(j, min(P, J - j * P), n) for j in range(JT) for n in range(INNER // 512)]

        with nc.Block(no_gpsimd_drain=True) as block:
            @block.sync
            def _(sp):
                sp.dma_start(ctxT[:, :, :], io["ctxT"].rearrange("(k p) j -> p k j", p=KP2)).then_inc(c_in, 16)
                sp.dma_start(Wk[:, :, :], io["Wk2"].rearrange("(k p) d -> p k d", p=KP2)).then_inc(c_in, 16)
                sp.dma_start(Wqf[:, :, :], io["Wq2"].rearrange("(k p) d -> p k d", p=P)).then_inc(q_in, 16)
                sp.dma_start(Wv[:, :, :], io["Wv2"].rearrange("(k p) d -> p k d", p=KP2)).then_inc(c_in, 16)
                sp.dma_start(Wout[:, :, :], io["Wout"].rearrange("(h p) e -> p h e", p=P)).then_inc(w_in, 16)
                sp.dma_start(w["bout"][:, :], io["bout"].partition_broadcast(P)).then_inc(w_in, 16)
                sp.dma_start(w["ident"][:, :], io["ident"]).then_inc(w_in, 16)
                sp.wait_ge(w_in, 48)

            @block.gpsimd
            def _(pool):
                nc.gpsimd.memset(w["nhalf"][:, :], -0.5).then_inc(consts, 1)
                pool.wait_ge(consts, 1)

            @block.tensor
            def _(pe):
                pe.wait_ge(c_in, 48)
                for h in range(H2):
                    if h >= 2:
                        pe.wait_ge(k_sum, h - 1)
                    for a in range(2):
                        for k in range(KT2):
                            last = nc.tensor.matmul(psK[h % 2][:, a, 0:JH], Wk[:, k, h * D2:(h + 1) * D2],
                                                    ctxT[:, k, a * JH:(a + 1) * JH], start=(k == 0), stop=(k == KT2 - 1))
                    last.then_inc(k_ps, 1)
                for i, (j, rows, n) in enumerate(pieces):
                    if i >= 2:
                        pe.wait_ge(v_lo, i - 1)
                    for k in range(KT2):
                        last = nc.tensor.matmul(psV[i % 2][0:rows, :], ctxT[:, k, j * P:j * P + rows],
                                                Wv[:, k, n * 512:(n + 1) * 512], start=(k == 0), stop=(k == KT2 - 1))
                    last.then_inc(v_ps, 1)

            @block.scalar
            def _(act):
                for h in range(H2):
                    act.wait_ge(k_ps, h + 1)
                    if h >= 2:
                        act.wait_ge(k_done, 3 * (h - 1))
                    nc.scalar.activation(kf[:, h % 2, :].rearrange("p (a w) -> p a w", a=2), psK[h % 2][:, :, 0:JH],
                                         ACT.Copy, accum_out=ksum[:, h:h + 1]).then_inc(k_sum, 1)
                act.wait_ge(q_in, 16)
                nc.scalar.activation(Wq[0][:, :, :], Wqf[:, :, :], ACT.Copy).then_inc(q_hi, 1)
                for i, (j, rows, n) in enumerate(pieces):
                    act.wait_ge(v_ps, i + 1)
                    nc.scalar.activation(V[0][0:rows, j, n * 512:(n + 1) * 512], psV[i % 2][0:rows, :], ACT.Copy).then_inc(v_hi, 1)

            @block.vector
            def _(dve):
                for h in range(H2):
                    dve.wait_ge(k_sum, h + 1)
                    nc.vector.tensor_scalar(kb[:, h:h + 1], ksum[:, h:h + 1], (1.0 - SHARPEN) * SCALE2 / J, None,
                                            ALU.mult).then_inc(kb_done, 1)
                    dve.wait_ge(kb_done, h + 1)
                    nc.vector.tensor_scalar(kf[:, h % 2, :], kf[:, h % 2, :], SHARPEN * SCALE2, kb[:, h:h + 1],
                                            ALU.mult, ALU.add).then_inc(k_done, 1)
                    dve.wait_ge(k_done, 3 * h + 1)
                    nc.vector.tensor_copy(K[0][:, h, :], kf[:, h % 2, :]).then_inc(k_done, 1)
                    dve.wait_ge(k_done, 3 * h + 2)
                    nc.vector.tensor_tensor(K[1][:, h, :], kf[:, h % 2, :], K[0][:, h, :].bitcast(F32),
                                            ALU.subtract).then_inc(k_done, 1)
                dve.wait_ge(q_hi, 1)
                nc.vector.tensor_tensor(Wq[1][:, :, :], Wqf[:, :, :], Wq[0][:, :, :].bitcast(F32), ALU.subtract)
                for i, (j, rows, n) in enumerate(pieces):
                    dve.wait_ge(v_hi, i + 1)
                    nc.vector.tensor_tensor(V[1][0:rows, j, n * 512:(n + 1) * 512], psV[i % 2][0:rows, :],
                                            V[0][0:rows, j, n * 512:(n + 1) * 512].bitcast(F32), ALU.subtract).then_inc(v_lo, 1)
        s.clear()


RING, PT_RING = 3, 4
UNITS = CHUNKS * H2


def tensor_order2():
    order = [("x", c, k) for c in range(CHUNKS) for k in range(CT)]
    for s in range(-2, UNITS + 2):
        step = [("q", s + 2, 0), ("pv", s - 1, 1), ("s", s + 1, 2), ("s", s + 1, 3), ("p", s, 0), ("pv", s - 1, 2),
                ("p", s, 1), ("pv", s - 1, 3), ("p", s, 2), ("pv", s - 1, 4), ("p", s, 3), ("s", s + 2, 0), ("p", s, 4),
                ("s", s + 2, 1), ("pv", s, 0)]
        for what, u, part in step:
            if 0 <= u < UNITS:
                order.append((what, u, part))
                if what == "s" and u >= H2 + 3 and u % H2 == 3:
                    order.append(("y", u // H2 - 1, part))
    return order + [("y", CHUNKS - 1, t) for t in range(TPC)]


def layer2(nc, io, x_prev, x_next):
    with Scope(nc, "keep2") as keep:
        w = dict(Wq=[keep.sb(f"Wq{i}", [P, CT, INNER], F32R) for i in range(2)],
                 K=[keep.sb(f"K{i}", [P, H2, J], F32R) for i in range(2)],
                 V=[keep.sb(f"V{i}", [P, JT, INNER], F32R) for i in range(2)],
                 Wout=keep.sb("Wout", [P, H2, C]), bout=keep.sb("bout", [P, C]), ident=keep.sb("ident", [P, P]),
                 nhalf=keep.sb("nhalf", [P, 1]))
        keys_and_values2(nc, io, w)
        Wq, K, V, Wout, ident = w["Wq"], w["K"], w["V"], w["Wout"], w["ident"]
        with Scope(nc, "attn2") as s:
            xn = s.sb("xn", [P, NT, C])
            xT = [s.sb(f"xT{i}", [P, CT, T], F32R) for i in range(2)]
            q = [s.sb(f"q{i}", [P, 2, CHUNK], F32R) for i in range(2)]
            prob = s.sb("prob", [P, 2 * TPC, J])
            pT = [s.sb(f"pT{i}", [P, PT_RING, CHUNK], F32R) for i in range(2)]
            outT = s.sb("outT", [P, CHUNKS, H2, CHUNK])
            y = xn
            NS = CHUNKS * H2 * TPC
            nmax = s.sb("nmax", [P, NS])
            rsum = s.sb("rsum", [P, NS])
            rinv = s.sb("rinv", [P, NS])
            stats = s.sb("stats", [P, NT, 6])
            mv = s.sb("mv", [P, NT, 2])
            veps = s.sb("veps", [P, NT])
            rstd = s.sb("rstd", [P, NT])
            psS = [s.ps(f"psS{i}", [P, 2, 512]) for i in range(2)]
            ring = [s.ps(f"ring{i}", [P, 512]) for i in range(RING)]
            psO = s.ps("psO", [P, 512])

            x_in, xb_done = s.sem("x_in"), s.sem("xb_done")
            q_ps, q_hi, q_lo = s.sem("q_ps"), s.sem("q_hi"), s.sem("q_lo")
            s_ps, max_done, exp_done, rinv_done, norm_done = (
                s.sem(n) for n in ("s_ps", "max_done", "exp_done", "rinv_done", "norm_done"))
            x_ps, x_hi, x_lo = s.sem("x_ps"), s.sem("x_hi"), s.sem("x_lo")
            p_ps, p_hi, p_lo = s.sem("p_ps"), s.sem("p_hi"), s.sem("p_lo")
            y_ps = s.sem("y_ps")
            pv_ps, o_done = s.sem("pv_ps"), s.sem("o_done")
            y_done, st_done, veps_done, rstd_done, ln_done, out_st = (
                s.sem(n) for n in ("y_done", "st_done", "veps_done", "rstd_done", "ln_done", "out_st"))

            order = tensor_order2()
            slots = [o for o in order if o[0] in "xqpy"]
            at = {o: i for i, o in enumerate(slots)}

            def score_tile(u, t):
                return TPC * u + t

            def block(u, j):
                return JT * u + j

            with nc.Fori(0, B) as b:
                with nc.Block(no_gpsimd_drain=True) as blk:
                    @blk.sync
                    def _(sp):
                        sp.dma_start(xn[:, :, :], x_prev[bass.ts(b, T), :].rearrange("(n p) c -> p n c", p=P)).then_inc(x_in, 16)
                        sp.wait_ge(ln_done, NT)
                        sp.dma_start(x_next[bass.ts(b, T), :].rearrange("(n p) c -> p n c", p=P), y[:, :, :]).then_inc(out_st, 16)
                        sp.wait_ge(out_st, 16)

                    @blk.gpsimd
                    def _(pool):
                        pool.wait_ge(x_ps, CHUNKS * CT)
                        for t in range(NT):
                            nc.gpsimd.tensor_tensor(xn[:, t, :], xn[:, t, :], w["bout"][:, :], ALU.add).then_inc(xb_done, 1)
                        for t in range(NT):
                            pool.wait_ge(veps_done, t + 1)
                            nc.gpsimd.tensor_tensor(rstd[:, t:t + 1], veps[:, t:t + 1], w["nhalf"][:, :], ALU.pow).then_inc(rstd_done, 1)

                    @blk.tensor
                    def _(pe):
                        def take(what, u, part):
                            i = at[what, u, part]
                            if i >= RING:
                                was, v, piece = slots[i - RING]
                                if was == "x":
                                    pe.wait_ge(x_lo, CT * v + piece + 1)
                                elif was == "q":
                                    pe.wait_ge(q_lo, v + 1)
                                elif was == "p":
                                    pe.wait_ge(p_lo, block(v, piece) + 1)
                                else:
                                    pe.wait_ge(y_done, TPC * v + piece + 1)
                            return ring[i % RING]

                        def transpose_x(c, k):
                            bank = take("x", c, k)
                            for t in range(TPC):
                                last = nc.tensor.transpose(bank[:, t * P:(t + 1) * P], xn[:, c * TPC + t, k * P:(k + 1) * P], ident[:, :])
                            last.then_inc(x_ps, 1)

                        def project_q(u, _):
                            c, h = divmod(u, H2)
                            bank = take("q", u, 0)
                            pe.wait_ge(x_lo, CT * (c + 1))
                            for k in range(CT):
                                last = mm3(nc, bank[:, :], [a[:, k, h * D2:(h + 1) * D2] for a in Wq],
                                           [a[:, k, c * CHUNK:(c + 1) * CHUNK] for a in xT], k == 0, k == CT - 1)
                            last.then_inc(q_ps, 1)

                        def scores(u, t):
                            n = score_tile(u, t)
                            pe.wait_ge(q_lo, u + 1)
                            if n >= 2:
                                pe.wait_ge(exp_done, n - 1)
                            for a in range(2):
                                last = mm3(nc, psS[n % 2][:, a, 0:JH], [z[:, u % 2, t * P:(t + 1) * P] for z in q],
                                           [z[:, u % H2, a * JH:(a + 1) * JH] for z in K], True, True)
                            last.then_inc(s_ps, 1)

                        def transpose_p(u, j):
                            rows = min(P, J - j * P)
                            bank = take("p", u, j)
                            pe.wait_ge(norm_done, score_tile(u + 1, 0))
                            for t in range(TPC):
                                last = nc.tensor.transpose(bank[0:rows, t * P:(t + 1) * P],
                                                           prob[:, u % 2 * TPC + t, j * P:j * P + rows], ident[:, :])
                            last.then_inc(p_ps, 1)

                        def weighted(u, j):
                            rows, h = min(P, J - j * P), u % H2
                            pe.wait_ge(p_lo, block(u, j) + 1)
                            if j == 0 and u >= 1:
                                pe.wait_ge(o_done, u)
                            mm3(nc, psO[:, :], [z[0:rows, j, h * D2:(h + 1) * D2] for z in V],
                                [z[0:rows, block(u, j) % PT_RING, :] for z in pT], j == 0, j == JT - 1).then_inc(pv_ps, 1)

                        def project_out(c, t):
                            bank = take("y", c, t)
                            pe.wait_ge(o_done, (c + 1) * H2)
                            for h in range(H2):
                                last = nc.tensor.matmul(bank[:, 0:C], outT[:, c, h, t * P:(t + 1) * P], Wout[:, h, :],
                                                        start=(h == 0), stop=(h == H2 - 1))
                            last.then_inc(y_ps, 1)

                        pe.wait_ge(x_in, 16)
                        for what, u, part in order:
                            {"x": transpose_x, "q": project_q, "s": scores, "p": transpose_p, "pv": weighted,
                             "y": project_out}[what](u, part)

                    @blk.scalar
                    def _(act):
                        def exps(u, t):
                            if not 0 <= u < UNITS:
                                return
                            n = score_tile(u, t)
                            act.wait_ge(max_done, n + 1)
                            if u >= 2:
                                act.wait_ge(p_ps, block(u - 1, 0))
                            nc.scalar.activation(prob[:, u % 2 * TPC + t, :].rearrange("p (a w) -> p a w", a=2),
                                                 psS[n % 2][:, :, 0:JH], ACT.Exp, bias=nmax[:, n:n + 1],
                                                 accum_out=rsum[:, n:n + 1]).then_inc(exp_done, 1)

                        def normalise_p(u, t):
                            if not 0 <= u < UNITS:
                                return
                            n = score_tile(u, t)
                            act.wait_ge(rinv_done, n + 1)
                            nc.scalar.activation(prob[:, u % 2 * TPC + t, :], prob[:, u % 2 * TPC + t, :], ACT.Copy,
                                                 scale=rinv[:, n:n + 1]).then_inc(norm_done, 1)

                        def p_high(u, j):
                            if not 0 <= u < UNITS:
                                return
                            rows, g = min(P, J - j * P), block(u, j)
                            act.wait_ge(p_ps, g + 1)
                            if g >= PT_RING:
                                act.wait_ge(pv_ps, g - PT_RING + 1)
                            nc.scalar.activation(pT[0][0:rows, g % PT_RING, :], ring[at["p", u, j] % RING][0:rows, :],
                                                 ACT.Copy).then_inc(p_hi, 1)

                        def q_high(u):
                            if not 0 <= u < UNITS:
                                return
                            act.wait_ge(q_ps, u + 1)
                            if u >= 2:
                                act.wait_ge(s_ps, score_tile(u - 1, 0))
                            nc.scalar.activation(q[0][:, u % 2, :], ring[at["q", u, 0] % RING][:, :], ACT.Copy).then_inc(q_hi, 1)

                        for c in range(CHUNKS):
                            for k in range(CT):
                                act.wait_ge(x_ps, CT * c + k + 1)
                                nc.scalar.activation(xT[0][:, k, c * CHUNK:(c + 1) * CHUNK], ring[at["x", c, k] % RING][:, :],
                                                     ACT.Copy).then_inc(x_hi, 1)
                        for s_ in range(-1, UNITS + 2):
                            exps(s_ - 1, 2)
                            p_high(s_ - 2, 1)
                            exps(s_ - 1, 3)
                            p_high(s_ - 2, 2)
                            normalise_p(s_ - 1, 1)
                            p_high(s_ - 2, 3)
                            normalise_p(s_ - 1, 2)
                            normalise_p(s_ - 1, 3)
                            exps(s_, 0)
                            exps(s_, 1)
                            p_high(s_ - 2, 4)
                            q_high(s_ + 1)
                            normalise_p(s_, 0)
                            p_high(s_ - 1, 0)

                    @blk.vector
                    def _(dve):
                        def row_max(u, t):
                            if not 0 <= u < UNITS:
                                return
                            n = score_tile(u, t)
                            dve.wait_ge(s_ps, n + 1)
                            nc.vector.tensor_reduce(nmax[:, n:n + 1], psS[n % 2][:, :, 0:JH], XY, ALU.max,
                                                    negate=True).then_inc(max_done, 1)

                        def chunk_out(u, *tiles):
                            if u >= H2 + 3 and u < UNITS and u % H2 == 3:
                                for t in tiles:
                                    residual(u // H2 - 1, t)
                                if tiles[-1] == TPC - 1:
                                    layer_norm(u // H2 - 1)

                        def invert_sum(u, t):
                            if not 0 <= u < UNITS:
                                return
                            n = score_tile(u, t)
                            dve.wait_ge(exp_done, n + 1)
                            nc.vector.reciprocal(rinv[:, n:n + 1], rsum[:, n:n + 1]).then_inc(rinv_done, 1)

                        def p_low(u, j):
                            if not 0 <= u < UNITS:
                                return
                            rows, g = min(P, J - j * P), block(u, j)
                            dve.wait_ge(p_hi, g + 1)
                            nc.vector.tensor_tensor(pT[1][0:rows, g % PT_RING, :], ring[at["p", u, j] % RING][0:rows, :],
                                                    pT[0][0:rows, g % PT_RING, :].bitcast(F32), ALU.subtract).then_inc(p_lo, 1)

                        def q_low(u):
                            if not 0 <= u < UNITS:
                                return
                            dve.wait_ge(q_hi, u + 1)
                            nc.vector.tensor_tensor(q[1][:, u % 2, :], ring[at["q", u, 0] % RING][:, :],
                                                    q[0][:, u % 2, :].bitcast(F32), ALU.subtract).then_inc(q_lo, 1)

                        def head_out(u):
                            if not 0 <= u < UNITS:
                                return
                            dve.wait_ge(pv_ps, block(u + 1, 0))
                            nc.vector.tensor_copy(outT[:, u // H2, u % H2, :], psO[:, :]).then_inc(o_done, 1)

                        def residual(c, t):
                            n = c * TPC + t
                            dve.wait_ge(y_ps, n + 1)
                            dve.wait_ge(xb_done, NT)
                            nc.vector.tensor_tensor(y[:, n, :], ring[at["y", c, t] % RING][:, 0:C], xn[:, n, :],
                                                    ALU.add).then_inc(y_done, 1)
                            dve.wait_ge(y_done, n + 1)
                            nc.vector.bn_stats(stats[:, n, :], y[:, n, :]).then_inc(st_done, 1)
                            dve.wait_ge(st_done, 2 * n + 1)
                            nc.vector.bn_aggr(mv[:, n, :], stats[:, n, :]).then_inc(st_done, 1)
                            dve.wait_ge(st_done, 2 * n + 2)
                            nc.vector.tensor_scalar(veps[:, n:n + 1], mv[:, n, 1:2], EPS, None, ALU.add).then_inc(veps_done, 1)

                        def layer_norm(c):
                            for n in range(c * TPC, (c + 1) * TPC):
                                dve.wait_ge(rstd_done, n + 1)
                                nc.vector.tensor_scalar(y[:, n, :], y[:, n, :], mv[:, n, 0:1], rstd[:, n:n + 1],
                                                        ALU.subtract, ALU.mult).then_inc(ln_done, 1)

                        for c in range(CHUNKS):
                            for k in range(CT):
                                dve.wait_ge(x_hi, CT * c + k + 1)
                                nc.vector.tensor_tensor(xT[1][:, k, c * CHUNK:(c + 1) * CHUNK], ring[at["x", c, k] % RING][:, :],
                                                        xT[0][:, k, c * CHUNK:(c + 1) * CHUNK].bitcast(F32),
                                                        ALU.subtract).then_inc(x_lo, 1)
                        for s_ in range(-2, UNITS + 2):
                            invert_sum(s_, 1)
                            p_low(s_ - 1, 1)
                            invert_sum(s_, 2)
                            invert_sum(s_, 3)
                            head_out(s_ - 2)
                            p_low(s_ - 1, 2)
                            row_max(s_ + 1, 0)
                            row_max(s_ + 1, 1)
                            invert_sum(s_ + 1, 0)
                            p_low(s_ - 1, 3)
                            p_low(s_ - 1, 4)
                            chunk_out(s_ + 1, 0, 1)
                            row_max(s_ + 1, 2)
                            chunk_out(s_ + 1, 2)
                            q_low(s_ + 2)
                            row_max(s_ + 1, 3)
                            chunk_out(s_ + 1, 3)
                            p_low(s_, 0)
                        for t in range(TPC):
                            residual(CHUNKS - 1, t)
                        layer_norm(CHUNKS - 1)
                s.clear()


def split(nc, block, name, s, pairs, ready, ready_at):
    hi_done, lo_done = s.sem(f"{name}_hi"), s.sem(f"{name}_lo")

    @block.scalar
    def _(act):
        act.wait_ge(ready, ready_at)
        for full, (hi, lo) in pairs:
            nc.scalar.activation(hi, full, ACT.Copy).then_inc(hi_done, 1)

    @block.vector
    def _(dve):
        for n, (full, (hi, lo)) in enumerate(pairs):
            dve.wait_ge(hi_done, n + 1)
            nc.vector.tensor_tensor(lo, full, hi.bitcast(F32), ALU.subtract).then_inc(lo_done, 1)


def load_layer3(nc, io, w):
    with Scope(nc, "load3") as s:
        Wf = s.sb("Wf", [P, CT, 4 * C])
        selF = s.sb("selF", [P, 16, P])
        maskf = s.sb("maskf", [P, 2, P])
        w_in, consts = s.sem("w_in"), s.sem("consts")
        with nc.Block(no_gpsimd_drain=True) as block:
            @block.sync
            def _(sp):
                loads = [(Wf[:, :, 0:3 * C], io["Win"].rearrange("(k p) d -> p k d", p=P)),
                         (Wf[:, :, 3 * C:4 * C], io["Wo3"].rearrange("(k p) d -> p k d", p=P)),
                         (selF[:, :, :], io["sel"].rearrange("n p m -> p n m")),
                         (w["bqk"][:, :], io["bqk"]), (w["ones_row"][:, :], io["ones_row"]),
                         (w["cos"][:, :, :], io["cos"].rearrange("(n p) d -> p n d", p=P)),
                         (w["sin"][:, :, :], io["sin"].rearrange("(n p) d -> p n d", p=P)),
                         (w["ident"][:, :], io["ident"]),
                         (maskf[:, 0, :], io["mask"]), (maskf[:, 1, :], io["maskT"])]
                loads += [(w[n][:, :], io[n].partition_broadcast(P)) for n in ("bv", "bo", "ln1w", "ln1b")]
                for dst, src in loads:
                    sp.dma_start(dst, src).then_inc(w_in, 16)
                sp.wait_ge(w_in, 16 * len(loads))

            @block.gpsimd
            def _(pool):
                nc.gpsimd.memset(w["nhalf"][:, :], -0.5).then_inc(consts, 1)
                nc.gpsimd.memset(w["V"][:, :, :, :], 1.0).then_inc(consts, 1)
                pool.wait_ge(consts, 2)
            split(nc, block, "w", s, [(Wf[:, :, :], [w[f"W{i}"][:, :, :] for i in range(2)])], w_in, 224)

            @block.scalar
            def _(act):
                nc.scalar.activation(w["sel"][:, :, :], selF[:, :, :], ACT.Copy)
                nc.scalar.activation(w["identb"][:, :], w["ident"][:, :], ACT.Copy)
                for i, name in enumerate(("maskb", "maskTb")):
                    nc.scalar.activation(w[name][:, :], maskf[:, i, :], ACT.Copy)
        s.clear()


def layer3_attention(nc, io, x_prev, x_next):
    with Scope(nc, "keep3") as keep:
        sb = keep.sb
        w = dict(W0=sb("W0", [P, CT, 4 * C], F32R), W1=sb("W1", [P, CT, 4 * C], F32R), sel=sb("sel", [P, 16, P], F32R),
                 bqk=sb("bqk", [P, 4]), ones_row=sb("ones_row", [P, 1]), cos=sb("cos", [P, NT, D3]),
                 sin=sb("sin", [P, NT, D3]), ident=sb("ident", [P, P]), identb=sb("identb", [P, P], BF16),
                 maskb=sb("maskb", [P, P], BF16), maskTb=sb("maskTb", [P, P], BF16), bv=sb("bv", [P, C]),
                 bo=sb("bo", [P, C]), ln1w=sb("ln1w", [P, C]), ln1b=sb("ln1b", [P, C]), nhalf=sb("nhalf", [P, 1]),
                 V=sb("V", [P, NT, H3, ROWS3]))
        load_layer3(nc, io, w)
        W = [w["W0"], w["W1"]]
        sel, V, ident, identb = w["sel"], w["V"], w["ident"], w["identb"]
        xn = sb("xn", [P, NT, C])
        qs = sb("qs", [P, PAIRS, T], F32R)
        ks = sb("ks", [P, PAIRS, T], F32R)
        ctx = sb("ctx", [P, NT, C])

        with nc.Fori(0, B) as b:
            with Scope(nc, "proj3") as s:
                rope = s.sb("rope", [P, NT, C])
                rope2 = s.sb("rope2", [P, NT, C])
                xT = [s.sb(f"xT{i}", [P, CT, T], F32R) for i in range(2)]
                rT = [s.sb(f"rT{i}", [P, CT, T], F32R) for i in range(2)]
                qk = [s.sb(f"qk{i}", [P, 2 * CT, T], F32R) for i in range(2)]
                NB = 8
                bank = [s.ps(f"bank{i}", [P, 512]) for i in range(NB)]
                x_in, rope_done, slot_ps, act_read, dve_read = (
                    s.sem(n) for n in ("x_in", "rope_done", "slot_ps", "act_read", "dve_read"))
                slots = [("x", c, k) for c in range(CHUNKS) for k in range(CT)]
                slots += [("v", t, 0) for t in range(NT)]
                slots += [("r", c, k) for c in range(CHUNKS) for k in range(CT)]
                slots += [("qk", m, c) for m in range(2 * CT) for c in range(CHUNKS)]
                slots += [(z, g, c) for g in range(PAIRS) for c in range(CHUNKS) for z in ("sq", "sk")]
                at = {n: i for i, n in enumerate(slots)}
                by_act = {n: sum(m[0] in ("x", "r", "qk", "sk") for m in slots[:i + 1]) for n, i in at.items()}
                by_dve = {n: sum(m[0] != "sk" for m in slots[:i + 1]) for n, i in at.items()}

                with nc.Block(no_gpsimd_drain=True) as block:
                    @block.sync
                    def _(sp):
                        sp.dma_start(xn[:, :, :], x_prev[bass.ts(b, T), :].rearrange("(n p) c -> p n c", p=P)).then_inc(x_in, 16)

                    @block.tensor
                    def _(pe):
                        def take(name):
                            i = at[name]
                            if i >= NB:
                                before = slots[i - NB]
                                if before[0] == "sk":
                                    pe.wait_ge(act_read, by_act[before])
                                else:
                                    pe.wait_ge(dve_read, by_dve[before])
                            return bank[i % NB]

                        pe.wait_ge(x_in, 16)
                        for name in slots:
                            kind, a, c = name
                            if kind == "r" and a == 0 and c == 0:
                                pe.wait_ge(rope_done, 4)
                            if kind == "v" and a == 0:
                                pe.wait_ge(dve_read, by_dve["x", CHUNKS - 1, CT - 1])
                            if kind == "qk" and a == 0 and c == 0:
                                pe.wait_ge(dve_read, by_dve["r", CHUNKS - 1, CT - 1])
                            if kind == "sq" and a % 4 == 0 and c == 0:
                                pe.wait_ge(dve_read, by_dve["qk", 2 * CT - 1, CHUNKS - 1])
                            ps = take(name)
                            if kind in "xr":
                                src = xn if kind == "x" else rope
                                for t in range(TPC):
                                    last = nc.tensor.transpose(ps[:, t * P:(t + 1) * P],
                                                               src[:, a * TPC + t, c * P:(c + 1) * P], ident[:, :])
                            elif kind == "v":
                                for k in range(CT):
                                    last = mm3(nc, ps[:, 0:C], [z[:, k, a * P:(a + 1) * P] for z in xT],
                                               [z[:, k, 2 * C:3 * C] for z in W], k == 0, k == CT - 1)
                            elif kind == "qk":
                                for k in range(CT):
                                    last = mm3(nc, ps[:, :], [z[:, k, a * P:(a + 1) * P] for z in W],
                                               [z[:, k, c * CHUNK:(c + 1) * CHUNK] for z in rT], k == 0, k == CT - 1)
                            else:
                                n, m = (0, 0) if kind == "sq" else (8, CT)
                                for i in range(2):
                                    last = nc.tensor.matmul(ps[:, :], sel[:, n + 2 * (a % 4) + i, :],
                                                            qk[i][:, m + a // 4, c * CHUNK:(c + 1) * CHUNK],
                                                            start=(i == 0), stop=(i == 1))
                            last.then_inc(slot_ps, 1)

                    @block.scalar
                    def _(act):
                        for name in slots:
                            kind, a, c = name
                            ps, cols = bank[at[name] % NB], slice(c * CHUNK, (c + 1) * CHUNK)
                            if kind in ("v", "sq"):
                                continue
                            act.wait_ge(slot_ps, at[name] + 1)
                            if kind in "xr":
                                dst = (xT if kind == "x" else rT)[0][:, c, a * CHUNK:(a + 1) * CHUNK]
                                i = nc.scalar.activation(dst, ps[:, :], ACT.Copy)
                            elif kind == "qk":
                                i = nc.scalar.activation(qk[0][:, a, cols], ps[:, :], ACT.Identity, bias=w["bqk"][:, a:a + 1])
                            else:
                                i = nc.scalar.activation(ks[:, a, cols], ps[:, :], ACT.Identity, bias=w["ones_row"][:, 0:1])
                            i.then_inc(act_read, 1)

                    @block.vector
                    def _(dve):
                        dve.wait_ge(x_in, 16)
                        x4 = xn[:, :, :].rearrange("p n (h i two) -> p n h i two", h=H3, two=2)
                        r4 = rope2[:, :, :].rearrange("p n (h i two) -> p n h i two", h=H3, two=2)
                        cosb = w["cos"][:, :, :].unsqueeze(2).to_broadcast([P, NT, H3, D3])
                        sin4 = w["sin"][:, :, :].rearrange("p n (i two) -> p n i two", two=2)
                        nc.vector.tensor_tensor(rope[:, :, :].rearrange("p n (h d) -> p n h d", h=H3),
                                                xn[:, :, :].rearrange("p n (h d) -> p n h d", h=H3), cosb, ALU.mult).then_inc(rope_done, 1)
                        for z in range(2):
                            nc.vector.tensor_tensor(r4[:, :, :, :, z], x4[:, :, :, :, 1 - z],
                                                    sin4[:, :, :, z].unsqueeze(2).to_broadcast([P, NT, H3, D3 // 2]),
                                                    ALU.mult).then_inc(rope_done, 1)
                        dve.wait_ge(rope_done, 3)
                        nc.vector.tensor_tensor(rope[:, :, :], rope[:, :, :], rope2[:, :, :], ALU.add).then_inc(rope_done, 1)
                        for name in slots:
                            kind, a, c = name
                            ps, cols = bank[at[name] % NB], slice(c * CHUNK, (c + 1) * CHUNK)
                            if kind == "sk":
                                continue
                            if kind in ("x", "r", "qk"):
                                dve.wait_ge(act_read, by_act[name])
                            else:
                                dve.wait_ge(slot_ps, at[name] + 1)
                            if kind in "xr":
                                hi, lo = [z[:, c, a * CHUNK:(a + 1) * CHUNK] for z in (xT if kind == "x" else rT)]
                                i = nc.vector.tensor_tensor(lo, ps[:, :], hi.bitcast(F32), ALU.subtract)
                            elif kind == "v":
                                i = nc.vector.tensor_tensor(V[:, a, :, 0:D3], ps[:, 0:C].rearrange("p (h d) -> p h d", h=H3),
                                                            w["bv"][:, :].rearrange("p (h d) -> p h d", h=H3), ALU.add)
                            elif kind == "qk":
                                i = nc.vector.scalar_tensor_tensor(out=qk[1][:, a, cols], in0=ps[:, :], scalar=w["bqk"][:, a:a + 1],
                                                                   in1=qk[0][:, a, cols].bitcast(F32), op0=ALU.add, op1=ALU.subtract)
                            else:
                                i = nc.vector.tensor_copy(qs[:, a, cols], ps[:, :])
                            i.then_inc(dve_read, 1)
                s.clear()

            with Scope(nc, "max3") as s:
                mx = s.sb("mx", [P, NT, 2, H3])
                mf = s.sb("mf", [P, NT, H3])
                mT = s.sb("mT", [H3, T], F32R)
                psS = [s.ps(f"psS{i}", [P, 4, 512]) for i in range(2)]
                s_ps, max_done, mf_done, t_ps, mT_done, rows_in = (
                    s.sem(n) for n in ("s_ps", "max_done", "mf_done", "t_ps", "mT_done", "rows_in"))
                units = [(t, c, gg) for t in range(NT) for c in range(t // TPC + 1) for gg in range(PAIRS // 2)]

                def width(t, c):
                    return min(CHUNK, (t + 1) * P - c * CHUNK)

                with nc.Block(no_gpsimd_drain=True) as block:
                    @block.tensor
                    def _(pe):
                        for n, (t, c, gg) in enumerate(units):
                            if n >= 2:
                                pe.wait_ge(max_done, n - 1)
                            ps, wd, diag = psS[n % 2], width(t, c), c == t // TPC
                            for i in range(4):
                                g, rows = 2 * gg + i // 2, slice(64 * (i % 2), 64 * (i % 2) + 64)
                                last = nc.tensor.matmul(ps[:, i, 0:wd], qs[rows, g, t * P:(t + 1) * P],
                                                        ks[rows, g, c * CHUNK:c * CHUNK + wd], start=True, stop=not diag)
                            if diag:
                                for i in range(4):
                                    last = nc.tensor.matmul(ps[:, i, wd - P:wd], identb[:, :], w["maskb"][:, :],
                                                            start=False, stop=True)
                            last.then_inc(s_ps, 1)
                        pe.wait_ge(mf_done, 2)
                        for t in range(NT):
                            last = nc.tensor.transpose(psS[0][0:H3, t // TPC, t % TPC * P:(t % TPC + 1) * P], mf[:, t, :], ident[:, :])
                        last.then_inc(t_ps, 1)

                    @block.vector
                    def _(dve):
                        for n, (t, c, gg) in enumerate(units):
                            dve.wait_ge(s_ps, n + 1)
                            out = mx[:, t, c, :].rearrange("p (two g) -> p g two", two=2)[:, 2 * gg:2 * gg + 2, :]
                            nc.vector.tensor_reduce(out, psS[n % 2][:, :, 0:width(t, c)].rearrange("p (g two) w -> p g two w", two=2),
                                                    X, ALU.max).then_inc(max_done, 1)
                        dve.wait_ge(max_done, len(units))
                        nc.vector.tensor_copy(mf[:, 0:TPC, :], mx[:, 0:TPC, 0, :]).then_inc(mf_done, 1)
                        nc.vector.tensor_tensor(mf[:, TPC:NT, :], mx[:, TPC:NT, 0, :], mx[:, TPC:NT, 1, :], ALU.max).then_inc(mf_done, 1)

                    @block.scalar
                    def _(act):
                        act.wait_ge(t_ps, 1)
                        nc.scalar.activation(mT[:, :].rearrange("h (c t) -> h c t", c=CHUNKS), psS[0][0:H3, 0:CHUNKS, :],
                                             ACT.Copy, scale=-1.0).then_inc(mT_done, 1)

                    @block.sync
                    def _(sp):
                        sp.wait_ge(mT_done, 1)
                        for p in range(2):
                            for g in range(PAIRS):
                                sp.dma_start(qs[64 * p + 32:64 * p + 33, g, :].bitcast(F32), mT[8 * p + g:8 * p + g + 1, :].bitcast(F32)).then_inc(rows_in, 16)
                        sp.wait_ge(rows_in, 16 * H3)
                s.clear()

            with Scope(nc, "attn3") as s:
                pT = s.sb("pT", [P, 3, 2, CHUNK])
                raw = s.sb("raw", [P, 2, CHUNK])
                rinv = s.sb("rinv", [P, 2, TPC, 4, 1])
                psS = [s.ps(f"psS{i}", [P, 2, 512]) for i in range(3)]
                psO = s.ps("psO", [P, CHUNK])
                psT = s.ps("psT", [P, TPC, 4, ROWS3])
                s_ps, exp_done, o_ps, raw_done, t_ps, r_done, c_done = (
                    s.sem(n) for n in ("s_ps", "exp_done", "o_ps", "raw_done", "t_ps", "r_done", "c_done"))
                rounds = [(c, gg) for c in range(CHUNKS) for gg in range(H3 // 4)]
                units = [(r, c, 2 * gg + z, j) for r, (c, gg) in enumerate(rounds) for j in range((c + 1) * TPC) for z in range(2)]

                def span(c, j):
                    lo = max(j * P, c * CHUNK)
                    return lo, (c + 1) * CHUNK - lo, j * P >= c * CHUNK

                with nc.Block(no_gpsimd_drain=True) as block:
                    @block.tensor
                    def _(pe):
                        def scores(n):
                            r, c, g, j = units[n]
                            lo, wd, diag = span(c, j)
                            if n >= 3:
                                pe.wait_ge(exp_done, n - 2)
                            for p in range(2):
                                last = nc.tensor.matmul(psS[n % 3][:, p, 0:wd], ks[64 * p:64 * p + 64, g, j * P:(j + 1) * P],
                                                        qs[64 * p:64 * p + 64, g, lo:lo + wd], start=True, stop=not diag)
                            if diag:
                                for p in range(2):
                                    last = nc.tensor.matmul(psS[n % 3][:, p, 0:P], identb[:, :], w["maskTb"][:, :],
                                                            start=False, stop=True)
                            last.then_inc(s_ps, 1)

                        def weighted(n):
                            r, c, g, j = units[n]
                            lo, wd, diag = span(c, j)
                            pe.wait_ge(exp_done, n + 1)
                            if j == 0 and r >= 1:
                                pe.wait_ge(raw_done, r)
                            for p in range(2):
                                i = 2 * (g % 2) + p
                                last = nc.tensor.matmul(psO[ROWS3 * i:ROWS3 * (i + 1), lo - c * CHUNK:CHUNK], V[:, j, 2 * g + p, :],
                                                        pT[:, n % 3, p, 0:wd], start=(j == 0), stop=(j == (c + 1) * TPC - 1))
                            last.then_inc(o_ps, 1)

                        def transpose_round(r):
                            pe.wait_ge(raw_done, r + 1)
                            if r >= 1:
                                pe.wait_ge(c_done, r)
                            for t in range(TPC):
                                last = nc.tensor.transpose(psT[:, t, :, :].rearrange("p h d -> p (h d)"),
                                                           raw[:, r % 2, t * P:(t + 1) * P], ident[:, :])
                            last.then_inc(t_ps, 1)

                        scores(0)
                        scores(1)
                        for n in range(len(units)):
                            if n + 2 < len(units):
                                scores(n + 2)
                            weighted(n)
                            r, j, second = units[n][0], units[n][3], n % 2 == 1
                            if r >= 1 and j == 1 and second:
                                transpose_round(r - 1)
                        transpose_round(len(rounds) - 1)

                    @block.scalar
                    def _(act):
                        for n, (r, c, g, j) in enumerate(units):
                            act.wait_ge(s_ps, n + 1)
                            if n >= 3:
                                act.wait_ge(o_ps, n - 2)
                            wd = span(c, j)[1]
                            nc.scalar.activation(pT[:, n % 3, :, 0:wd], psS[n % 3][:, :, 0:wd], ACT.Exp, scale=SCALE3).then_inc(exp_done, 1)

                    @block.vector
                    def _(dve):
                        def divide(r):
                            c, gg = rounds[r]
                            dve.wait_ge(t_ps, r + 1)
                            nc.vector.reciprocal(rinv[:, r % 2, :, :, :], psT[:, :, :, D3:D3 + 1]).then_inc(r_done, 1)
                            dve.wait_ge(r_done, r + 1)
                            nc.vector.tensor_tensor(
                                ctx[:, c * TPC:(c + 1) * TPC, 4 * gg * D3:(4 * gg + 4) * D3].rearrange("p t (h d) -> p t h d", h=4),
                                psT[:, :, :, 0:D3], rinv[:, r % 2, :, :, :].to_broadcast([P, TPC, 4, D3]),
                                ALU.mult).then_inc(c_done, 1)

                        done = 0
                        for r, (c, gg) in enumerate(rounds):
                            done += 2 * (c + 1) * TPC
                            dve.wait_ge(o_ps, done)
                            nc.vector.tensor_copy(raw[:, r % 2, :], psO[:, :]).then_inc(raw_done, 1)
                            if r >= 1:
                                divide(r - 1)
                        divide(len(rounds) - 1)
                s.clear()

            with Scope(nc, "out3") as s:
                cT = [s.sb(f"cT{i}", [P, CT, T], F32R) for i in range(2)]
                y = s.sb("y", [P, NT, C])
                stats = s.sb("stats", [P, NT, 6])
                mv = s.sb("mv", [P, NT, 2])
                veps = s.sb("veps", [P, NT])
                rstd = s.sb("rstd", [P, NT])
                psT = [s.ps(f"psT{i}", [P, 512]) for i in range(4)]
                psY = [s.ps(f"psY{i}", [P, 512]) for i in range(4)]
                xb_done, t_ps, hi_done, lo_done, y_ps, y_done = (
                    s.sem(n) for n in ("xb_done", "t_ps", "hi_done", "lo_done", "y_ps", "y_done"))
                st_done, veps_done, rstd_done, ln_done, aff_done, out_st = (
                    s.sem(n) for n in ("st_done", "veps_done", "rstd_done", "ln_done", "aff_done", "out_st"))
                groups = [(c, k) for c in range(CHUNKS) for k in range(CT)]
                with nc.Block(no_gpsimd_drain=True) as block:
                    @block.sync
                    def _(sp):
                        sp.wait_ge(aff_done, 2 * NT)
                        sp.dma_start(x_next[bass.ts(b, T), :].rearrange("(n p) c -> p n c", p=P), y[:, :, :]).then_inc(out_st, 16)
                        sp.wait_ge(out_st, 16)

                    @block.tensor
                    def _(pe):
                        for n, (c, k) in enumerate(groups):
                            for t in range(TPC):
                                last = nc.tensor.transpose(psT[n][:, t * P:(t + 1) * P], ctx[:, c * TPC + t, k * P:(k + 1) * P], ident[:, :])
                            last.then_inc(t_ps, 1)
                        for t in range(NT):
                            pe.wait_ge(lo_done, CT * (t // TPC + 1))
                            if t >= 4:
                                pe.wait_ge(y_done, t - 3)
                            for k in range(CT):
                                last = mm3(nc, psY[t % 4][:, 0:C], [z[:, k, t * P:(t + 1) * P] for z in cT],
                                           [z[:, k, 3 * C:4 * C] for z in W], k == 0, k == CT - 1)
                            last.then_inc(y_ps, 1)

                    @block.scalar
                    def _(act):
                        for n, (c, k) in enumerate(groups):
                            act.wait_ge(t_ps, n + 1)
                            nc.scalar.activation(cT[0][:, k, c * CHUNK:(c + 1) * CHUNK], psT[n][:, :], ACT.Copy).then_inc(hi_done, 1)

                    @block.gpsimd
                    def _(pool):
                        for t in range(NT):
                            nc.gpsimd.tensor_tensor(xn[:, t, :], xn[:, t, :], w["bo"][:, :], ALU.add).then_inc(xb_done, 1)
                        for t in range(NT):
                            pool.wait_ge(veps_done, t + 1)
                            nc.gpsimd.tensor_tensor(rstd[:, t:t + 1], veps[:, t:t + 1], w["nhalf"][:, :], ALU.pow).then_inc(rstd_done, 1)

                    @block.vector
                    def _(dve):
                        for n, (c, k) in enumerate(groups):
                            dve.wait_ge(hi_done, n + 1)
                            cols = slice(c * CHUNK, (c + 1) * CHUNK)
                            nc.vector.tensor_tensor(cT[1][:, k, cols], psT[n][:, :], cT[0][:, k, cols].bitcast(F32), ALU.subtract).then_inc(lo_done, 1)

                        def affine(t):
                            dve.wait_ge(rstd_done, t + 1)
                            nc.vector.tensor_scalar(y[:, t, :], y[:, t, :], mv[:, t, 0:1], rstd[:, t:t + 1],
                                                    ALU.subtract, ALU.mult).then_inc(ln_done, 1)
                            dve.wait_ge(ln_done, t + 1)
                            nc.vector.tensor_tensor(y[:, t, :], y[:, t, :], w["ln1w"][:, :], ALU.mult).then_inc(aff_done, 1)
                            dve.wait_ge(aff_done, 2 * t + 1)
                            nc.vector.tensor_tensor(y[:, t, :], y[:, t, :], w["ln1b"][:, :], ALU.add).then_inc(aff_done, 1)

                        for t in range(NT):
                            dve.wait_ge(y_ps, t + 1)
                            dve.wait_ge(xb_done, t + 1)
                            nc.vector.tensor_tensor(y[:, t, :], psY[t % 4][:, 0:C], xn[:, t, :], ALU.add).then_inc(y_done, 1)
                            dve.wait_ge(y_done, t + 1)
                            nc.vector.bn_stats(stats[:, t, :], y[:, t, :]).then_inc(st_done, 1)
                            dve.wait_ge(st_done, 2 * t + 1)
                            nc.vector.bn_aggr(mv[:, t, :], stats[:, t, :]).then_inc(st_done, 1)
                            dve.wait_ge(st_done, 2 * t + 2)
                            nc.vector.tensor_scalar(veps[:, t:t + 1], mv[:, t, 1:2], EPS, None, ALU.add).then_inc(veps_done, 1)
                            if t >= 1:
                                affine(t - 1)
                        affine(NT - 1)
                s.clear()


def experts(nc, io, x_prev, x1_in, out):
    with Scope(nc, "keep4") as keep:
        sb = keep.sb
        We = [sb(f"We{i}", [P, CT, NE * C], F32R) for i in range(2)]
        Wg = [sb(f"Wg{i}", [P, CT, NE], F32R) for i in range(2)]
        eb = sb("eb", [NE, C])
        gb, ln2w, ln2b = sb("gb", [P, NE]), sb("ln2w", [P, C]), sb("ln2b", [P, C])
        ident, nhalf, number = sb("ident", [P, P]), sb("nhalf", [P, 1]), sb("number", [P, NE])
        with Scope(nc, "load4") as s:
            Wf = s.sb("Wf", [P, CT, NE * C])
            Wgf = s.sb("Wgf", [P, CT, NE])
            w_in, consts = s.sem("w_in"), s.sem("consts")
            with nc.Block(no_gpsimd_drain=True) as block:
                @block.sync
                def _(sp):
                    for dst, src in ((Wf[:, :, :], io["We"].rearrange("(k p) f -> p k f", p=P)),
                                     (Wgf[:, :, :], io["Wg"].rearrange("(k p) e -> p k e", p=P)), (eb[:, :], io["eb"]),
                                     (gb[:, :], io["gb"].partition_broadcast(P)), (ln2w[:, :], io["ln2w"].partition_broadcast(P)),
                                     (ln2b[:, :], io["ln2b"].partition_broadcast(P)), (ident[:, :], io["ident"]),
                                     (number[:, :], io["number"].partition_broadcast(P))):
                        sp.dma_start(dst, src).then_inc(w_in, 16)
                    sp.wait_ge(w_in, 128)

                @block.gpsimd
                def _(pool):
                    nc.gpsimd.memset(nhalf[:, :], -0.5).then_inc(consts, 1)
                    pool.wait_ge(consts, 1)
                split(nc, block, "w", s, [(Wf[:, k, :], [z[:, k, :] for z in We]) for k in range(CT)]
                      + [(Wgf[:, :, :], [z[:, :, :] for z in Wg])], w_in, 128)
            s.clear()

        with Scope(nc, "moe") as s:
            xn = s.sb("xn", [P, NT, C])
            x1 = s.sb("x1", [P, NT, C])
            xT = [s.sb(f"xT{i}", [P, CT, T], F32R) for i in range(2)]
            lg = s.sb("lg", [P, NT, NE])
            ex = s.sb("ex", [P, NT, NE])
            gate = s.sb("gate", [P, NT, NE])
            is1, is2 = s.sb("is1", [P, NT, NE]), s.sb("is2", [P, NT, NE])
            top = s.sb("top", [P, NT, 8])
            idx = s.sb("idx", [P, NT, 8], U32)
            idxf = s.sb("idxf", [P, NT, 8])
            gsum, ginv = s.sb("gsum", [P, NT]), s.sb("ginv", [P, NT])
            gT = s.sb("gT", [NE, T])
            acc = s.sb("acc", [P, NT, C])
            stats = s.sb("stats", [P, 2 * NT, 6])
            mv = s.sb("mv", [P, 2 * NT, 2])
            veps = s.sb("veps", [P, 2 * NT])
            rstd = s.sb("rstd", [P, 2 * NT])
            psE = [s.ps(f"psE{i}", [P, 2, C]) for i in range(6)]
            psB = [s.ps(f"psB{i}", [P, 512]) for i in range(2)]
            x_in, t_ps, hi_done, lo_done = s.sem("x_in"), s.sem("t_ps"), s.sem("hi_done"), s.sem("lo_done")
            g_ps, lg_done, top_done, ex_done, gate_step, gate_done, gT_ps, gT_done = (
                s.sem(n) for n in ("g_ps", "lg_done", "top_done", "ex_done", "gate_step", "gate_done", "gT_ps", "gT_done"))
            e_ps, e_done, b_ps, b_done = s.sem("e_ps"), s.sem("e_done"), s.sem("b_ps"), s.sem("b_done")
            st_done, veps_done, rstd_done, ln2_done, aff_w, aff_b, res_done, fin_done, out_st = (
                s.sem(n) for n in ("st_done", "veps_done", "rstd_done", "ln2_done", "aff_w", "aff_b", "res_done", "fin_done", "out_st"))
            groups = [(c, k) for c in range(CHUNKS) for k in range(CT)]
            EP = NE // 2
            norms = [("moe", 0)]
            for t in range(1, NT):
                norms += [("moe", t), ("out", t - 1)]
            norms.append(("out", NT - 1))
            nth = {name: n for n, name in enumerate(norms)}

            with nc.Fori(0, B) as b:
                with nc.Block(no_gpsimd_drain=True) as block:
                    @block.sync
                    def _(sp):
                        sp.dma_start(x1[:, :, :], x1_in[bass.ts(b, T), :].rearrange("(n p) c -> p n c", p=P)).then_inc(x_in, 16)
                        sp.dma_start(xn[:, :, :], x_prev[bass.ts(b, T), :].rearrange("(n p) c -> p n c", p=P)).then_inc(x_in, 16)
                        sp.wait_ge(fin_done, NT)
                        sp.dma_start(out[bass.ts(b, T), :].rearrange("(n p) c -> p n c", p=P), acc[:, :, :]).then_inc(out_st, 16)
                        sp.wait_ge(out_st, 16)

                    @block.tensor
                    def _(pe):
                        pe.wait_ge(x_in, 32)
                        for n, (c, k) in enumerate(groups):
                            for t in range(TPC):
                                last = nc.tensor.transpose(psE[n][:, t // 2, t % 2 * P:(t % 2 + 1) * P],
                                                           x1[:, c * TPC + t, k * P:(k + 1) * P], ident[:, :])
                            last.then_inc(t_ps, 1)
                        pe.wait_ge(lo_done, len(groups))
                        for t in range(NT):
                            for k in range(CT):
                                last = mm3(nc, psB[0][:, t * NE:(t + 1) * NE], [z[:, k, t * P:(t + 1) * P] for z in xT],
                                           [z[:, k, :] for z in Wg], k == 0, k == CT - 1)
                        last.then_inc(g_ps, 1)

                        def expert_pair(n):
                            t, e = divmod(n, EP)
                            if n >= 6:
                                pe.wait_ge(e_done, 2 * (n - 5))
                            for k in range(CT):
                                last = mm3(nc, psE[n % 6][:, :, :], [z[:, k, t * P:(t + 1) * P] for z in xT],
                                           [z[:, k, 2 * e * C:(2 * e + 2) * C] for z in We], k == 0, k == CT - 1)
                            last.then_inc(e_ps, 1)

                        for n in range(NT * EP):
                            expert_pair(n)
                            if n == 5:
                                pe.wait_ge(gate_done, 1)
                                for t in range(NT):
                                    last = nc.tensor.transpose(psB[t // TPC][0:NE, t % TPC * P:(t % TPC + 1) * P], gate[:, t, :], ident[:, :])
                                last.then_inc(gT_ps, 1)
                                pe.wait_ge(gT_done, 2)
                                for t in range(2):
                                    nc.tensor.matmul(psB[t][:, 0:C], gT[:, t * P:(t + 1) * P], eb[:, :], start=True, stop=True).then_inc(b_ps, 1)
                            if n % EP == EP - 1 and 2 <= n // EP + 1 < NT and n > 5:
                                t = n // EP + 1
                                pe.wait_ge(b_done, t - 1)
                                nc.tensor.matmul(psB[t % 2][:, 0:C], gT[:, t * P:(t + 1) * P], eb[:, :], start=True, stop=True).then_inc(b_ps, 1)

                    @block.scalar
                    def _(act):
                        for n, (c, k) in enumerate(groups):
                            act.wait_ge(t_ps, n + 1)
                            nc.scalar.activation(xT[0][:, k, c * CHUNK:(c + 1) * CHUNK], psE[n][:, :, :].rearrange("p a w -> p (a w)"),
                                                 ACT.Copy).then_inc(hi_done, 1)
                        act.wait_ge(gate_step, 1)
                        nc.scalar.activation(ex[:, :, :], ex[:, :, :], ACT.Exp).then_inc(ex_done, 1)
                        act.wait_ge(gT_ps, 1)
                        for c in range(CHUNKS):
                            nc.scalar.activation(gT[:, c * CHUNK:(c + 1) * CHUNK], psB[c][0:NE, :], ACT.Copy).then_inc(gT_done, 1)

                    @block.gpsimd
                    def _(pool):
                        for n in range(2 * NT):
                            pool.wait_ge(veps_done, n + 1)
                            i = nc.gpsimd.tensor_tensor(rstd[:, n:n + 1], veps[:, n:n + 1], nhalf[:, :], ALU.pow)
                            i.then_inc(rstd_done, 1)

                    @block.vector
                    def _(dve):
                        for n, (c, k) in enumerate(groups):
                            dve.wait_ge(hi_done, n + 1)
                            cols = slice(c * CHUNK, (c + 1) * CHUNK)
                            nc.vector.tensor_tensor(xT[1][:, k, cols], psE[n][:, :, :].rearrange("p a w -> p (a w)"),
                                                    xT[0][:, k, cols].bitcast(F32), ALU.subtract).then_inc(lo_done, 1)
                        dve.wait_ge(g_ps, 1)
                        nc.vector.tensor_tensor(lg[:, :, :], psB[0][:, 0:NT * NE].rearrange("p (t e) -> p t e", e=NE),
                                                gb[:, :].unsqueeze(1).to_broadcast([P, NT, NE]), ALU.add).then_inc(lg_done, 1)
                        dve.wait_ge(lg_done, 1)
                        for t in range(NT):
                            last = nc.vector.max(top[:, t, :], lg[:, t, :])
                        last.then_inc(top_done, 1)
                        dve.wait_ge(top_done, 1)
                        nc.vector.tensor_tensor(ex[:, :, :], lg[:, :, :], top[:, :, 0:1].to_broadcast([P, NT, NE]),
                                                ALU.subtract).then_inc(gate_step, 1)
                        for t in range(NT):
                            last = nc.vector.max_index(idx[:, t, :], top[:, t, :], lg[:, t, :])
                        last.then_inc(top_done, 1)
                        dve.wait_ge(top_done, 2)
                        nc.vector.tensor_copy(idxf[:, :, :], idx[:, :, :]).then_inc(gate_step, 1)
                        dve.wait_ge(gate_step, 2)
                        numbers = number[:, :].unsqueeze(1).to_broadcast([P, NT, NE])
                        nc.vector.tensor_tensor(is1[:, :, :], numbers, idxf[:, :, 0:1].to_broadcast([P, NT, NE]), ALU.is_equal).then_inc(gate_step, 1)
                        nc.vector.tensor_tensor(is2[:, :, :], numbers, idxf[:, :, 1:2].to_broadcast([P, NT, NE]), ALU.is_equal).then_inc(gate_step, 1)
                        dve.wait_ge(gate_step, 4)
                        nc.vector.tensor_tensor(is1[:, :, :], is1[:, :, :], is2[:, :, :], ALU.add).then_inc(gate_step, 1)
                        dve.wait_ge(ex_done, 1)
                        nc.vector.tensor_reduce(gsum[:, :], ex[:, :, :], X, ALU.add).then_inc(gate_step, 1)
                        dve.wait_ge(gate_step, 6)
                        nc.vector.reciprocal(ginv[:, :], gsum[:, :]).then_inc(gate_step, 1)
                        nc.vector.tensor_tensor(gate[:, :, :], ex[:, :, :], is1[:, :, :], ALU.mult).then_inc(gate_step, 1)
                        dve.wait_ge(gate_step, 8)
                        nc.vector.tensor_tensor(gate[:, :, :], gate[:, :, :], ginv[:, :].unsqueeze(2).to_broadcast([P, NT, NE]),
                                                ALU.mult).then_inc(gate_done, 1)

                        def statistics(n, src):
                            nc.vector.bn_stats(stats[:, n, :], src).then_inc(st_done, 1)
                            dve.wait_ge(st_done, 2 * n + 1)
                            nc.vector.bn_aggr(mv[:, n, :], stats[:, n, :]).then_inc(st_done, 1)
                            dve.wait_ge(st_done, 2 * n + 2)
                            nc.vector.tensor_scalar(veps[:, n:n + 1], mv[:, n, 1:2], EPS, None, ALU.add).then_inc(veps_done, 1)

                        def scaled(n, t, done):
                            dve.wait_ge(rstd_done, n + 1)
                            nc.vector.tensor_scalar(acc[:, t, :], acc[:, t, :], mv[:, n, 0:1], rstd[:, n:n + 1],
                                                    ALU.subtract, ALU.mult).then_inc(done, 1)

                        def ending(t):
                            scaled(nth["moe", t], t, ln2_done)
                            dve.wait_ge(ln2_done, t + 1)
                            nc.vector.tensor_tensor(acc[:, t, :], acc[:, t, :], ln2w[:, :], ALU.mult).then_inc(aff_w, 1)
                            dve.wait_ge(aff_w, t + 1)
                            nc.vector.tensor_tensor(acc[:, t, :], acc[:, t, :], ln2b[:, :], ALU.add).then_inc(aff_b, 1)
                            dve.wait_ge(aff_b, t + 1)
                            nc.vector.tensor_tensor(acc[:, t, :], acc[:, t, :], xn[:, t, :], ALU.add).then_inc(res_done, 1)
                            dve.wait_ge(res_done, t + 1)
                            statistics(nth["out", t], acc[:, t, :])

                        for t in range(NT):
                            dve.wait_ge(b_ps, t + 1)
                            if t == 0:
                                dve.wait_ge(gate_done, 1)
                            nc.vector.tensor_tensor(acc[:, t, :], psB[t % 2][:, 0:C], x1[:, t, :], ALU.add).then_inc(b_done, 1)
                            dve.wait_ge(b_done, t + 1)
                            for e in range(NE):
                                n = t * EP + e // 2
                                if e % 2 == 0:
                                    dve.wait_ge(e_ps, n + 1)
                                if t * NE + e > 0 and e > 0:
                                    dve.wait_ge(e_done, t * NE + e)
                                nc.vector.scalar_tensor_tensor(out=acc[:, t, :], in0=psE[n % 6][:, e % 2, :], scalar=gate[:, t, e:e + 1],
                                                               in1=acc[:, t, :], op0=ALU.mult, op1=ALU.add).then_inc(e_done, 1)
                            dve.wait_ge(e_done, (t + 1) * NE)
                            statistics(nth["moe", t], acc[:, t, :])
                            if t >= 2:
                                scaled(nth["out", t - 2], t - 2, fin_done)
                            if t >= 1:
                                ending(t - 1)
                        scaled(nth["out", NT - 2], NT - 2, fin_done)
                        ending(NT - 1)
                        scaled(nth["out", NT - 1], NT - 1, fin_done)
                s.clear()


def build(nc, io, out):
    x1, x2, x3 = (nc.dram_tensor(n, (TOKENS, C), F32).ap() for n in ("x_layer1", "x_layer2", "x_attended"))
    layer1(nc, io, x1)
    layer2(nc, io, x1, x2)
    layer3_attention(nc, io, x2, x3)
    experts(nc, io, x2, x3, out)


def lay_out(inputs):
    v = {k: np.asarray(a) for k, a in inputs.items()}
    c = np.ascontiguousarray
    x = v["x"].reshape(TOKENS, C)
    eye = np.eye(P, dtype=np.float32)
    later = np.triu(np.full((P, P), -1e30, np.float32), 1)
    a = dict(
        x=x, xT=c(x.T), WaT=c(v["L0_attn_W_attn"].T), AaT=c(v["L0_attn_lora_attn_A"].T), Ba=v["L0_attn_lora_attn_B"],
        ApT=c(v["L0_attn_lora_proj_A"].T), Bp=v["L0_attn_lora_proj_B"], Wp=v["L0_attn_W_proj"],
        WpT=c(v["L0_attn_W_proj"].T), gamma=c(v["L0_attn_bn_gamma"].reshape(DT, P).T),
        beta=c(v["L0_attn_bn_beta"].reshape(DT, P).T), ident=eye, mask=later)
    a.update(
        ctxT=c(v["ctx_768"].reshape(J, CD).T), Wq2=v["L0_xattn_Wq"], Wk2=v["L0_xattn_Wk"], Wv2=v["L0_xattn_Wv"],
        Wout=v["L0_xattn_Wout"], bout=v["L0_xattn_bout"])
    inverse = (1.0 / 10000.0 ** (np.arange(0, D3, 2, dtype=np.float32) / D3)).astype(np.float32)
    angle = np.arange(T, dtype=np.float32)[:, None] * inverse[None, :]
    cos, sin = np.cos(angle), np.sin(angle)
    sel = np.zeros((2, 4, 2, P, P), np.float32)
    d = np.arange(D3)
    for pair in range(4):
        for p in range(2):
            rows, base = (2 * pair + p) * D3 + d, 64 * p
            sel[0, pair, 0, rows, base + d] = 1
            sel[0, pair, 0, rows, base + D3 + d] = 1
            sel[0, pair, 1, rows, base + 3 * D3 + d] = 1
            sel[1, pair, 0, rows, base + d] = 1
            sel[1, pair, 0, rows, base + 3 * D3 + d] = 1
            sel[1, pair, 1, rows, base + D3 + d] = 1
    ones_row = np.zeros((P, 1), np.float32)
    ones_row[[32, 96]] = 1
    a.update(
        Win=c(v["L0_ffn_in_proj_w"].T), Wo3=c(v["L0_ffn_out_proj_w"].T),
        bqk=c(v["L0_ffn_in_proj_b"][:2 * C].reshape(2 * CT, P).T), bv=v["L0_ffn_in_proj_b"][2 * C:],
        bo=v["L0_ffn_out_proj_b"], ln1w=v["L0_ffn_ln1_w"], ln1b=v["L0_ffn_ln1_b"], ln2w=v["L0_ffn_ln2_w"], ln2b=v["L0_ffn_ln2_b"],
        Wg=c(v["L0_ffn_gate_w"].T), gb=v["L0_ffn_gate_b"], eb=v["L0_ffn_expert_b"],
        We=c(v["L0_ffn_expert_w"].transpose(2, 0, 1).reshape(C, NE * C)),
        cos=c(np.repeat(cos, 2, 1)), sin=c(np.stack([-sin, sin], -1).reshape(T, D3)), sel=sel.reshape(16, P, P),
        ones_row=ones_row, maskT=c(later.T), number=np.arange(NE, dtype=np.float32))
    return a


def kernel(**inputs):
    import numpy as _np
    import concourse.bacc as _bacc
    from concourse import mybir as _mybir
    from concourse.bass_utils import run_bass_kernel_spmd as _run

    nc = _bacc.Bacc("TRN2", target_bir_lowering=False, num_devices=1)
    arrays = lay_out(inputs)
    io = {}
    for name, a in arrays.items():
        io[name] = nc.dram_tensor(f"in_{name}", a.shape, _mybir.dt.from_np(a.dtype), kind="ExternalInput").ap()
    out = nc.dram_tensor("out", (TOKENS, C), _mybir.dt.float32, kind="ExternalOutput").ap()
    build(nc, io, out)
    r = _run(nc, [{f"in_{name}": a for name, a in arrays.items()}], core_ids=[0])
    return r.results[0]["out"].reshape(B, T, C)
```

```python
import numpy as np
import concourse.bass as bass
from concourse import mybir
from contextlib import ExitStack

F32 = mybir.dt.float32
F32R = mybir.dt.float32r
BF16 = mybir.dt.bfloat16
U32 = mybir.dt.uint32
ALU = mybir.AluOpType
ACT = mybir.ActivationFunctionType
X = mybir.AxisListType.X
XY = mybir.AxisListType.XY

P = 128
B, T, C = 4, 1024, 256
CT = C // P
NT = T // P
TOKENS = B * T
EPS = 1e-5
SCALE1 = C ** -0.5
QKV = 3 * C
DT = QKV // P
LORA = 64

M, J, CD = 154, B * 154, 192
H2, D2 = 8, 128
KT2, KP2 = 2, CD // 2
JT = (J + P - 1) // P
JH = J // 2
INNER = H2 * D2
SCALE2 = D2 ** -0.5
SHARPEN = 1.5
CHUNK = 512
CHUNKS = T // CHUNK
TPC = CHUNK // P

H3, D3 = 16, 16
SCALE3 = D3 ** -0.5
PAIRS = H3 // 2
ROWS3 = 32
NE = 8


class Scope:

    def __init__(self, nc, name):
        self.nc, self.name, self.stack, self.sems = nc, name, ExitStack(), []

    def __enter__(self):
        self.stack.__enter__()
        return self

    def __exit__(self, *e):
        return self.stack.__exit__(*e)

    def sb(self, name, shape, dt=F32):
        return self.stack.enter_context(self.nc.sbuf_tensor(f"{self.name}_{name}", shape, dt))

    def ps(self, name, shape, dt=F32):
        return self.stack.enter_context(self.nc.psum_tensor(f"{self.name}_{name}", shape, dt))

    def sem(self, name):
        s = self.stack.enter_context(self.nc.semaphore(f"{self.name}_{name}"))
        self.sems.append(s)
        return s

    def clear(self):
        with self.nc.Block(no_gpsimd_drain=True) as block:
            @block.sync
            def _(sp):
                for s in self.sems:
                    sp.sem_clear(s)


def mm3(nc, out, lhs, rhs, start, stop):
    (ah, al), (bh, bl) = lhs, rhs
    nc.tensor.matmul(out, al, bh, start=start, stop=False)
    nc.tensor.matmul(out, ah, bl, start=False, stop=False)
    return nc.tensor.matmul(out, ah, bh, start=False, stop=stop)


def fold_layer1(nc, io, keep):
    WmT, Mv, cb, bn_scale, bn_shift = (keep[k] for k in ("WmT", "Mv", "cb", "bn_scale", "bn_shift"))
    ident = keep["ident"]
    with Scope(nc, "fold") as s:
        x_all = s.sb("x_all", [P, B * NT, C + 1])
        WaT = s.sb("WaT", [P, CT, QKV])
        AaT = s.sb("AaT", [LORA, C])
        Ba = s.sb("Ba", [LORA, QKV])
        ApT = s.sb("ApT", [LORA, C])
        Bp = s.sb("Bp", [LORA, C])
        Wp = s.sb("Wp", [P, CT, C])
        WpT = s.sb("WpT", [P, CT, C])
        WmpT = s.sb("WmpT", [P, CT, C])
        Wcomb = s.sb("Wcomb", [P, CT, C])
        WcombS = s.sb("WcombS", [P, CT, C])
        Wv = s.sb("Wv", [P, CT, C])
        G = s.sb("G", [P, CT, C + 1])
        prod = s.sb("prod", [P, CT, QKV])
        ones = s.sb("ones", [P, P])
        gamma = s.sb("gamma", [P, DT])
        beta = s.sb("beta", [P, DT])
        mean = s.sb("mean", [P, DT])
        ex2 = s.sb("ex2", [P, DT])
        msq = s.sb("msq", [P, DT])
        var = s.sb("var", [P, DT])
        nhalf = s.sb("nhalf", [P, DT])
        rstd = s.sb("rstd", [P, DT])
        shiftB = s.sb("shiftB", [P, CT, P])
        psL = [s.ps(f"psL{i}", [P, 1024]) for i in range(CT)]
        psM = s.ps("psM", [P, 512])
        psG = [s.ps(f"psG{i}", [P, 512]) for i in range(CT)]
        psX = s.ps("psX", [P, 512])

        x_in = [s.sem(f"x_in{n}") for n in range(B)]
        w_in, c_in, first_in = s.sem("w_in"), s.sem("c_in"), s.sem("first_in")
        consts = s.sem("consts")
        lora_a, lora_p, wm_done, wmp_done = (s.sem(n) for n in ("lora_a", "lora_p", "wm_done", "wmp_done"))
        comb_ps, comb_done, wvt_ps, wv_done = (s.sem(n) for n in ("comb_ps", "comb_done", "wvt_ps", "wv_done"))
        gram_ps, gram_done, h_ps, prod_done = (s.sem(n) for n in ("gram_ps", "gram_done", "h_ps", "prod_done"))
        stat_ps, stat, pow_done, fold_ps = (s.sem(n) for n in ("stat_ps", "stat", "pow_done", "fold_ps"))

        with nc.Block(no_gpsimd_drain=True) as block:
            @block.sync
            def _(sp):
                for b in range(B):
                    sp.dma_start(x_all[:, b * NT:(b + 1) * NT, 0:C],
                                 io["x"][b * T:(b + 1) * T, :].rearrange("(n p) c -> p n c", p=P)).then_inc(x_in[b], 16)
                    if b == 0:
                        sp.dma_start(AaT[:, :], io["AaT"]).then_inc(w_in, 16)
                        sp.dma_start(Ba[:, :], io["Ba"]).then_inc(w_in, 16)
                        sp.dma_start(WaT[:, :, :], io["WaT"].rearrange("(k p) d -> p k d", p=P)).then_inc(w_in, 16)
                sp.dma_start(keep["xT"][:, :, :], io["xT"][:, 0:T].rearrange("(k p) t -> p k t", p=P)).then_inc(first_in, 16)
                sp.dma_start(keep["maskf"][:, :], io["mask"]).then_inc(first_in, 16)
                sp.dma_start(keep["xs"][:, :, :], io["x"][0:T, :].rearrange("(n p) c -> p n c", p=P)).then_inc(keep["out_st"], 16)
                sp.wait_ge(first_in, 32)
                sp.wait_ge(keep["out_st"], 16)

            @block.scalar
            def _(act):
                act.dma_start(ApT[:, :], io["ApT"]).then_inc(c_in, 16)
                act.dma_start(Bp[:, :], io["Bp"]).then_inc(c_in, 16)
                act.dma_start(Wp[:, :, :], io["Wp"].rearrange("(k p) d -> p k d", p=P)).then_inc(c_in, 16)
                act.dma_start(WpT[:, :, :], io["WpT"].rearrange("(k p) d -> p k d", p=P)).then_inc(c_in, 16)
                act.dma_start(gamma[:, :], io["gamma"]).then_inc(c_in, 16)
                act.dma_start(beta[:, :], io["beta"]).then_inc(c_in, 16)
                act.dma_start(ident[:, :], io["ident"]).then_inc(c_in, 16)

            @block.gpsimd
            def _(pool):
                nc.gpsimd.memset(x_all[:, :, C:C + 1], 1.0).then_inc(consts, 1)
                nc.gpsimd.memset(ones[:, :], 1.0).then_inc(consts, 1)
                nc.gpsimd.memset(nhalf[:, :], -0.5).then_inc(consts, 1)
                pool.wait_ge(consts, 3)
                pool.wait_ge(stat, 4)
                nc.gpsimd.tensor_tensor(rstd[:, :], var[:, :], nhalf[:, :], ALU.pow).then_inc(pow_done, 1)

            @block.tensor
            def _(pe):
                def gram(b):
                    pe.wait_ge(x_in[b], 16)
                    for n in range(b * NT, (b + 1) * NT):
                        for k in range(CT):
                            last = nc.tensor.matmul(psG[k][:, 0:C + 1], x_all[:, n, k * P:(k + 1) * P],
                                                    x_all[:, n, :], start=(n == 0), stop=(n == B * NT - 1))
                    return last

                pe.wait_ge(consts, 1)
                gram(0)
                pe.wait_ge(w_in, 48)
                for k in range(CT):
                    for r in range(3):
                        last = nc.tensor.matmul(psL[k][:, r * C:(r + 1) * C],
                                                Ba[:, r * C + k * P:r * C + (k + 1) * P], AaT[:, :],
                                                start=True, stop=True)
                    last.then_inc(lora_a, 1)
                pe.wait_ge(c_in, 112)
                for k in range(CT):
                    last = nc.tensor.matmul(psM[:, k * C:(k + 1) * C], Bp[:, k * P:(k + 1) * P], ApT[:, :],
                                            start=True, stop=True)
                last.then_inc(lora_p, 1)
                gram(1)
                pe.wait_ge(wmp_done, 1)
                for d in range(CT):
                    for k in range(CT):
                        last = nc.tensor.matmul(psM[:, d * C:(d + 1) * C], Wp[:, k, d * P:(d + 1) * P],
                                                WmpT[:, k, :], start=(k == 0), stop=(k == CT - 1))
                last.then_inc(comb_ps, 1)
                gram(2)
                pe.wait_ge(wm_done, 2)
                for d in range(CT):
                    for k in range(CT):
                        last = nc.tensor.transpose(psX[:, d * C + k * P:d * C + (k + 1) * P],
                                                   WmT[:, k, 2 * C + d * P:2 * C + (d + 1) * P], ident[:, :])
                last.then_inc(wvt_ps, 1)
                gram(3).then_inc(gram_ps, 1)
                pe.wait_ge(gram_done, 1)
                for c in range(CT):
                    for lo, hi in ((0, 512), (512, QKV)):
                        for k in range(CT):
                            last = nc.tensor.matmul(psL[c][:, lo:hi], G[:, k, c * P:(c + 1) * P],
                                                    WmT[:, k, lo:hi], start=(k == 0), stop=(k == CT - 1))
                    last.then_inc(h_ps, 1)
                pe.wait_ge(prod_done, 2)
                pe.wait_ge(consts, 2)
                for d in range(DT):
                    for k in range(CT):
                        nc.tensor.matmul(psG[0][:, d:d + 1], prod[:, k, d * P:(d + 1) * P], ones[:, 0:1],
                                         start=(k == 0), stop=(k == CT - 1))
                for d in range(DT):
                    for k in range(CT):
                        last = nc.tensor.matmul(psG[0][:, DT + d:DT + d + 1], WmT[:, k, d * P:(d + 1) * P],
                                                G[:, k, C:C + 1], start=(k == 0), stop=(k == CT - 1))
                last.then_inc(stat_ps, 1)
                pe.wait_ge(stat, 8)
                for c in range(CT):
                    for k in range(CT):
                        last = nc.tensor.matmul(psM[:, c * C:(c + 1) * C], Wv[:, k, c * P:(c + 1) * P],
                                                WcombS[:, k, :], start=(k == 0), stop=(k == CT - 1))
                for k in range(CT):
                    last = nc.tensor.matmul(psX[:, 0:C], shiftB[:, k, :], Wcomb[:, k, :],
                                            start=(k == 0), stop=(k == CT - 1))
                last.then_inc(fold_ps, 1)

            @block.vector
            def _(dve):
                dve.wait_ge(w_in, 48)
                for k in range(CT):
                    dve.wait_ge(lora_a, k + 1)
                    nc.vector.tensor_tensor(
                        WmT[:, k, :].rearrange("p (i r) -> p i r", r=3),
                        WaT[:, k, :].rearrange("p (i r) -> p i r", r=3),
                        psL[k][:, 0:QKV].rearrange("p (r i) -> p i r", r=3), ALU.add).then_inc(wm_done, 1)
                dve.wait_ge(c_in, 112)
                dve.wait_ge(lora_p, 1)
                nc.vector.tensor_tensor(WmpT[:, :, :], WpT[:, :, :],
                                        psM[:, :].rearrange("p (k e) -> p k e", k=CT), ALU.add).then_inc(wmp_done, 1)
                dve.wait_ge(comb_ps, 1)
                nc.vector.tensor_copy(Wcomb[:, :, :], psM[:, :].rearrange("p (k e) -> p k e", k=CT)).then_inc(comb_done, 1)
                dve.wait_ge(wvt_ps, 1)
                nc.vector.tensor_copy(Wv[:, :, :], psX[:, :].rearrange("p (k e) -> p k e", k=CT)).then_inc(wv_done, 1)
                dve.wait_ge(gram_ps, 1)
                nc.vector.tensor_copy(G[:, 0, :], psG[0][:, 0:C + 1])
                nc.vector.tensor_copy(G[:, 1, :], psG[1][:, 0:C + 1]).then_inc(gram_done, 1)
                for c in range(CT):
                    dve.wait_ge(h_ps, c + 1)
                    nc.vector.tensor_tensor(prod[:, c, :], WmT[:, c, :], psL[c][:, 0:QKV], ALU.mult).then_inc(prod_done, 1)
                dve.wait_ge(stat_ps, 1)
                nc.vector.tensor_scalar(ex2[:, :], psG[0][:, 0:DT], 1.0 / TOKENS, EPS, ALU.mult, ALU.add).then_inc(stat, 1)
                nc.vector.tensor_scalar(mean[:, :], psG[0][:, DT:2 * DT], 1.0 / TOKENS, None, ALU.mult).then_inc(stat, 1)
                dve.wait_ge(stat, 2)
                nc.vector.tensor_tensor(msq[:, :], mean[:, :], mean[:, :], ALU.mult).then_inc(stat, 1)
                dve.wait_ge(stat, 3)
                nc.vector.tensor_tensor(var[:, :], ex2[:, :], msq[:, :], ALU.subtract).then_inc(stat, 1)
                dve.wait_ge(pow_done, 1)
                nc.vector.tensor_tensor(bn_scale[:, :], gamma[:, :], rstd[:, :], ALU.mult).then_inc(stat, 1)
                dve.wait_ge(stat, 5)
                nc.vector.tensor_tensor(msq[:, :], mean[:, :], bn_scale[:, :], ALU.mult).then_inc(stat, 1)
                dve.wait_ge(stat, 6)
                nc.vector.tensor_tensor(bn_shift[:, :], beta[:, :], msq[:, :], ALU.subtract).then_inc(stat, 1)
                dve.wait_ge(stat, 7)
                dve.wait_ge(comb_done, 1)
                for k in range(CT):
                    nc.vector.tensor_scalar(WcombS[:, k, :], Wcomb[:, k, :], bn_scale[:, 4 + k:5 + k], None, ALU.mult)
                    last = nc.vector.tensor_scalar(shiftB[:, k, :], ones[:, :], bn_shift[:, 4 + k:5 + k], None, ALU.mult)
                last.then_inc(stat, 1)
                dve.wait_ge(stat, 8)
                nc.vector.tensor_scalar(bn_scale[:, 0:CT], bn_scale[:, 0:CT], SCALE1, None, ALU.mult)
                nc.vector.tensor_scalar(bn_shift[:, 0:CT], bn_shift[:, 0:CT], SCALE1, None, ALU.mult)
                dve.wait_ge(fold_ps, 1)
                nc.vector.tensor_copy(Mv[:, :, :], psM[:, :].rearrange("p (k e) -> p k e", k=CT))
                nc.vector.tensor_copy(cb[:, :], psX[:, 0:C])
        s.clear()


def layer1(nc, io, x_next):
    with Scope(nc, "keep1") as keep:
        k = dict(WmT=keep.sb("WmT", [P, CT, QKV]), Mv=keep.sb("Mv", [P, CT, C]), cb=keep.sb("cb", [P, C]),
                 bn_scale=keep.sb("bn_scale", [P, DT]), bn_shift=keep.sb("bn_shift", [P, DT]),
                 ident=keep.sb("ident", [P, P]), xT=keep.sb("xT", [P, CT, T]), maskf=keep.sb("maskf", [P, P]),
                 xs=keep.sb("xs", [P, NT, C]),
                 out_st=keep.sem("out_st"))
        fold_layer1(nc, io, k)
        WmT, Mv, cb, bn_scale, bn_shift, ident = (k[n] for n in ("WmT", "Mv", "cb", "bn_scale", "bn_shift", "ident"))
        xT, maskf, xs, out_st = (k[n] for n in ("xT", "maskf", "xs", "out_st"))
        with Scope(nc, "attn1") as s:
            xn = s.sb("xn", [P, NT, C])
            Wqk = [s.sb(f"Wqk{i}", [P, CT, 2 * C], F32R) for i in range(2)]
            Mvs = [s.sb(f"Mv{i}", [P, CT, C], F32R) for i in range(2)]
            x = [s.sb(f"x{i}", [P, CT, T], F32R) for i in range(2)]
            q = [s.sb(f"q{i}", [P, CT, T], F32R) for i in range(2)]
            kk = [s.sb(f"k{i}", [P, CT, T], F32R) for i in range(2)]
            V = [s.sb(f"V{i}", [P, NT, C], F32R) for i in range(2)]
            probT = [s.sb(f"probT{i}", [P, 2, T], F32R) for i in range(2)]
            qk_whole = s.sb("qk_whole", [P, 2, CHUNK])
            v_whole = s.sb("v_whole", [P, 2, C])
            prob = s.sb("prob", [P, 2, T])
            y = s.sb("y", [P, NT, C])
            stats = s.sb("stats", [P, NT, 6])
            mv = s.sb("mv", [P, NT, 2])
            veps = s.sb("veps", [P, NT])
            rstd = s.sb("rstd", [P, NT])
            nmax = s.sb("nmax", [P, NT])
            rsum = s.sb("rsum", [P, NT])
            rinv = s.sb("rinv", [P, NT])
            nhalf = s.sb("nhalf", [P, 1])
            identb = s.sb("identb", [P, P], BF16)
            maskb = s.sb("maskb", [P, P], BF16)
            psS = [s.ps(f"psS{i}", [P, 1024]) for i in range(2)]
            psT = [s.ps(f"psT{i}", [P, 512]) for i in range(2)]
            psO = [s.ps(f"psO{i}", [P, 512]) for i in range(2)]

            next_in, kept, consts = s.sem("next_in"), s.sem("kept"), s.sem("consts")
            w_hi, x_hi, x_lo = s.sem("w_hi"), s.sem("x_hi"), s.sem("x_lo")
            qk_ps, qk_hi, qk_read, qk_lo = s.sem("qk_ps"), s.sem("qk_hi"), s.sem("qk_read"), s.sem("qk_lo")
            v_ps, v_read, v_hi, v_lo = s.sem("v_ps"), s.sem("v_read"), s.sem("v_hi"), s.sem("v_lo")
            s_ps, max_done, exp_done = s.sem("s_ps"), s.sem("max_done"), s.sem("exp_done")
            t_ps, t_hi, t_done, o_ps, y_done = s.sem("t_ps"), s.sem("t_hi"), s.sem("t_done"), s.sem("o_ps"), s.sem("y_done")
            rinv_done, st_done, veps_done, rstd_done, ln_done = (
                s.sem(n) for n in ("rinv_done", "st_done", "veps_done", "rstd_done", "ln_done"))

            groups = []
            for t in range(NT):
                for g in range(0, t + 1, 4):
                    groups.append((t, g, min(4, t + 1 - g)))
            first_group = {t: min(i for i, g in enumerate(groups) if g[0] == t) for t in range(NT)}
            last_group = {t: max(i for i, g in enumerate(groups) if g[0] == t) for t in range(NT)}

            with nc.Block(no_gpsimd_drain=True) as block:
                @block.scalar
                def _(act):
                    nc.scalar.activation(identb[:, :], ident[:, :], ACT.Copy)
                    nc.scalar.activation(maskb[:, :], maskf[:, :], ACT.Copy)
                    nc.scalar.activation(Mvs[0][:, :, :], Mv[:, :, :], ACT.Copy).then_inc(w_hi, 1)
                    nc.scalar.activation(Wqk[0][:, :, :], WmT[:, :, 0:2 * C], ACT.Copy).then_inc(w_hi, 1)

                @block.vector
                def _(dve):
                    dve.wait_ge(w_hi, 1)
                    nc.vector.tensor_tensor(Mvs[1][:, :, :], Mv[:, :, :], Mvs[0][:, :, :].bitcast(F32), ALU.subtract)
                    dve.wait_ge(w_hi, 2)
                    nc.vector.tensor_tensor(Wqk[1][:, :, :], WmT[:, :, 0:2 * C], Wqk[0][:, :, :].bitcast(F32), ALU.subtract)

                @block.gpsimd
                def _(pool):
                    nc.gpsimd.memset(nhalf[:, :], -0.5).then_inc(consts, 1)
                    pool.wait_ge(consts, 1)
            s.clear()

            projections = [(c, d) for c in range(CHUNKS) for d in range(2 * CT)]

            def qk_bank(n):
                return psS[n // 2 % 2][:, (n % 2) * 512:(n % 2) * 512 + 512]

            with nc.Fori(0, B) as b:
                with nc.Block(no_gpsimd_drain=True) as block:
                    @block.sync
                    def _(sp):
                        sp.wait_ge(kept, 1)
                        sp.dma_start(xs[:, :, :], io["x"][bass.ts((b + 1) % B, T), :].rearrange("(n p) c -> p n c", p=P)).then_inc(next_in, 16)
                        sp.wait_ge(x_lo, CHUNKS * CT)
                        sp.dma_start(xT[:, :, :], io["xT"][:, bass.ts((b + 1) % B, T)].rearrange("(k p) t -> p k t", p=P)).then_inc(next_in, 16)
                        for c in range(CHUNKS):
                            sp.wait_ge(ln_done, (c + 1) * TPC)
                            sp.dma_start(x_next[bass.ds(b * T + c * CHUNK, CHUNK), :].rearrange("(n p) c -> p n c", p=P),
                                         y[:, c * TPC:(c + 1) * TPC, :]).then_inc(out_st, 16)
                        sp.wait_ge(next_in, 32)

                    @block.tensor
                    def _(pe):
                        for n, (c, d) in enumerate(projections):
                            pe.wait_ge(x_lo, CT * (c + 1))
                            if n >= 4:
                                pe.wait_ge(qk_read, n - 3)
                            for k in range(CT):
                                last = mm3(nc, qk_bank(n), [z[:, k, d * P:(d + 1) * P] for z in Wqk],
                                           [z[:, k, c * CHUNK:(c + 1) * CHUNK] for z in x], k == 0, k == CT - 1)
                            last.then_inc(qk_ps, 1)
                        for t in range(NT):
                            if t >= 2:
                                pe.wait_ge(v_read, t - 1)
                            for k in range(CT):
                                last = mm3(nc, psO[t % 2][:, 0:C], [z[:, k, t * P:(t + 1) * P] for z in x],
                                           [z[:, k, :] for z in Mvs], k == 0, k == CT - 1)
                            last.then_inc(v_ps, 1)
                        pe.wait_ge(qk_lo, len(projections))

                        def scores(t):
                            if t >= 2:
                                pe.wait_ge(exp_done, t - 1)
                            for c in range(0, (t + 1) * P, 512):
                                w = min(512, (t + 1) * P - c)
                                diag = c + w == (t + 1) * P
                                for k in range(CT):
                                    last = mm3(nc, psS[t % 2][:, c:c + w], [z[:, k, t * P:(t + 1) * P] for z in q],
                                               [z[:, k, c:c + w] for z in kk], k == 0, k == CT - 1 and not diag)
                                if diag:
                                    last = nc.tensor.matmul(psS[t % 2][:, t * P:(t + 1) * P], identb[:, :], maskb[:, :],
                                                            start=False, stop=True)
                            last.then_inc(s_ps, 1)

                        def transposed(t):
                            pe.wait_ge(exp_done, t + 1)
                            for i in range(first_group[t], last_group[t] + 1):
                                _, g, n = groups[i]
                                if i >= 2:
                                    pe.wait_ge(t_done, i - 1)
                                for j in range(n):
                                    last = nc.tensor.transpose(psT[i % 2][:, j * P:(j + 1) * P],
                                                               prob[:, t % 2, (g + j) * P:(g + j + 1) * P], ident[:, :])
                                last.then_inc(t_ps, 1)

                        def weighted(t):
                            pe.wait_ge(t_done, last_group[t] + 1)
                            if t == 0:
                                pe.wait_ge(v_lo, NT)
                            if t >= 2:
                                pe.wait_ge(y_done, t - 1)
                            for j in range(t + 1):
                                last = mm3(nc, psO[t % 2][:, 0:C], [z[:, t % 2, j * P:(j + 1) * P] for z in probT],
                                           [z[:, j, :] for z in V], j == 0, j == t)
                            last.then_inc(o_ps, 1)

                        scores(0)
                        scores(1)
                        for t in range(NT):
                            transposed(t)
                            if t + 2 < NT:
                                scores(t + 2)
                            weighted(t)

                    @block.scalar
                    def _(act):
                        for c in range(CHUNKS):
                            for k in range(CT):
                                nc.scalar.activation(x[0][:, k, c * CHUNK:(c + 1) * CHUNK], xT[:, k, c * CHUNK:(c + 1) * CHUNK],
                                                     ACT.Copy).then_inc(x_hi, 1)
                        for n, (c, d) in enumerate(projections):
                            act.wait_ge(qk_ps, n + 1)
                            dst = q if d < CT else kk
                            nc.scalar.activation(dst[0][:, d % CT, c * CHUNK:(c + 1) * CHUNK], qk_bank(n), ACT.Identity,
                                                 bias=bn_shift[:, d:d + 1], scale=bn_scale[:, d:d + 1]).then_inc(qk_hi, 1)
                        for t in range(NT):
                            act.wait_ge(v_read, t + 1)
                            nc.scalar.activation(V[0][:, t, :], v_whole[:, t % 2, :], ACT.Copy).then_inc(v_hi, 1)

                        def softmax(t):
                            act.wait_ge(max_done, t + 1)
                            if t >= 2:
                                act.wait_ge(t_ps, last_group[t - 2] + 1)
                            nc.scalar.activation(prob[:, t % 2, 0:(t + 1) * P], psS[t % 2][:, 0:(t + 1) * P], ACT.Exp,
                                                 bias=nmax[:, t:t + 1], accum_out=rsum[:, t:t + 1]).then_inc(exp_done, 1)

                        softmax(0)
                        softmax(1)
                        for t in range(NT):
                            for i in range(first_group[t], last_group[t] + 1):
                                _, g, n = groups[i]
                                act.wait_ge(t_ps, i + 1)
                                if t >= 2:
                                    act.wait_ge(o_ps, t - 1)
                                nc.scalar.activation(probT[0][:, t % 2, g * P:(g + n) * P], psT[i % 2][:, 0:n * P], ACT.Copy).then_inc(t_hi, 1)
                            if t + 2 < NT:
                                softmax(t + 2)

                    @block.gpsimd
                    def _(pool):
                        nc.gpsimd.tensor_copy(xn[:, :, :], xs[:, :, :]).then_inc(kept, 1)
                        for t in range(NT):
                            pool.wait_ge(veps_done, t + 1)
                            nc.gpsimd.tensor_tensor(rstd[:, t:t + 1], veps[:, t:t + 1], nhalf[:, :], ALU.pow).then_inc(rstd_done, 1)

                    @block.vector
                    def _(dve):
                        for i, (c, k) in enumerate((c, k) for c in range(CHUNKS) for k in range(CT)):
                            cols = slice(c * CHUNK, (c + 1) * CHUNK)
                            dve.wait_ge(x_hi, i + 1)
                            nc.vector.tensor_tensor(x[1][:, k, cols], xT[:, k, cols], x[0][:, k, cols].bitcast(F32),
                                                    ALU.subtract).then_inc(x_lo, 1)
                        for n in range(len(projections) + 1):
                            if n < len(projections):
                                c, d = projections[n]
                                dve.wait_ge(qk_hi, n + 1)
                                if n >= 2:
                                    dve.wait_ge(qk_lo, n - 1)
                                nc.vector.tensor_scalar(qk_whole[:, n % 2, :], qk_bank(n), bn_scale[:, d:d + 1], bn_shift[:, d:d + 1],
                                                        ALU.mult, ALU.add).then_inc(qk_read, 1)
                            if n >= 1:
                                c, d = projections[n - 1]
                                hi, lo = [z[:, d % CT, c * CHUNK:(c + 1) * CHUNK] for z in (q if d < CT else kk)]
                                dve.wait_ge(qk_read, n)
                                nc.vector.tensor_tensor(lo, qk_whole[:, (n - 1) % 2, :], hi.bitcast(F32), ALU.subtract).then_inc(qk_lo, 1)
                        for t in range(NT + 1):
                            if t < NT:
                                dve.wait_ge(v_ps, t + 1)
                                if t >= 2:
                                    dve.wait_ge(v_lo, t - 1)
                                nc.vector.tensor_tensor(v_whole[:, t % 2, :], psO[t % 2][:, 0:C], cb[:, :], ALU.add).then_inc(v_read, 1)
                            if t >= 1:
                                dve.wait_ge(v_hi, t)
                                nc.vector.tensor_tensor(V[1][:, t - 1, :], v_whole[:, (t - 1) % 2, :], V[0][:, t - 1, :].bitcast(F32),
                                                        ALU.subtract).then_inc(v_lo, 1)
                        dve.wait_ge(kept, 1)
                        dve.wait_ge(out_st, b * (16 * CHUNKS) + 16)

                        def row_max(t):
                            dve.wait_ge(s_ps, t + 1)
                            nc.vector.tensor_reduce(nmax[:, t:t + 1], psS[t % 2][:, 0:(t + 1) * P], X, ALU.max,
                                                    negate=True).then_inc(max_done, 1)

                        def normalise(t):
                            dve.wait_ge(rstd_done, t + 1)
                            nc.vector.tensor_scalar(y[:, t, :], y[:, t, :], mv[:, t, 0:1], rstd[:, t:t + 1],
                                                    ALU.subtract, ALU.mult).then_inc(ln_done, 1)

                        row_max(0)
                        row_max(1)
                        for t in range(NT):
                            for i in range(first_group[t], last_group[t] + 1):
                                _, g, n = groups[i]
                                dve.wait_ge(t_hi, i + 1)
                                cols = slice(g * P, (g + n) * P)
                                nc.vector.tensor_tensor(probT[1][:, t % 2, cols], psT[i % 2][:, 0:n * P], probT[0][:, t % 2, cols].bitcast(F32),
                                                        ALU.subtract).then_inc(t_done, 1)
                            if t + 2 < NT:
                                row_max(t + 2)
                            if t >= 1:
                                normalise(t - 1)
                            dve.wait_ge(exp_done, t + 1)
                            nc.vector.reciprocal(rinv[:, t:t + 1], rsum[:, t:t + 1]).then_inc(rinv_done, 1)
                            dve.wait_ge(rinv_done, t + 1)
                            dve.wait_ge(o_ps, t + 1)
                            nc.vector.scalar_tensor_tensor(out=y[:, t, :], in0=psO[t % 2][:, 0:C], scalar=rinv[:, t:t + 1],
                                                           in1=xn[:, t, :], op0=ALU.mult, op1=ALU.add).then_inc(y_done, 1)
                            dve.wait_ge(y_done, t + 1)
                            nc.vector.bn_stats(stats[:, t, :], y[:, t, :]).then_inc(st_done, 1)
                            dve.wait_ge(st_done, 2 * t + 1)
                            nc.vector.bn_aggr(mv[:, t, :], stats[:, t, :]).then_inc(st_done, 1)
                            dve.wait_ge(st_done, 2 * t + 2)
                            nc.vector.tensor_scalar(veps[:, t:t + 1], mv[:, t, 1:2], EPS, None, ALU.add).then_inc(veps_done, 1)
                        normalise(NT - 1)
                s.clear()
            with nc.Block(no_gpsimd_drain=True) as block:
                @block.sync
                def _(sp):
                    sp.wait_ge(out_st, B * (16 * CHUNKS) + 16)


def keys_and_values2(nc, io, w, x_prev, out_st):
    Wq, K, V, Wout = w["Wq"], w["K"], w["V"], w["Wout"]
    with Scope(nc, "keys2") as s:
        ctxT = s.sb("ctxT", [KP2, KT2, J])
        Wk = s.sb("Wk", [KP2, KT2, INNER])
        Wv = s.sb("Wv", [KP2, KT2, INNER])
        Wqf = s.sb("Wqf", [P, CT, INNER])
        kf = s.sb("kf", [P, 2, J])
        ksum = s.sb("ksum", [P, H2])
        kb = s.sb("kb", [P, H2])
        psK = [s.ps(f"psK{i}", [P, 2, 512]) for i in range(2)]
        psV = [s.ps(f"psV{i}", [P, 512]) for i in range(2)]
        c_in, v_in, q_in, w_in, consts = s.sem("c_in"), s.sem("v_in"), s.sem("q_in"), s.sem("w_in"), s.sem("consts")
        k_ps, k_sum, kb_done, k_done = s.sem("k_ps"), s.sem("k_sum"), s.sem("kb_done"), s.sem("k_done")
        q_hi, v_ps, v_hi, v_lo = s.sem("q_hi"), s.sem("v_ps"), s.sem("v_hi"), s.sem("v_lo")
        pieces = [(j, min(P, J - j * P), n) for j in range(JT) for n in range(INNER // 512)]

        with nc.Block(no_gpsimd_drain=True) as block:
            @block.sync
            def _(sp):
                sp.dma_start(ctxT[:, :, :], io["ctxT"].rearrange("(k p) j -> p k j", p=KP2)).then_inc(c_in, 16)
                sp.dma_start(Wk[:, :, :], io["Wk2"].rearrange("(k p) d -> p k d", p=KP2)).then_inc(c_in, 16)
                sp.dma_start(Wv[:, :, :], io["Wv2"].rearrange("(k p) d -> p k d", p=KP2)).then_inc(v_in, 16)
                sp.dma_start(Wqf[:, :, :], io["Wq2"].rearrange("(k p) d -> p k d", p=P)).then_inc(q_in, 16)
                sp.dma_start(Wout[:, :, :], io["Wout"].rearrange("(h p) e -> p h e", p=P)).then_inc(w_in, 16)
                sp.dma_start(w["bout"][:, :], io["bout"].partition_broadcast(P)).then_inc(out_st, 16)
                sp.dma_start(w["xs"][:, :, :], x_prev[0:T, :].rearrange("(n p) c -> p n c", p=P)).then_inc(w_in, 16)
                sp.dma_start(w["ident"][:, :], io["ident"]).then_inc(w_in, 16)
                sp.wait_ge(w_in, 48)
                sp.wait_ge(out_st, 16)

            @block.gpsimd
            def _(pool):
                nc.gpsimd.memset(w["nhalf"][:, :], -0.5).then_inc(consts, 1)
                pool.wait_ge(consts, 1)

            @block.tensor
            def _(pe):
                pe.wait_ge(c_in, 32)
                for h in range(H2):
                    if h >= 2:
                        pe.wait_ge(k_sum, h - 1)
                    for a in range(2):
                        for k in range(KT2):
                            last = nc.tensor.matmul(psK[h % 2][:, a, 0:JH], Wk[:, k, h * D2:(h + 1) * D2],
                                                    ctxT[:, k, a * JH:(a + 1) * JH], start=(k == 0), stop=(k == KT2 - 1))
                    last.then_inc(k_ps, 1)
                pe.wait_ge(v_in, 16)
                for i, (j, rows, n) in enumerate(pieces):
                    if i >= 2:
                        pe.wait_ge(v_lo, i - 1)
                    for k in range(KT2):
                        last = nc.tensor.matmul(psV[i % 2][0:rows, :], ctxT[:, k, j * P:j * P + rows],
                                                Wv[:, k, n * 512:(n + 1) * 512], start=(k == 0), stop=(k == KT2 - 1))
                    last.then_inc(v_ps, 1)

            @block.scalar
            def _(act):
                for h in range(H2):
                    act.wait_ge(k_ps, h + 1)
                    if h >= 2:
                        act.wait_ge(k_done, 3 * (h - 1))
                    nc.scalar.activation(kf[:, h % 2, :].rearrange("p (a w) -> p a w", a=2), psK[h % 2][:, :, 0:JH],
                                         ACT.Copy, accum_out=ksum[:, h:h + 1]).then_inc(k_sum, 1)
                act.wait_ge(q_in, 16)
                nc.scalar.activation(Wq[0][:, :, :], Wqf[:, :, :], ACT.Copy).then_inc(q_hi, 1)
                for i, (j, rows, n) in enumerate(pieces):
                    act.wait_ge(v_ps, i + 1)
                    nc.scalar.activation(V[0][0:rows, j, n * 512:(n + 1) * 512], psV[i % 2][0:rows, :], ACT.Copy).then_inc(v_hi, 1)

            @block.vector
            def _(dve):
                for h in range(H2):
                    dve.wait_ge(k_sum, h + 1)
                    nc.vector.tensor_scalar(kb[:, h:h + 1], ksum[:, h:h + 1], (1.0 - SHARPEN) * SCALE2 / J, None,
                                            ALU.mult).then_inc(kb_done, 1)
                    dve.wait_ge(kb_done, h + 1)
                    nc.vector.tensor_scalar(kf[:, h % 2, :], kf[:, h % 2, :], SHARPEN * SCALE2, kb[:, h:h + 1],
                                            ALU.mult, ALU.add).then_inc(k_done, 1)
                    dve.wait_ge(k_done, 3 * h + 1)
                    nc.vector.tensor_copy(K[0][:, h, :], kf[:, h % 2, :]).then_inc(k_done, 1)
                    dve.wait_ge(k_done, 3 * h + 2)
                    nc.vector.tensor_tensor(K[1][:, h, :], kf[:, h % 2, :], K[0][:, h, :].bitcast(F32),
                                            ALU.subtract).then_inc(k_done, 1)
                dve.wait_ge(q_hi, 1)
                nc.vector.tensor_tensor(Wq[1][:, :, :], Wqf[:, :, :], Wq[0][:, :, :].bitcast(F32), ALU.subtract)
                for i, (j, rows, n) in enumerate(pieces):
                    dve.wait_ge(v_hi, i + 1)
                    nc.vector.tensor_tensor(V[1][0:rows, j, n * 512:(n + 1) * 512], psV[i % 2][0:rows, :],
                                            V[0][0:rows, j, n * 512:(n + 1) * 512].bitcast(F32), ALU.subtract).then_inc(v_lo, 1)
        s.clear()


RING, PT_RING = 3, 4
OUT_RING = 12
UNITS = CHUNKS * H2


def tensor_order2():
    order = [("x", c, k) for c in range(CHUNKS) for k in range(CT)]
    for s in range(-2, UNITS + 2):
        step = [("q", s + 2, 0), ("pv", s - 1, 1), ("s", s + 1, 2), ("s", s + 1, 3), ("p", s, 0), ("pv", s - 1, 2),
                ("p", s, 1), ("pv", s - 1, 3), ("p", s, 2), ("pv", s - 1, 4), ("p", s, 3), ("s", s + 2, 0), ("p", s, 4),
                ("s", s + 2, 1), ("pv", s, 0)]
        for what, u, part in step:
            if 0 <= u < UNITS:
                order.append((what, u, part))
                if what == "s" and u >= H2 + 3 and u % H2 == 3:
                    order.append(("y", u // H2 - 1, part))
    return order + [("y", CHUNKS - 1, t) for t in range(TPC)]


def layer2(nc, io, x_prev, x_next):
    with Scope(nc, "keep2") as keep:
        w = dict(Wq=[keep.sb(f"Wq{i}", [P, CT, INNER], F32R) for i in range(2)],
                 K=[keep.sb(f"K{i}", [P, H2, J], F32R) for i in range(2)],
                 V=[keep.sb(f"V{i}", [P, JT, INNER], F32R) for i in range(2)],
                 Wout=keep.sb("Wout", [P, H2, C]), bout=keep.sb("bout", [P, C]), ident=keep.sb("ident", [P, P]),
                 nhalf=keep.sb("nhalf", [P, 1]), xs=keep.sb("xs", [P, NT, C]))
        out_st = keep.sem("out_st")
        keys_and_values2(nc, io, w, x_prev, out_st)
        xs = w["xs"]
        Wq, K, V, Wout, ident = w["Wq"], w["K"], w["V"], w["Wout"], w["ident"]
        with Scope(nc, "attn2") as s:
            xn = s.sb("xn", [P, NT, C])
            xT = [s.sb(f"xT{i}", [P, CT, T], F32R) for i in range(2)]
            q = [s.sb(f"q{i}", [P, 2, CHUNK], F32R) for i in range(2)]
            prob = s.sb("prob", [P, 2 * TPC, J])
            pT = [s.sb(f"pT{i}", [P, PT_RING, CHUNK], F32R) for i in range(2)]
            outT = s.sb("outT", [P, OUT_RING, CHUNK])
            y = xn
            NS = CHUNKS * H2 * TPC
            nmax = s.sb("nmax", [P, NS])
            rsum = s.sb("rsum", [P, NS])
            rinv = s.sb("rinv", [P, NS])
            stats = s.sb("stats", [P, NT, 6])
            mv = s.sb("mv", [P, NT, 2])
            veps = s.sb("veps", [P, NT])
            rstd = s.sb("rstd", [P, NT])
            psS = [s.ps(f"psS{i}", [P, 2, 512]) for i in range(2)]
            ring = [s.ps(f"ring{i}", [P, 512]) for i in range(RING)]
            psO = s.ps("psO", [P, 512])

            next_in, xb_done = s.sem("next_in"), s.sem("xb_done")
            q_ps, q_hi, q_lo = s.sem("q_ps"), s.sem("q_hi"), s.sem("q_lo")
            s_ps, max_done, exp_done, rinv_done, norm_done = (
                s.sem(n) for n in ("s_ps", "max_done", "exp_done", "rinv_done", "norm_done"))
            x_ps, x_hi, x_lo = s.sem("x_ps"), s.sem("x_hi"), s.sem("x_lo")
            p_ps, p_hi, p_lo = s.sem("p_ps"), s.sem("p_hi"), s.sem("p_lo")
            y_ps = s.sem("y_ps")
            pv_ps, o_done = s.sem("pv_ps"), s.sem("o_done")
            y_done, st_done, veps_done, rstd_done, ln_done = (
                s.sem(n) for n in ("y_done", "st_done", "veps_done", "rstd_done", "ln_done"))

            order = tensor_order2()
            slots = [o for o in order if o[0] in "xqpy"]
            at = {o: i for i, o in enumerate(slots)}

            def score_tile(u, t):
                return TPC * u + t

            def block(u, j):
                return JT * u + j

            with nc.Fori(0, B) as b:
                with nc.Block(no_gpsimd_drain=True) as blk:
                    @blk.sync
                    def _(sp):
                        sp.wait_ge(x_ps, CHUNKS * CT)
                        sp.wait_ge(xb_done, NT)
                        sp.dma_start(xs[:, :, :], x_prev[bass.ts((b + 1) % B, T), :].rearrange("(n p) c -> p n c", p=P)).then_inc(next_in, 16)
                        sp.wait_ge(next_in, 16)
                        for c in range(CHUNKS):
                            sp.wait_ge(ln_done, (c + 1) * TPC)
                            sp.dma_start(x_next[bass.ds(b * T + c * CHUNK, CHUNK), :].rearrange("(n p) c -> p n c", p=P),
                                         y[:, c * TPC:(c + 1) * TPC, :]).then_inc(out_st, 16)

                    @blk.gpsimd
                    def _(pool):
                        pool.wait_ge(out_st, b * (16 * CHUNKS) + 16)
                        for t in range(NT):
                            nc.gpsimd.tensor_tensor(xn[:, t, :], xs[:, t, :], w["bout"][:, :], ALU.add).then_inc(xb_done, 1)
                        for t in range(NT):
                            pool.wait_ge(veps_done, t + 1)
                            nc.gpsimd.tensor_tensor(rstd[:, t:t + 1], veps[:, t:t + 1], w["nhalf"][:, :], ALU.pow).then_inc(rstd_done, 1)

                    @blk.tensor
                    def _(pe):
                        def take(what, u, part):
                            i = at[what, u, part]
                            if i >= RING:
                                was, v, piece = slots[i - RING]
                                if was == "x":
                                    pe.wait_ge(x_lo, CT * v + piece + 1)
                                elif was == "q":
                                    pe.wait_ge(q_lo, v + 1)
                                elif was == "p":
                                    pe.wait_ge(p_lo, block(v, piece) + 1)
                                else:
                                    pe.wait_ge(y_done, TPC * v + piece + 1)
                            return ring[i % RING]

                        def transpose_x(c, k):
                            bank = take("x", c, k)
                            for t in range(TPC):
                                last = nc.tensor.transpose(bank[:, t * P:(t + 1) * P], xs[:, c * TPC + t, k * P:(k + 1) * P], ident[:, :])
                            last.then_inc(x_ps, 1)

                        def project_q(u, _):
                            c, h = divmod(u, H2)
                            bank = take("q", u, 0)
                            pe.wait_ge(x_lo, CT * (c + 1))
                            for k in range(CT):
                                last = mm3(nc, bank[:, :], [a[:, k, h * D2:(h + 1) * D2] for a in Wq],
                                           [a[:, k, c * CHUNK:(c + 1) * CHUNK] for a in xT], k == 0, k == CT - 1)
                            last.then_inc(q_ps, 1)

                        def scores(u, t):
                            n = score_tile(u, t)
                            pe.wait_ge(q_lo, u + 1)
                            if n >= 2:
                                pe.wait_ge(exp_done, n - 1)
                            for a in range(2):
                                last = mm3(nc, psS[n % 2][:, a, 0:JH], [z[:, u % 2, t * P:(t + 1) * P] for z in q],
                                           [z[:, u % H2, a * JH:(a + 1) * JH] for z in K], True, True)
                            last.then_inc(s_ps, 1)

                        def transpose_p(u, j):
                            rows = min(P, J - j * P)
                            bank = take("p", u, j)
                            pe.wait_ge(norm_done, score_tile(u + 1, 0))
                            for t in range(TPC):
                                last = nc.tensor.transpose(bank[0:rows, t * P:(t + 1) * P],
                                                           prob[:, u % 2 * TPC + t, j * P:j * P + rows], ident[:, :])
                            last.then_inc(p_ps, 1)

                        def weighted(u, j):
                            rows, h = min(P, J - j * P), u % H2
                            pe.wait_ge(p_lo, block(u, j) + 1)
                            if j == 0 and u >= 1:
                                pe.wait_ge(o_done, u)
                            mm3(nc, psO[:, :], [z[0:rows, j, h * D2:(h + 1) * D2] for z in V],
                                [z[0:rows, block(u, j) % PT_RING, :] for z in pT], j == 0, j == JT - 1).then_inc(pv_ps, 1)

                        def project_out(c, t):
                            bank = take("y", c, t)
                            pe.wait_ge(o_done, (c + 1) * H2)
                            for h in range(H2):
                                last = nc.tensor.matmul(bank[:, 0:C], outT[:, (c * H2 + h) % OUT_RING, t * P:(t + 1) * P], Wout[:, h, :],
                                                        start=(h == 0), stop=(h == H2 - 1))
                            last.then_inc(y_ps, 1)

                        for what, u, part in order:
                            {"x": transpose_x, "q": project_q, "s": scores, "p": transpose_p, "pv": weighted,
                             "y": project_out}[what](u, part)

                    @blk.scalar
                    def _(act):
                        def exps(u, t):
                            if not 0 <= u < UNITS:
                                return
                            n = score_tile(u, t)
                            act.wait_ge(max_done, n + 1)
                            if u >= 2:
                                act.wait_ge(p_ps, block(u - 1, 0))
                            nc.scalar.activation(prob[:, u % 2 * TPC + t, :].rearrange("p (a w) -> p a w", a=2),
                                                 psS[n % 2][:, :, 0:JH], ACT.Exp, bias=nmax[:, n:n + 1],
                                                 accum_out=rsum[:, n:n + 1]).then_inc(exp_done, 1)

                        def normalise_p(u, t):
                            if not 0 <= u < UNITS:
                                return
                            n = score_tile(u, t)
                            act.wait_ge(rinv_done, n + 1)
                            nc.scalar.activation(prob[:, u % 2 * TPC + t, :], prob[:, u % 2 * TPC + t, :], ACT.Copy,
                                                 scale=rinv[:, n:n + 1]).then_inc(norm_done, 1)

                        def p_high(u, j):
                            if not 0 <= u < UNITS:
                                return
                            rows, g = min(P, J - j * P), block(u, j)
                            act.wait_ge(p_ps, g + 1)
                            if g >= PT_RING:
                                act.wait_ge(pv_ps, g - PT_RING + 1)
                            nc.scalar.activation(pT[0][0:rows, g % PT_RING, :], ring[at["p", u, j] % RING][0:rows, :],
                                                 ACT.Copy).then_inc(p_hi, 1)

                        def q_high(u):
                            if not 0 <= u < UNITS:
                                return
                            act.wait_ge(q_ps, u + 1)
                            if u >= 2:
                                act.wait_ge(s_ps, score_tile(u - 1, 0))
                            nc.scalar.activation(q[0][:, u % 2, :], ring[at["q", u, 0] % RING][:, :], ACT.Copy).then_inc(q_hi, 1)

                        for c in range(CHUNKS):
                            for k in range(CT):
                                act.wait_ge(x_ps, CT * c + k + 1)
                                nc.scalar.activation(xT[0][:, k, c * CHUNK:(c + 1) * CHUNK], ring[at["x", c, k] % RING][:, :],
                                                     ACT.Copy).then_inc(x_hi, 1)
                        for s_ in range(-1, UNITS + 2):
                            exps(s_ - 1, 2)
                            p_high(s_ - 2, 1)
                            exps(s_ - 1, 3)
                            p_high(s_ - 2, 2)
                            normalise_p(s_ - 1, 1)
                            p_high(s_ - 2, 3)
                            normalise_p(s_ - 1, 2)
                            normalise_p(s_ - 1, 3)
                            exps(s_, 0)
                            exps(s_, 1)
                            p_high(s_ - 2, 4)
                            q_high(s_ + 1)
                            normalise_p(s_, 0)
                            p_high(s_ - 1, 0)

                    @blk.vector
                    def _(dve):
                        def row_max(u, t):
                            if not 0 <= u < UNITS:
                                return
                            n = score_tile(u, t)
                            dve.wait_ge(s_ps, n + 1)
                            nc.vector.tensor_reduce(nmax[:, n:n + 1], psS[n % 2][:, :, 0:JH], XY, ALU.max,
                                                    negate=True).then_inc(max_done, 1)

                        def chunk_out(u, *tiles):
                            if u >= H2 + 3 and u < UNITS and u % H2 == 3:
                                for t in tiles:
                                    residual(u // H2 - 1, t)
                                if tiles[-1] == TPC - 1:
                                    layer_norm(u // H2 - 1)

                        def invert_sum(u, t):
                            if not 0 <= u < UNITS:
                                return
                            n = score_tile(u, t)
                            dve.wait_ge(exp_done, n + 1)
                            nc.vector.reciprocal(rinv[:, n:n + 1], rsum[:, n:n + 1]).then_inc(rinv_done, 1)

                        def p_low(u, j):
                            if not 0 <= u < UNITS:
                                return
                            rows, g = min(P, J - j * P), block(u, j)
                            dve.wait_ge(p_hi, g + 1)
                            nc.vector.tensor_tensor(pT[1][0:rows, g % PT_RING, :], ring[at["p", u, j] % RING][0:rows, :],
                                                    pT[0][0:rows, g % PT_RING, :].bitcast(F32), ALU.subtract).then_inc(p_lo, 1)

                        def q_low(u):
                            if not 0 <= u < UNITS:
                                return
                            dve.wait_ge(q_hi, u + 1)
                            nc.vector.tensor_tensor(q[1][:, u % 2, :], ring[at["q", u, 0] % RING][:, :],
                                                    q[0][:, u % 2, :].bitcast(F32), ALU.subtract).then_inc(q_lo, 1)

                        def head_out(u):
                            if not 0 <= u < UNITS:
                                return
                            dve.wait_ge(pv_ps, block(u + 1, 0))
                            if u == OUT_RING:
                                dve.wait_ge(y_ps, TPC)
                            nc.vector.tensor_copy(outT[:, u % OUT_RING, :], psO[:, :]).then_inc(o_done, 1)

                        def residual(c, t):
                            n = c * TPC + t
                            dve.wait_ge(y_ps, n + 1)
                            dve.wait_ge(xb_done, NT)
                            nc.vector.tensor_tensor(y[:, n, :], ring[at["y", c, t] % RING][:, 0:C], xn[:, n, :],
                                                    ALU.add).then_inc(y_done, 1)
                            dve.wait_ge(y_done, n + 1)
                            nc.vector.bn_stats(stats[:, n, :], y[:, n, :]).then_inc(st_done, 1)
                            dve.wait_ge(st_done, 2 * n + 1)
                            nc.vector.bn_aggr(mv[:, n, :], stats[:, n, :]).then_inc(st_done, 1)
                            dve.wait_ge(st_done, 2 * n + 2)
                            nc.vector.tensor_scalar(veps[:, n:n + 1], mv[:, n, 1:2], EPS, None, ALU.add).then_inc(veps_done, 1)

                        def layer_norm(c):
                            for n in range(c * TPC, (c + 1) * TPC):
                                dve.wait_ge(rstd_done, n + 1)
                                nc.vector.tensor_scalar(y[:, n, :], y[:, n, :], mv[:, n, 0:1], rstd[:, n:n + 1],
                                                        ALU.subtract, ALU.mult).then_inc(ln_done, 1)

                        for c in range(CHUNKS):
                            for k in range(CT):
                                dve.wait_ge(x_hi, CT * c + k + 1)
                                nc.vector.tensor_tensor(xT[1][:, k, c * CHUNK:(c + 1) * CHUNK], ring[at["x", c, k] % RING][:, :],
                                                        xT[0][:, k, c * CHUNK:(c + 1) * CHUNK].bitcast(F32),
                                                        ALU.subtract).then_inc(x_lo, 1)
                        for s_ in range(-2, UNITS + 2):
                            invert_sum(s_, 1)
                            p_low(s_ - 1, 1)
                            invert_sum(s_, 2)
                            invert_sum(s_, 3)
                            head_out(s_ - 2)
                            p_low(s_ - 1, 2)
                            row_max(s_ + 1, 0)
                            row_max(s_ + 1, 1)
                            invert_sum(s_ + 1, 0)
                            p_low(s_ - 1, 3)
                            p_low(s_ - 1, 4)
                            chunk_out(s_ + 1, 0, 1)
                            row_max(s_ + 1, 2)
                            chunk_out(s_ + 1, 2)
                            q_low(s_ + 2)
                            row_max(s_ + 1, 3)
                            chunk_out(s_ + 1, 3)
                            p_low(s_, 0)
                        for t in range(TPC):
                            residual(CHUNKS - 1, t)
                        layer_norm(CHUNKS - 1)
                s.clear()
        with nc.Block(no_gpsimd_drain=True) as block:
            @block.sync
            def _(sp):
                sp.wait_ge(out_st, B * (16 * CHUNKS) + 16)


def split(nc, block, name, s, pairs):
    hi_done, lo_done = s.sem(f"{name}_hi"), s.sem(f"{name}_lo")

    @block.scalar
    def _(act):
        for full, (hi, lo), loaded, count in pairs:
            act.wait_ge(loaded, count)
            nc.scalar.activation(hi, full, ACT.Copy).then_inc(hi_done, 1)

    @block.vector
    def _(dve):
        for n, (full, (hi, lo), loaded, count) in enumerate(pairs):
            dve.wait_ge(hi_done, n + 1)
            nc.vector.tensor_tensor(lo, full, hi.bitcast(F32), ALU.subtract).then_inc(lo_done, 1)


LOADS3 = 12


def load_layer3(nc, io, w, x_prev, out_st):
    with Scope(nc, "load3") as s:
        Wf = s.sb("Wf", [P, CT, 4 * C])
        selF = s.sb("selF", [P, 16, P])
        maskf = s.sb("maskf", [P, 2, P])
        W_in, w_in, consts = s.sem("W_in"), s.sem("w_in"), s.sem("consts")
        with nc.Block(no_gpsimd_drain=True) as block:
            @block.sync
            def _(sp):
                sp.dma_start(Wf[:, :, 0:3 * C], io["Win"].rearrange("(k p) d -> p k d", p=P)).then_inc(W_in, 16)
                sp.dma_start(Wf[:, :, 3 * C:4 * C], io["Wo3"].rearrange("(k p) d -> p k d", p=P)).then_inc(W_in, 16)
                loads = [(selF[:, :, :], io["sel"].rearrange("n p m -> p n m")),
                         (w["ones_row"][:, :], io["ones_row"]),
                         (w["cos"][:, :, :], io["cos"].rearrange("(n p) d -> p n d", p=P)),
                         (w["sin"][:, :, :], io["sin"].rearrange("(n p) d -> p n d", p=P)),
                         (w["ident"][:, :], io["ident"]),
                         (maskf[:, 0, :], io["mask"]), (maskf[:, 1, :], io["maskT"])]
                loads += [(w[n][:, :], io[n].partition_broadcast(P)) for n in ("bv", "bo", "ln1w", "ln1b")]
                loads += [(w["xs"][:, :, :], x_prev[0:T, :].rearrange("(n p) c -> p n c", p=P))]
                assert len(loads) == LOADS3
                for dst, src in loads:
                    sp.dma_start(dst, src).then_inc(w_in, 16)
                sp.dma_start(w["bqk"][:, :], io["bqk"]).then_inc(out_st, 16)
                sp.wait_ge(w_in, 16 * LOADS3)
                sp.wait_ge(out_st, 16)

            @block.gpsimd
            def _(pool):
                nc.gpsimd.memset(w["nhalf"][:, :], -0.5).then_inc(consts, 1)
                nc.gpsimd.memset(w["V"][:, :, :, :], 1.0).then_inc(consts, 1)
                pool.wait_ge(consts, 2)
            split(nc, block, "w", s, [(Wf[:, :, :], [w[f"W{i}"][:, :, :] for i in range(2)], W_in, 32)])

            @block.scalar
            def _(act):
                act.wait_ge(w_in, 16 * LOADS3)
                nc.scalar.activation(w["sel"][:, :, :], selF[:, :, :], ACT.Copy)
                nc.scalar.activation(w["identb"][:, :], w["ident"][:, :], ACT.Copy)
                for i, name in enumerate(("maskb", "maskTb")):
                    nc.scalar.activation(w[name][:, :], maskf[:, i, :], ACT.Copy)
        s.clear()


def layer3_attention(nc, io, x_prev, x_next):
    with Scope(nc, "keep3") as keep:
        sb = keep.sb
        w = dict(W0=sb("W0", [P, CT, 4 * C], F32R), W1=sb("W1", [P, CT, 4 * C], F32R), sel=sb("sel", [P, 16, P], F32R),
                 bqk=sb("bqk", [P, 4]), ones_row=sb("ones_row", [P, 1]), cos=sb("cos", [P, NT, D3]),
                 sin=sb("sin", [P, NT, D3]), ident=sb("ident", [P, P]), identb=sb("identb", [P, P], BF16),
                 maskb=sb("maskb", [P, P], BF16), maskTb=sb("maskTb", [P, P], BF16), bv=sb("bv", [P, C]),
                 bo=sb("bo", [P, C]), ln1w=sb("ln1w", [P, C]), ln1b=sb("ln1b", [P, C]), nhalf=sb("nhalf", [P, 1]),
                 V=sb("V", [P, NT, H3, ROWS3]), xs=sb("xs", [P, NT, C]))
        out_st = keep.sem("out_st")
        load_layer3(nc, io, w, x_prev, out_st)
        xs = w["xs"]
        y = sb("y", [P, NT, C])
        mT = sb("mT", [H3, T], F32R)
        m_rows = nc.dram_tensor("m_rows", (H3, T), F32R).ap()
        W = [w["W0"], w["W1"]]
        sel, V, ident, identb = w["sel"], w["V"], w["ident"], w["identb"]
        xn = sb("xn", [P, NT, C])
        qs = sb("qs", [P, PAIRS, T], F32R)
        ks = sb("ks", [P, PAIRS, T], F32R)
        ctx = sb("ctx", [P, NT, C])

        def store_maxima(sp, c, rows_out, rows_in):
            cols = slice(c * CHUNK, (c + 1) * CHUNK)
            sp.dma_start(m_rows[:, cols].bitcast(F32), mT[:, cols].bitcast(F32)).then_inc(rows_out, 16)
            sp.wait_ge(rows_out, 16)
            for p in range(2):
                sp.dma_start(qs[64 * p + 32:64 * p + 33, :, cols].bitcast(F32),
                             m_rows[PAIRS * p:PAIRS * (p + 1), cols].unsqueeze(0).bitcast(F32)).then_inc(rows_in, 16)
            sp.wait_ge(rows_in, 32)

        with nc.Fori(0, B) as b:
            with Scope(nc, "proj3") as s:
                rope = s.sb("rope", [P, NT, C])
                rope2 = ctx
                shared = s.sb("shared", [P, 2 * CT, T], F32R)
                xT = [shared[:, i * CT:(i + 1) * CT, :] for i in range(2)]
                rT = [s.sb(f"rT{i}", [P, CT, T], F32R) for i in range(2)]
                qk = [s.sb("qk", [P, 2 * CT, T], F32R), shared]
                NB = 8
                bank = [s.ps(f"bank{i}", [P, 512]) for i in range(NB)]
                next_in, cos_done, sin_done, rope_done, xb_done, slot_ps, act_read, dve_read = (
                    s.sem(n) for n in ("next_in", "cos_done", "sin_done", "rope_done", "xb_done", "slot_ps", "act_read", "dve_read"))
                slots = [("x", c, k) for c in range(CHUNKS) for k in range(CT)]
                slots += [("v", t, 0) for t in range(NT)]
                slots += [("r", c, k) for c in range(CHUNKS) for k in range(CT)]
                slots += [("qk", m, c) for m in range(2 * CT) for c in range(CHUNKS)]
                slots += [(z, g, c) for g in range(PAIRS) for c in range(CHUNKS) for z in ("sq", "sk")]
                at = {n: i for i, n in enumerate(slots)}
                by_act = {n: sum(m[0] in ("x", "r", "qk", "sk") for m in slots[:i + 1]) for n, i in at.items()}
                by_dve = {n: sum(m[0] != "sk" for m in slots[:i + 1]) for n, i in at.items()}

                with nc.Block(no_gpsimd_drain=True) as block:
                    @block.sync
                    def _(sp):
                        sp.wait_ge(slot_ps, CHUNKS * CT)
                        sp.wait_ge(cos_done, 1)
                        sp.wait_ge(sin_done, 2)
                        sp.wait_ge(xb_done, NT)
                        sp.dma_start(xs[:, :, :], x_prev[bass.ts((b + 1) % B, T), :].rearrange("(n p) c -> p n c", p=P)).then_inc(next_in, 16)
                        sp.wait_ge(next_in, 16)

                    @block.tensor
                    def _(pe):
                        def take(name):
                            i = at[name]
                            if i >= NB:
                                before = slots[i - NB]
                                if before[0] == "sk":
                                    pe.wait_ge(act_read, by_act[before])
                                else:
                                    pe.wait_ge(dve_read, by_dve[before])
                            return bank[i % NB]

                        for name in slots:
                            kind, a, c = name
                            if kind == "r" and a == 0 and c == 0:
                                pe.wait_ge(rope_done, 1)
                            if kind == "v" and a == 0:
                                pe.wait_ge(dve_read, by_dve["x", CHUNKS - 1, CT - 1])
                            if kind == "qk" and a == 0 and c == 0:
                                pe.wait_ge(dve_read, by_dve["r", CHUNKS - 1, CT - 1])
                            if kind == "sq" and a % 4 == 0 and c == 0:
                                pe.wait_ge(dve_read, by_dve["qk", 2 * CT - 1, CHUNKS - 1])
                            ps = take(name)
                            if kind in "xr":
                                src = xs if kind == "x" else rope
                                for t in range(TPC):
                                    last = nc.tensor.transpose(ps[:, t * P:(t + 1) * P],
                                                               src[:, a * TPC + t, c * P:(c + 1) * P], ident[:, :])
                            elif kind == "v":
                                for k in range(CT):
                                    last = mm3(nc, ps[:, 0:C], [z[:, k, a * P:(a + 1) * P] for z in xT],
                                               [z[:, k, 2 * C:3 * C] for z in W], k == 0, k == CT - 1)
                            elif kind == "qk":
                                for k in range(CT):
                                    last = mm3(nc, ps[:, :], [z[:, k, a * P:(a + 1) * P] for z in W],
                                               [z[:, k, c * CHUNK:(c + 1) * CHUNK] for z in rT], k == 0, k == CT - 1)
                            else:
                                n, m = (0, 0) if kind == "sq" else (8, CT)
                                for i in range(2):
                                    last = nc.tensor.matmul(ps[:, :], sel[:, n + 2 * (a % 4) + i, :],
                                                            qk[i][:, m + a // 4, c * CHUNK:(c + 1) * CHUNK],
                                                            start=(i == 0), stop=(i == 1))
                            last.then_inc(slot_ps, 1)

                    @block.gpsimd
                    def _(pool):
                        x4 = xs[:, :, :].rearrange("p n (h i two) -> p n h i two", h=H3, two=2)
                        r4 = rope2[:, :, :].rearrange("p n (h i two) -> p n h i two", h=H3, two=2)
                        sin4 = w["sin"][:, :, :].rearrange("p n (i two) -> p n i two", two=2)
                        for z in range(2):
                            nc.gpsimd.tensor_tensor(r4[:, :, :, :, z], x4[:, :, :, :, 1 - z],
                                                    sin4[:, :, :, z].unsqueeze(2).to_broadcast([P, NT, H3, D3 // 2]),
                                                    ALU.mult).then_inc(sin_done, 1)
                        for t in range(NT):
                            nc.gpsimd.tensor_tensor(xn[:, t, :], xs[:, t, :], w["bo"][:, :], ALU.add).then_inc(xb_done, 1)

                    @block.scalar
                    def _(act):
                        for name in slots:
                            kind, a, c = name
                            ps, cols = bank[at[name] % NB], slice(c * CHUNK, (c + 1) * CHUNK)
                            if kind in ("v", "sq"):
                                continue
                            act.wait_ge(slot_ps, at[name] + 1)
                            if kind in "xr":
                                dst = (xT if kind == "x" else rT)[0][:, c, a * CHUNK:(a + 1) * CHUNK]
                                i = nc.scalar.activation(dst, ps[:, :], ACT.Copy)
                            elif kind == "qk":
                                i = nc.scalar.activation(qk[0][:, a, cols], ps[:, :], ACT.Identity, bias=w["bqk"][:, a:a + 1])
                            else:
                                i = nc.scalar.activation(ks[:, a, cols], ps[:, :], ACT.Identity, bias=w["ones_row"][:, 0:1])
                            i.then_inc(act_read, 1)

                    @block.vector
                    def _(dve):
                        cosb = w["cos"][:, :, :].unsqueeze(2).to_broadcast([P, NT, H3, D3])
                        nc.vector.tensor_tensor(rope[:, :, :].rearrange("p n (h d) -> p n h d", h=H3),
                                                xs[:, :, :].rearrange("p n (h d) -> p n h d", h=H3), cosb, ALU.mult).then_inc(cos_done, 1)
                        for name in slots:
                            kind, a, c = name
                            ps, cols = bank[at[name] % NB], slice(c * CHUNK, (c + 1) * CHUNK)
                            if kind == "sk":
                                continue
                            if name == ("v", 0, 0):
                                dve.wait_ge(cos_done, 1)
                                dve.wait_ge(sin_done, 2)
                                nc.vector.tensor_tensor(rope[:, :, :], rope[:, :, :], rope2[:, :, :], ALU.add).then_inc(rope_done, 1)
                            if kind in ("x", "r", "qk"):
                                dve.wait_ge(act_read, by_act[name])
                            else:
                                dve.wait_ge(slot_ps, at[name] + 1)
                            if kind in "xr":
                                hi, lo = [z[:, c, a * CHUNK:(a + 1) * CHUNK] for z in (xT if kind == "x" else rT)]
                                i = nc.vector.tensor_tensor(lo, ps[:, :], hi.bitcast(F32), ALU.subtract)
                            elif kind == "v":
                                i = nc.vector.tensor_tensor(V[:, a, :, 0:D3], ps[:, 0:C].rearrange("p (h d) -> p h d", h=H3),
                                                            w["bv"][:, :].rearrange("p (h d) -> p h d", h=H3), ALU.add)
                            elif kind == "qk":
                                i = nc.vector.scalar_tensor_tensor(out=qk[1][:, a, cols], in0=ps[:, :], scalar=w["bqk"][:, a:a + 1],
                                                                   in1=qk[0][:, a, cols].bitcast(F32), op0=ALU.add, op1=ALU.subtract)
                            else:
                                i = nc.vector.tensor_copy(qs[:, a, cols], ps[:, :])
                            i.then_inc(dve_read, 1)
                s.clear()

            with Scope(nc, "max3") as s:
                mx = s.sb("mx", [P, NT, 2, H3])
                mf = s.sb("mf", [P, NT, H3])
                psS = [s.ps(f"psS{i}", [P, 2, 512]) for i in range(3)]
                psM = s.ps("psM", [H3, T])
                s_ps, max_done, mf_done, t_ps, mT_done, rows_out, rows_in = (
                    s.sem(n) for n in ("s_ps", "max_done", "mf_done", "t_ps", "mT_done", "rows_out", "rows_in"))
                units = [(t, c, g) for t in range(NT) for c in range(t // TPC + 1) for g in range(PAIRS)]
                first = sum(t < TPC for t, c, g in units)

                def width(t, c):
                    return min(CHUNK, (t + 1) * P - c * CHUNK)

                with nc.Block(no_gpsimd_drain=True) as block:
                    @block.tensor
                    def _(pe):
                        def transpose_maxima(c):
                            pe.wait_ge(mf_done, c + 1)
                            for t in range(c * TPC, (c + 1) * TPC):
                                last = nc.tensor.transpose(psM[:, t * P:(t + 1) * P], mf[:, t, :], ident[:, :])
                            last.then_inc(t_ps, 1)

                        for n, (t, c, g) in enumerate(units):
                            if n >= 3:
                                pe.wait_ge(max_done, n - 2)
                            ps, wd, diag = psS[n % 3], width(t, c), c == t // TPC
                            for i in range(2):
                                rows = slice(64 * i, 64 * i + 64)
                                last = nc.tensor.matmul(ps[:, i, 0:wd], qs[rows, g, t * P:(t + 1) * P],
                                                        ks[rows, g, c * CHUNK:c * CHUNK + wd], start=True, stop=not diag)
                            if diag:
                                for i in range(2):
                                    last = nc.tensor.matmul(ps[:, i, wd - P:wd], identb[:, :], w["maskb"][:, :],
                                                            start=False, stop=True)
                            last.then_inc(s_ps, 1)
                            if n == first + PAIRS:
                                transpose_maxima(0)
                        transpose_maxima(1)

                    @block.vector
                    def _(dve):
                        for n, (t, c, g) in enumerate(units):
                            dve.wait_ge(s_ps, n + 1)
                            out = mx[:, t, c, :].rearrange("p (two g) -> p g two", two=2)[:, g, :]
                            nc.vector.tensor_reduce(out, psS[n % 3][:, :, 0:width(t, c)], X, ALU.max).then_inc(max_done, 1)
                            if n == first:
                                dve.wait_ge(max_done, first)
                                nc.vector.tensor_copy(mf[:, 0:TPC, :], mx[:, 0:TPC, 0, :]).then_inc(mf_done, 1)
                        dve.wait_ge(max_done, len(units))
                        nc.vector.tensor_tensor(mf[:, TPC:NT, :], mx[:, TPC:NT, 0, :], mx[:, TPC:NT, 1, :], ALU.max).then_inc(mf_done, 1)

                    @block.scalar
                    def _(act):
                        for c in range(CHUNKS):
                            act.wait_ge(t_ps, c + 1)
                            cols = slice(c * CHUNK, (c + 1) * CHUNK)
                            nc.scalar.activation(mT[:, cols], psM[:, cols], ACT.Copy, scale=-1.0).then_inc(mT_done, 1)

                    @block.sync
                    def _(sp):
                        sp.wait_ge(mT_done, 1)
                        store_maxima(sp, 0, rows_out, rows_in)
                s.clear()

            with Scope(nc, "attn3") as s:
                pT = s.sb("pT", [P, 3, 2, CHUNK])
                raw = s.sb("raw", [P, 2, CHUNK])
                rinv = s.sb("rinv", [P, 2, TPC, 4, 1])
                psS = [s.ps(f"psS{i}", [P, 2, 512]) for i in range(3)]
                psO = s.ps("psO", [P, CHUNK])
                psT = s.ps("psT", [P, TPC, 4, ROWS3])
                rows_out, rows_in, s_ps, exp_done, o_ps, raw_done, t_ps, r_done, c_done = (
                    s.sem(n) for n in ("rows_out", "rows_in", "s_ps", "exp_done", "o_ps", "raw_done", "t_ps", "r_done", "c_done"))
                rounds = [(c, gg) for c in range(CHUNKS) for gg in range(H3 // 4)]
                units = [(r, c, 2 * gg + z, j) for r, (c, gg) in enumerate(rounds) for j in range((c + 1) * TPC) for z in range(2)]

                def span(c, j):
                    lo = max(j * P, c * CHUNK)
                    return lo, (c + 1) * CHUNK - lo, j * P >= c * CHUNK

                with nc.Block(no_gpsimd_drain=True) as block:
                    @block.sync
                    def _(sp):
                        store_maxima(sp, 1, rows_out, rows_in)

                    @block.tensor
                    def _(pe):
                        def scores(n):
                            r, c, g, j = units[n]
                            lo, wd, diag = span(c, j)
                            if c > 0 and units[n - 1][1] == 0:
                                pe.wait_ge(rows_in, 32)
                            if n >= 3:
                                pe.wait_ge(exp_done, n - 2)
                            for p in range(2):
                                last = nc.tensor.matmul(psS[n % 3][:, p, 0:wd], ks[64 * p:64 * p + 64, g, j * P:(j + 1) * P],
                                                        qs[64 * p:64 * p + 64, g, lo:lo + wd], start=True, stop=not diag)
                            if diag:
                                for p in range(2):
                                    last = nc.tensor.matmul(psS[n % 3][:, p, 0:P], identb[:, :], w["maskTb"][:, :],
                                                            start=False, stop=True)
                            last.then_inc(s_ps, 1)

                        def weighted(n):
                            r, c, g, j = units[n]
                            lo, wd, diag = span(c, j)
                            pe.wait_ge(exp_done, n + 1)
                            if j == 0 and r >= 1:
                                pe.wait_ge(raw_done, r)
                            for p in range(2):
                                i = 2 * (g % 2) + p
                                last = nc.tensor.matmul(psO[ROWS3 * i:ROWS3 * (i + 1), lo - c * CHUNK:CHUNK], V[:, j, 2 * g + p, :],
                                                        pT[:, n % 3, p, 0:wd], start=(j == 0), stop=(j == (c + 1) * TPC - 1))
                            last.then_inc(o_ps, 1)

                        def transpose_round(r):
                            pe.wait_ge(raw_done, r + 1)
                            if r >= 1:
                                pe.wait_ge(c_done, r)
                            for t in range(TPC):
                                last = nc.tensor.transpose(psT[:, t, :, :].rearrange("p h d -> p (h d)"),
                                                           raw[:, r % 2, t * P:(t + 1) * P], ident[:, :])
                            last.then_inc(t_ps, 1)

                        scores(0)
                        scores(1)
                        for n in range(len(units)):
                            if n + 2 < len(units):
                                scores(n + 2)
                            weighted(n)
                            r, j, second = units[n][0], units[n][3], n % 2 == 1
                            if r >= 1 and j == 1 and second:
                                transpose_round(r - 1)
                        transpose_round(len(rounds) - 1)

                    @block.scalar
                    def _(act):
                        for n, (r, c, g, j) in enumerate(units):
                            act.wait_ge(s_ps, n + 1)
                            if n >= 3:
                                act.wait_ge(o_ps, n - 2)
                            wd = span(c, j)[1]
                            nc.scalar.activation(pT[:, n % 3, :, 0:wd], psS[n % 3][:, :, 0:wd], ACT.Exp, scale=SCALE3).then_inc(exp_done, 1)

                    @block.vector
                    def _(dve):
                        def divide(r):
                            c, gg = rounds[r]
                            dve.wait_ge(t_ps, r + 1)
                            nc.vector.reciprocal(rinv[:, r % 2, :, :, :], psT[:, :, :, D3:D3 + 1]).then_inc(r_done, 1)
                            dve.wait_ge(r_done, r + 1)
                            nc.vector.tensor_tensor(
                                ctx[:, c * TPC:(c + 1) * TPC, 4 * gg * D3:(4 * gg + 4) * D3].rearrange("p t (h d) -> p t h d", h=4),
                                psT[:, :, :, 0:D3], rinv[:, r % 2, :, :, :].to_broadcast([P, TPC, 4, D3]),
                                ALU.mult).then_inc(c_done, 1)

                        done = 0
                        for r, (c, gg) in enumerate(rounds):
                            done += 2 * (c + 1) * TPC
                            dve.wait_ge(o_ps, done)
                            nc.vector.tensor_copy(raw[:, r % 2, :], psO[:, :]).then_inc(raw_done, 1)
                            if r >= 1:
                                divide(r - 1)
                        divide(len(rounds) - 1)
                s.clear()

            with Scope(nc, "out3") as s:
                cT = [s.sb(f"cT{i}", [P, CT, T], F32R) for i in range(2)]
                stats = s.sb("stats", [P, NT, 6])
                mv = s.sb("mv", [P, NT, 2])
                veps = s.sb("veps", [P, NT])
                rstd = s.sb("rstd", [P, NT])
                psT = [s.ps(f"psT{i}", [P, 512]) for i in range(4)]
                psY = [s.ps(f"psY{i}", [P, 512]) for i in range(4)]
                t_ps, hi_done, lo_done, y_ps, y_done = (
                    s.sem(n) for n in ("t_ps", "hi_done", "lo_done", "y_ps", "y_done"))
                st_done, veps_done, rstd_done, ln_done, pool_w, pool_b, dve_w, dve_b = (
                    s.sem(n) for n in ("st_done", "veps_done", "rstd_done", "ln_done", "pool_w", "pool_b", "dve_w", "dve_b"))
                BY_POOL = 5
                groups = [(c, k) for c in range(CHUNKS) for k in range(CT)]
                with nc.Block(no_gpsimd_drain=True) as block:
                    @block.sync
                    def _(sp):
                        for c in range(CHUNKS):
                            sp.wait_ge(pool_b, min(BY_POOL, TPC * (c + 1)))
                            if TPC * (c + 1) > BY_POOL:
                                sp.wait_ge(dve_b, NT - BY_POOL)
                            sp.dma_start(x_next[bass.ds(b * T + c * CHUNK, CHUNK), :].rearrange("(n p) c -> p n c", p=P),
                                         y[:, c * TPC:(c + 1) * TPC, :]).then_inc(out_st, 16)

                    @block.tensor
                    def _(pe):
                        for n, (c, k) in enumerate(groups):
                            for t in range(TPC):
                                last = nc.tensor.transpose(psT[n][:, t * P:(t + 1) * P], ctx[:, c * TPC + t, k * P:(k + 1) * P], ident[:, :])
                            last.then_inc(t_ps, 1)
                        for t in range(NT):
                            pe.wait_ge(lo_done, CT * (t // TPC + 1))
                            if t >= 4:
                                pe.wait_ge(y_done, t - 3)
                            for k in range(CT):
                                last = mm3(nc, psY[t % 4][:, 0:C], [z[:, k, t * P:(t + 1) * P] for z in cT],
                                           [z[:, k, 3 * C:4 * C] for z in W], k == 0, k == CT - 1)
                            last.then_inc(y_ps, 1)

                    @block.scalar
                    def _(act):
                        for n, (c, k) in enumerate(groups):
                            act.wait_ge(t_ps, n + 1)
                            nc.scalar.activation(cT[0][:, k, c * CHUNK:(c + 1) * CHUNK], psT[n][:, :], ACT.Copy).then_inc(hi_done, 1)

                    @block.gpsimd
                    def _(pool):
                        for t in range(NT):
                            pool.wait_ge(veps_done, t + 1)
                            nc.gpsimd.tensor_tensor(rstd[:, t:t + 1], veps[:, t:t + 1], w["nhalf"][:, :], ALU.pow).then_inc(rstd_done, 1)
                            u = t - 2 if t < NT - 1 else t - 3
                            if 0 <= u < BY_POOL and t != NT - 2:
                                pool.wait_ge(ln_done, u + 1)
                                nc.gpsimd.tensor_tensor(y[:, u, :], y[:, u, :], w["ln1w"][:, :], ALU.mult).then_inc(pool_w, 1)
                                pool.wait_ge(pool_w, u + 1)
                                nc.gpsimd.tensor_tensor(y[:, u, :], y[:, u, :], w["ln1b"][:, :], ALU.add).then_inc(pool_b, 1)

                    @block.vector
                    def _(dve):
                        for n, (c, k) in enumerate(groups):
                            dve.wait_ge(hi_done, n + 1)
                            cols = slice(c * CHUNK, (c + 1) * CHUNK)
                            nc.vector.tensor_tensor(cT[1][:, k, cols], psT[n][:, :], cT[0][:, k, cols].bitcast(F32), ALU.subtract).then_inc(lo_done, 1)

                        def scaled(t):
                            dve.wait_ge(rstd_done, t + 1)
                            nc.vector.tensor_scalar(y[:, t, :], y[:, t, :], mv[:, t, 0:1], rstd[:, t:t + 1],
                                                    ALU.subtract, ALU.mult).then_inc(ln_done, 1)

                        for t in range(NT):
                            dve.wait_ge(y_ps, t + 1)
                            if t == 0:
                                dve.wait_ge(out_st, b * (16 * CHUNKS) + 16)
                            nc.vector.tensor_tensor(y[:, t, :], psY[t % 4][:, 0:C], xn[:, t, :], ALU.add).then_inc(y_done, 1)
                            dve.wait_ge(y_done, t + 1)
                            nc.vector.bn_stats(stats[:, t, :], y[:, t, :]).then_inc(st_done, 1)
                            dve.wait_ge(st_done, 2 * t + 1)
                            nc.vector.bn_aggr(mv[:, t, :], stats[:, t, :]).then_inc(st_done, 1)
                            dve.wait_ge(st_done, 2 * t + 2)
                            nc.vector.tensor_scalar(veps[:, t:t + 1], mv[:, t, 1:2], EPS, None, ALU.add).then_inc(veps_done, 1)
                            if t >= 2:
                                scaled(t - 2)
                        scaled(NT - 2)
                        scaled(NT - 1)
                        for t in range(BY_POOL, NT):
                            dve.wait_ge(ln_done, t + 1)
                            nc.vector.tensor_tensor(y[:, t, :], y[:, t, :], w["ln1w"][:, :], ALU.mult).then_inc(dve_w, 1)
                        for t in range(BY_POOL, NT):
                            dve.wait_ge(dve_w, t - BY_POOL + 1)
                            nc.vector.tensor_tensor(y[:, t, :], y[:, t, :], w["ln1b"][:, :], ALU.add).then_inc(dve_b, 1)
                s.clear()
        with nc.Block(no_gpsimd_drain=True) as block:
            @block.sync
            def _(sp):
                sp.wait_ge(out_st, B * (16 * CHUNKS) + 16)


def experts(nc, io, x_prev, x1_in, out):
    with Scope(nc, "keep4") as keep:
        sb = keep.sb
        We = [sb(f"We{i}", [P, CT, NE * C], F32R) for i in range(2)]
        Wg = [sb(f"Wg{i}", [P, CT, NE], F32R) for i in range(2)]
        eb = sb("eb", [NE, C])
        gb, ln2w, ln2b = sb("gb", [P, NE]), sb("ln2w", [P, C]), sb("ln2b", [P, C])
        ident, nhalf, number = sb("ident", [P, P]), sb("nhalf", [P, 1]), sb("number", [P, NE])
        x1s, xns = sb("x1s", [P, NT, C]), sb("xns", [P, NT, C])
        out_st = keep.sem("out_st")
        with Scope(nc, "load4") as s:
            Wf = s.sb("Wf", [P, CT, NE * C])
            Wgf = s.sb("Wgf", [P, CT, NE])
            W_in = [s.sem(f"W_in{k}") for k in range(CT)]
            w_in, consts = s.sem("w_in"), s.sem("consts")
            with nc.Block(no_gpsimd_drain=True) as block:
                @block.sync
                def _(sp):
                    for k in range(CT):
                        sp.dma_start(Wf[:, k, :], io["We"][k * P:(k + 1) * P, :]).then_inc(W_in[k], 16)
                    for dst, src in ((Wgf[:, :, :], io["Wg"].rearrange("(k p) e -> p k e", p=P)),
                                     (gb[:, :], io["gb"].partition_broadcast(P)), (ln2w[:, :], io["ln2w"].partition_broadcast(P)),
                                     (ln2b[:, :], io["ln2b"].partition_broadcast(P)), (ident[:, :], io["ident"]),
                                     (number[:, :], io["number"].partition_broadcast(P)),
                                     (x1s[:, :, :], x1_in[0:T, :].rearrange("(n p) c -> p n c", p=P)),
                                     (xns[:, :, :], x_prev[0:T, :].rearrange("(n p) c -> p n c", p=P))):
                        sp.dma_start(dst, src).then_inc(w_in, 16)
                    sp.dma_start(eb[:, :], io["eb"]).then_inc(out_st, 16)
                    sp.wait_ge(w_in, 128)
                    sp.wait_ge(out_st, 16)

                @block.gpsimd
                def _(pool):
                    nc.gpsimd.memset(nhalf[:, :], -0.5).then_inc(consts, 1)
                    pool.wait_ge(consts, 1)
                split(nc, block, "w", s, [(Wf[:, k, :], [z[:, k, :] for z in We], W_in[k], 16) for k in range(CT)]
                      + [(Wgf[:, :, :], [z[:, :, :] for z in Wg], w_in, 128)])
            s.clear()

        with Scope(nc, "moe") as s:
            xn = s.sb("xn", [P, NT, C])
            x1 = s.sb("x1", [P, NT, C])
            xT = [s.sb(f"xT{i}", [P, CT, T], F32R) for i in range(2)]
            lg = s.sb("lg", [P, NT, NE])
            ex = s.sb("ex", [P, NT, NE])
            gate = s.sb("gate", [P, NT, NE])
            is1, is2 = s.sb("is1", [P, NT, NE]), s.sb("is2", [P, NT, NE])
            top = s.sb("top", [P, NT, 8])
            idx = s.sb("idx", [P, NT, 8], U32)
            idxf = s.sb("idxf", [P, NT, 8])
            gsum, ginv = s.sb("gsum", [P, NT]), s.sb("ginv", [P, NT])
            gT = s.sb("gT", [NE, T])
            acc = s.sb("acc", [P, NT, C])
            stats = s.sb("stats", [P, 2 * NT, 6])
            mv = s.sb("mv", [P, 2 * NT, 2])
            veps = s.sb("veps", [P, 2 * NT])
            rstd = s.sb("rstd", [P, 2 * NT])
            psE = [s.ps(f"psE{i}", [P, 2, C]) for i in range(6)]
            psB = [s.ps(f"psB{i}", [P, 512]) for i in range(2)]
            x1_kept, xn_kept, next_in = s.sem("x1_kept"), s.sem("xn_kept"), s.sem("next_in")
            t_ps, hi_done, lo_done = s.sem("t_ps"), s.sem("hi_done"), s.sem("lo_done")
            g_ps, top_done, ex_done, gate_step, gate_done, gT_ps, gT_done = (
                s.sem(n) for n in ("g_ps", "top_done", "ex_done", "gate_step", "gate_done", "gT_ps", "gT_done"))
            e_ps, e_done, b_ps, b_done = s.sem("e_ps"), s.sem("e_done"), s.sem("b_ps"), s.sem("b_done")
            st_done, ag_done, veps_done, rstd_done, ln2_done, aff_w, aff_b, res_done, fin_done, tail_step = (
                s.sem(n) for n in ("st_done", "ag_done", "veps_done", "rstd_done", "ln2_done", "aff_w", "aff_b", "res_done", "fin_done", "tail_step"))
            groups = [(c, k) for c in range(CHUNKS) for k in range(CT)]
            EP = NE // 2
            norms = []
            for tt in range(NT // 2 + 1):
                norms += [("moe", 2 * tt + z) for z in range(2) if tt < NT // 2]
                norms += [("out", 2 * tt - 2 + z) for z in range(2) if tt > 0]
            nth = {name: n for n, name in enumerate(norms)}

            def tile_pair(n):
                return n // (2 * EP) * 2 + n % 2, n // 2 % EP

            def scaled_sum(t, e):
                return (t // 2) * 2 * NE + 2 * e + t % 2 + 1

            def transposes_and_logits(pe, after_experts):
                for n, (c, k) in enumerate(groups):
                    if after_experts:
                        unit = NT * EP - 6 + n
                        t, pair = tile_pair(unit)
                        pe.wait_ge(e_done, scaled_sum(t, 2 * pair + 1))
                    for t in range(TPC):
                        last = nc.tensor.transpose(psE[2 + n][:, t // 2, t % 2 * P:(t % 2 + 1) * P],
                                                   x1s[:, c * TPC + t, k * P:(k + 1) * P], ident[:, :])
                    last.then_inc(t_ps, 1)
                pe.wait_ge(lo_done, len(groups))
                for t in range(NT):
                    for k in range(CT):
                        last = mm3(nc, psB[0][:, t * NE:(t + 1) * NE], [z[:, k, t * P:(t + 1) * P] for z in xT],
                                   [z[:, k, :] for z in Wg], k == 0, k == CT - 1)
                last.then_inc(g_ps, 1)

            def high_parts(act):
                for n, (c, k) in enumerate(groups):
                    act.wait_ge(t_ps, n + 1)
                    nc.scalar.activation(xT[0][:, k, c * CHUNK:(c + 1) * CHUNK], psE[2 + n][:, :, :].rearrange("p a w -> p (a w)"),
                                         ACT.Copy).then_inc(hi_done, 1)

            def low_parts(dve):
                for n, (c, k) in enumerate(groups):
                    dve.wait_ge(hi_done, n + 1)
                    cols = slice(c * CHUNK, (c + 1) * CHUNK)
                    nc.vector.tensor_tensor(xT[1][:, k, cols], psE[2 + n][:, :, :].rearrange("p a w -> p (a w)"),
                                            xT[0][:, k, cols].bitcast(F32), ALU.subtract).then_inc(lo_done, 1)

            def logits_out(dve):
                dve.wait_ge(g_ps, 1)
                nc.vector.tensor_tensor(lg[:, :, :], psB[0][:, 0:NT * NE].rearrange("p (t e) -> p t e", e=NE),
                                        gb[:, :].unsqueeze(1).to_broadcast([P, NT, NE]), ALU.add)

            with nc.Block(no_gpsimd_drain=True) as block:
                @block.tensor
                def _(pe):
                    transposes_and_logits(pe, False)

                @block.scalar
                def _(act):
                    high_parts(act)

                @block.vector
                def _(dve):
                    low_parts(dve)
                    logits_out(dve)
            s.clear()

            with nc.Fori(0, B) as b:
                with nc.Block(no_gpsimd_drain=True) as block:
                    @block.sync
                    def _(sp):
                        sp.wait_ge(x1_kept, 1)
                        sp.dma_start(x1s[:, :, :], x1_in[bass.ts((b + 1) % B, T), :].rearrange("(n p) c -> p n c", p=P)).then_inc(next_in, 16)
                        sp.wait_ge(xn_kept, 1)
                        sp.dma_start(xns[:, :, :], x_prev[bass.ts((b + 1) % B, T), :].rearrange("(n p) c -> p n c", p=P)).then_inc(next_in, 16)
                        for tt in range(NT // 2):
                            sp.wait_ge(fin_done, 2 * tt + 2)
                            sp.dma_start(out[bass.ds(b * T + 2 * tt * P, 2 * P), :].rearrange("(n p) c -> p n c", p=P),
                                         acc[:, 2 * tt:2 * tt + 2, :]).then_inc(out_st, 16)
                        sp.wait_ge(next_in, 32)

                    @block.tensor
                    def _(pe):
                        def expert_pair(n):
                            t, e = tile_pair(n)
                            if n >= 6:
                                before, pair = tile_pair(n - 6)
                                pe.wait_ge(e_done, scaled_sum(before, 2 * pair + 1))
                            for k in range(CT):
                                last = mm3(nc, psE[n % 6][:, :, :], [z[:, k, t * P:(t + 1) * P] for z in xT],
                                           [z[:, k, 2 * e * C:(2 * e + 2) * C] for z in We], k == 0, k == CT - 1)
                            last.then_inc(e_ps, 1)

                        for n in range(NT * EP):
                            expert_pair(n)
                            if n == 3:
                                pe.wait_ge(gate_done, 1)
                                for t in range(NT):
                                    last = nc.tensor.transpose(psB[t // TPC][0:NE, t % TPC * P:(t % TPC + 1) * P], gate[:, t, :], ident[:, :])
                                last.then_inc(gT_ps, 1)
                            if n % (2 * EP) == 5:
                                if n == 5:
                                    pe.wait_ge(gT_done, 2)
                                for t in (n // (2 * EP) * 2, n // (2 * EP) * 2 + 1):
                                    if t >= 2:
                                        pe.wait_ge(b_done, t - 1)
                                    nc.tensor.matmul(psB[t % 2][:, 0:C], gT[:, t * P:(t + 1) * P], eb[:, :], start=True, stop=True).then_inc(b_ps, 1)

                        pe.wait_ge(next_in, 32)
                        pe.wait_ge(b_done, NT)
                        transposes_and_logits(pe, True)

                    @block.scalar
                    def _(act):
                        nc.scalar.activation(x1[:, :, :], x1s[:, :, :], ACT.Copy).then_inc(x1_kept, 1)
                        act.wait_ge(gate_step, 1)
                        nc.scalar.activation(ex[:, :, :], ex[:, :, :], ACT.Exp).then_inc(ex_done, 1)
                        act.wait_ge(gT_ps, 1)
                        for c in range(CHUNKS):
                            nc.scalar.activation(gT[:, c * CHUNK:(c + 1) * CHUNK], psB[c][0:NE, :], ACT.Copy).then_inc(gT_done, 1)
                        high_parts(act)

                    @block.gpsimd
                    def _(pool):
                        nc.gpsimd.tensor_copy(xn[:, :, :], xns[:, :, :]).then_inc(xn_kept, 1)
                        pool.wait_ge(xn_kept, 1)
                        for tt in range(NT // 2 + 1):
                            for name in norms:
                                if name in (("moe", 2 * tt), ("moe", 2 * tt + 1), ("out", 2 * tt - 2), ("out", 2 * tt - 1)):
                                    n = nth[name]
                                    pool.wait_ge(veps_done, n + 1)
                                    nc.gpsimd.tensor_tensor(rstd[:, n:n + 1], veps[:, n:n + 1], nhalf[:, :], ALU.pow).then_inc(rstd_done, 1)
                            if tt < NT // 2 - 1:
                                two = (2 * tt, 2 * tt + 1)
                                for t in two:
                                    pool.wait_ge(ln2_done, t + 1)
                                    nc.gpsimd.tensor_tensor(acc[:, t, :], acc[:, t, :], ln2w[:, :], ALU.mult).then_inc(aff_w, 1)
                                for t in two:
                                    pool.wait_ge(aff_w, t + 1)
                                    nc.gpsimd.tensor_tensor(acc[:, t, :], acc[:, t, :], ln2b[:, :], ALU.add).then_inc(aff_b, 1)
                                for t in two:
                                    pool.wait_ge(aff_b, t + 1)
                                    nc.gpsimd.tensor_tensor(acc[:, t, :], acc[:, t, :], xn[:, t, :], ALU.add).then_inc(res_done, 1)

                    @block.vector
                    def _(dve):
                        for t in range(NT):
                            last = nc.vector.max(top[:, t, :], lg[:, t, :])
                        last.then_inc(top_done, 1)
                        dve.wait_ge(top_done, 1)
                        nc.vector.tensor_tensor(ex[:, :, :], lg[:, :, :], top[:, :, 0:1].to_broadcast([P, NT, NE]),
                                                ALU.subtract).then_inc(gate_step, 1)
                        for t in range(NT):
                            last = nc.vector.max_index(idx[:, t, :], top[:, t, :], lg[:, t, :])
                        last.then_inc(top_done, 1)
                        dve.wait_ge(top_done, 2)
                        nc.vector.tensor_copy(idxf[:, :, :], idx[:, :, :]).then_inc(gate_step, 1)
                        dve.wait_ge(gate_step, 2)
                        numbers = number[:, :].unsqueeze(1).to_broadcast([P, NT, NE])
                        nc.vector.tensor_tensor(is1[:, :, :], numbers, idxf[:, :, 0:1].to_broadcast([P, NT, NE]), ALU.is_equal).then_inc(gate_step, 1)
                        nc.vector.tensor_tensor(is2[:, :, :], numbers, idxf[:, :, 1:2].to_broadcast([P, NT, NE]), ALU.is_equal).then_inc(gate_step, 1)
                        dve.wait_ge(gate_step, 4)
                        nc.vector.tensor_tensor(is1[:, :, :], is1[:, :, :], is2[:, :, :], ALU.add).then_inc(gate_step, 1)
                        dve.wait_ge(ex_done, 1)
                        nc.vector.tensor_reduce(gsum[:, :], ex[:, :, :], X, ALU.add).then_inc(gate_step, 1)
                        dve.wait_ge(gate_step, 6)
                        nc.vector.reciprocal(ginv[:, :], gsum[:, :]).then_inc(gate_step, 1)
                        nc.vector.tensor_tensor(gate[:, :, :], ex[:, :, :], is1[:, :, :], ALU.mult).then_inc(gate_step, 1)
                        dve.wait_ge(gate_step, 8)
                        nc.vector.tensor_tensor(gate[:, :, :], gate[:, :, :], ginv[:, :].unsqueeze(2).to_broadcast([P, NT, NE]),
                                                ALU.mult).then_inc(gate_done, 1)

                        def statistics(kind, tt):
                            two = [(nth[kind, t], t) for t in (2 * tt, 2 * tt + 1)]
                            for n, t in two:
                                if kind == "moe":
                                    dve.wait_ge(b_done, t + 1)
                                nc.vector.bn_stats(stats[:, n, :], acc[:, t, :]).then_inc(st_done, 1)
                            for n, t in two:
                                dve.wait_ge(st_done, n + 1)
                                nc.vector.bn_aggr(mv[:, n, :], stats[:, n, :]).then_inc(ag_done, 1)
                            for n, t in two:
                                dve.wait_ge(ag_done, n + 1)
                                nc.vector.tensor_scalar(veps[:, n:n + 1], mv[:, n, 1:2], EPS, None, ALU.add).then_inc(veps_done, 1)

                        def scaled(kind, tt, done):
                            for t in (2 * tt, 2 * tt + 1):
                                n = nth[kind, t]
                                dve.wait_ge(rstd_done, n + 1)
                                nc.vector.tensor_scalar(acc[:, t, :], acc[:, t, :], mv[:, n, 0:1], rstd[:, n:n + 1],
                                                        ALU.subtract, ALU.mult).then_inc(done, 1)

                        for tt in range(NT // 2 + 2):
                            if tt < NT // 2:
                                two = (2 * tt, 2 * tt + 1)
                                if tt == 0:
                                    dve.wait_ge(x1_kept, 1)
                                    dve.wait_ge(gate_done, 1)
                                    dve.wait_ge(out_st, b * (16 * NT // 2) + 16)
                                for e in range(NE):
                                    for t in two:
                                        n = tt * 2 * EP + 2 * (e // 2) + t % 2
                                        if e % 2 == 0:
                                            dve.wait_ge(e_ps, n + 1)
                                        if e > 0:
                                            dve.wait_ge(e_done, scaled_sum(t, e - 1))
                                        nc.vector.scalar_tensor_tensor(out=acc[:, t, :], in0=psE[n % 6][:, e % 2, :], scalar=gate[:, t, e:e + 1],
                                                                       in1=(acc if e else x1)[:, t, :], op0=ALU.mult, op1=ALU.add).then_inc(e_done, 1)
                                    if e == 2 and tt >= 1:
                                        scaled("moe", tt - 1, ln2_done)
                                    if e == 5 and tt >= 2:
                                        scaled("out", tt - 2, fin_done)
                                for t in two:
                                    dve.wait_ge(b_ps, t + 1)
                                    dve.wait_ge(e_done, scaled_sum(t, NE - 1))
                                    nc.vector.tensor_tensor(acc[:, t, :], psB[t % 2][:, 0:C], acc[:, t, :], ALU.add).then_inc(b_done, 1)
                                statistics("moe", tt)
                                if tt == NT // 2 - 1:
                                    low_parts(dve)
                            if tt == NT // 2:
                                scaled("moe", tt - 1, ln2_done)
                                dve.wait_ge(xn_kept, 1)
                                for i, (op, other) in enumerate(((ALU.mult, lambda t: ln2w[:, :]), (ALU.add, lambda t: ln2b[:, :]),
                                                                 (ALU.add, lambda t: xn[:, t, :]))):
                                    for z, t in enumerate((NT - 2, NT - 1)):
                                        if i == 0:
                                            dve.wait_ge(ln2_done, t + 1)
                                        else:
                                            dve.wait_ge(tail_step, 2 * i + z - 1)
                                        nc.vector.tensor_tensor(acc[:, t, :], acc[:, t, :], other(t), op).then_inc(tail_step, 1)
                                dve.wait_ge(tail_step, 6)
                            elif 1 <= tt < NT // 2:
                                dve.wait_ge(res_done, 2 * tt)
                            if 1 <= tt <= NT // 2:
                                statistics("out", tt - 1)
                            if tt >= NT // 2:
                                scaled("out", tt - 2, fin_done)
                        logits_out(dve)
                s.clear()
        with nc.Block(no_gpsimd_drain=True) as block:
            @block.sync
            def _(sp):
                sp.wait_ge(out_st, B * (16 * NT // 2) + 16)


def build(nc, io, out):
    x1, x2, x3 = (nc.dram_tensor(n, (TOKENS, C), F32).ap() for n in ("x_layer1", "x_layer2", "x_attended"))
    layer1(nc, io, x1)
    layer2(nc, io, x1, x2)
    layer3_attention(nc, io, x2, x3)
    experts(nc, io, x2, x3, out)


def lay_out(inputs):
    v = {k: np.asarray(a) for k, a in inputs.items()}
    c = np.ascontiguousarray
    x = v["x"].reshape(TOKENS, C)
    eye = np.eye(P, dtype=np.float32)
    later = np.triu(np.full((P, P), -1e30, np.float32), 1)
    a = dict(
        x=x, xT=c(x.T), WaT=c(v["L0_attn_W_attn"].T), AaT=c(v["L0_attn_lora_attn_A"].T), Ba=v["L0_attn_lora_attn_B"],
        ApT=c(v["L0_attn_lora_proj_A"].T), Bp=v["L0_attn_lora_proj_B"], Wp=v["L0_attn_W_proj"],
        WpT=c(v["L0_attn_W_proj"].T), gamma=c(v["L0_attn_bn_gamma"].reshape(DT, P).T),
        beta=c(v["L0_attn_bn_beta"].reshape(DT, P).T), ident=eye, mask=later)
    a.update(
        ctxT=c(v["ctx_768"].reshape(J, CD).T), Wq2=v["L0_xattn_Wq"], Wk2=v["L0_xattn_Wk"], Wv2=v["L0_xattn_Wv"],
        Wout=v["L0_xattn_Wout"], bout=v["L0_xattn_bout"])
    inverse = (1.0 / 10000.0 ** (np.arange(0, D3, 2, dtype=np.float32) / D3)).astype(np.float32)
    angle = np.arange(T, dtype=np.float32)[:, None] * inverse[None, :]
    cos, sin = np.cos(angle), np.sin(angle)
    sel = np.zeros((2, 4, 2, P, P), np.float32)
    d = np.arange(D3)
    for pair in range(4):
        for p in range(2):
            rows, base = (2 * pair + p) * D3 + d, 64 * p
            sel[0, pair, 0, rows, base + d] = 1
            sel[0, pair, 0, rows, base + D3 + d] = 1
            sel[0, pair, 1, rows, base + 3 * D3 + d] = 1
            sel[1, pair, 0, rows, base + d] = 1
            sel[1, pair, 0, rows, base + 3 * D3 + d] = 1
            sel[1, pair, 1, rows, base + D3 + d] = 1
    ones_row = np.zeros((P, 1), np.float32)
    ones_row[[32, 96]] = 1
    a.update(
        Win=c(v["L0_ffn_in_proj_w"].T), Wo3=c(v["L0_ffn_out_proj_w"].T),
        bqk=c(v["L0_ffn_in_proj_b"][:2 * C].reshape(2 * CT, P).T), bv=v["L0_ffn_in_proj_b"][2 * C:],
        bo=v["L0_ffn_out_proj_b"], ln1w=v["L0_ffn_ln1_w"], ln1b=v["L0_ffn_ln1_b"], ln2w=v["L0_ffn_ln2_w"], ln2b=v["L0_ffn_ln2_b"],
        Wg=c(v["L0_ffn_gate_w"].T), gb=v["L0_ffn_gate_b"], eb=v["L0_ffn_expert_b"],
        We=c(v["L0_ffn_expert_w"].transpose(2, 0, 1).reshape(C, NE * C)),
        cos=c(np.repeat(cos, 2, 1)), sin=c(np.stack([-sin, sin], -1).reshape(T, D3)), sel=sel.reshape(16, P, P),
        ones_row=ones_row, maskT=c(later.T), number=np.arange(NE, dtype=np.float32))
    return a


def kernel(**inputs):
    import numpy as _np
    import concourse.bacc as _bacc
    from concourse import mybir as _mybir
    from concourse.bass_utils import run_bass_kernel_spmd as _run

    nc = _bacc.Bacc("TRN2", target_bir_lowering=False, num_devices=1)
    arrays = lay_out(inputs)
    io = {}
    for name, a in arrays.items():
        io[name] = nc.dram_tensor(f"in_{name}", a.shape, _mybir.dt.from_np(a.dtype), kind="ExternalInput").ap()
    out = nc.dram_tensor("out", (TOKENS, C), _mybir.dt.float32, kind="ExternalOutput").ap()
    build(nc, io, out)
    r = _run(nc, [{f"in_{name}": a for name, a in arrays.items()}], core_ids=[0])
    return r.results[0]["out"].reshape(B, T, C)
```
